# Optimizing a Trainium2 kernel written in Bass

```python
import numpy as np
import jax
import jax.numpy as jnp

def _softmax(x, axis=-1):
    return jax.nn.softmax(x, axis=axis)

def _gelu(x):
    return jax.nn.gelu(x, approximate=True)

def _silu(x):
    return jax.nn.silu(x)

def _sigmoid(x):
    return jax.nn.sigmoid(x)

def _layernorm(x, axis=-1, eps=1e-05):
    m = jnp.mean(x, axis=axis, keepdims=True)
    v = jnp.var(x, axis=axis, keepdims=True)
    return (x - m) / jnp.sqrt(v + eps)

def _scatter_add(tgt, idx, src, axis=0):
    return tgt.at[idx].add(src)

def _segment_sum(src, seg, n):
    return jax.ops.segment_sum(src, seg, n)
kernel_name = 'mk_early_fusion_embed_d2_tok_img1024_r4_b25d7f'

def setup_inputs(seed: int=0):
    np.random.seed(seed)
    _w = jnp.asarray

    def _rec_inputs():
        import jax
        import jax.numpy as jnp
        _rk = jax.random.key(seed)
        x = -0.00016672 + 0.999947 * jax.random.normal(jax.random.fold_in(_rk, 1), (32, 3, 96, 96), jnp.float32)
        x_txt = jax.random.randint(jax.random.fold_in(_rk, 51), (32, 77), 0, 12564, jnp.int32)
        return (x, x_txt)
    x, x_txt = _rec_inputs()

    def _L0_tok_setup():
        import jax, jax.numpy as jnp
        import numpy as np
        IMG, P, C, D = (96, 16, 3, 256)
        G = IMG // P
        NP = G * G
        K = P * P * C
        key = jax.random.key(seed)
        k1, k2, k3, k4, k5 = jax.random.split(key, 5)
        x = jax.random.normal(k1, (64, C, IMG, IMG), dtype=jnp.float32)
        W = jax.random.normal(k2, (D, K), dtype=jnp.float32) * (1.0 / np.sqrt(K))
        b = jax.random.normal(k3, (D,), dtype=jnp.float32) * 0.01
        pos_embedding = jax.random.normal(k4, (1, NP + 1, D), dtype=jnp.float32)
        cls_token = jax.random.normal(k5, (1, 1, D), dtype=jnp.float32)
        return {'x': x, 'W': W, 'b': b, 'pos_embedding': pos_embedding, 'cls_token': cls_token}
    _L0_tok_all = _L0_tok_setup()
    _L0_tok_in = {k: v for k, v in _L0_tok_all.items() if k in ('W', 'b', 'pos_embedding', 'cls_token')}
    del _L0_tok_all

    def _L0_txt_setup():
        import jax, jax.numpy as jnp
        import numpy as np
        VOCAB = 50257
        D_MODEL = 256
        key = jax.random.key(seed)
        k1, k2 = jax.random.split(key)
        X = jax.random.randint(k1, (4, 2048), 0, VOCAB, dtype=jnp.int64 if jax.config.jax_enable_x64 else jnp.int32)
        std = np.sqrt(2.0 / (VOCAB + D_MODEL))
        embeddings = jax.random.truncated_normal(k2, -3.0, 3.0, (VOCAB, D_MODEL), dtype=jnp.float32) * std
        return {'X': X, 'embeddings': embeddings}
    _L0_txt_all = _L0_txt_setup()
    _L0_txt_in = {k: v for k, v in _L0_txt_all.items() if k in ('embeddings',)}
    del _L0_txt_all

    def _L0_attn_setup():
        import jax, jax.numpy as jnp
        import numpy as np
        N_EMBD = 256
        N_HEAD = 16
        SEQ = 512
        BATCH = 2
        NEG = -1000000000.0
        key = jax.random.key(seed)
        k0, k1, k2 = jax.random.split(key, 3)
        return {'hidden_states': jax.random.normal(k0, (BATCH, SEQ, N_EMBD), dtype=jnp.float32), 'w_attn': jax.random.normal(k1, (3 * N_EMBD, N_EMBD), dtype=jnp.float32) * 0.02, 'b_attn': jnp.zeros((3 * N_EMBD,), dtype=jnp.float32), 'w_proj': jax.random.normal(k2, (N_EMBD, N_EMBD), dtype=jnp.float32) * 0.02, 'b_proj': jnp.zeros((N_EMBD,), dtype=jnp.float32)}
    _L0_attn_all = _L0_attn_setup()
    _L0_attn_in = {k: v for k, v in _L0_attn_all.items() if k in ('w_attn', 'b_attn', 'w_proj', 'b_proj')}
    del _L0_attn_all

    def _L0_ffn_setup():
        import jax, jax.numpy as jnp
        import numpy as np
        TOP_K = 4
        key = jax.random.key(seed)
        ks = jax.random.split(key, 5)
        B, T, D = (2, 256, 256)
        P, PD = (64, 32)
        return {'x': jax.random.normal(ks[0], (B, T, D), dtype=jnp.float32), 'hasher_w': jax.random.normal(ks[1], (PD, D), dtype=jnp.float32) * 0.03, 'keys': jax.random.normal(ks[2], (P, PD), dtype=jnp.float32) * 0.1, 'values_down': jax.random.normal(ks[3], (P, D, PD), dtype=jnp.float32) * 0.01, 'values_up': jax.random.normal(ks[4], (P, PD, D), dtype=jnp.float32) * 0.01, 'scale': jnp.full((1,), 0.1, dtype=jnp.float32)}
    _L0_ffn_all = _L0_ffn_setup()
    _L0_ffn_in = {k: v for k, v in _L0_ffn_all.items() if k in ('hasher_w', 'keys', 'values_down', 'values_up', 'scale')}
    del _L0_ffn_all

    def _L1_attn_setup():
        import jax, jax.numpy as jnp
        import numpy as np
        import math
        B, T, C = (4, 512, 256)
        H, DQK, DV = (16, 64, 64)
        key = jax.random.key(seed)
        k1, k2, k3, k4, k5 = jax.random.split(key, 5)
        x_q = jax.random.normal(k1, (B, T, C), dtype=jnp.float32)
        w_q = jax.random.normal(k2, (H, DQK, C), dtype=jnp.float32) / math.sqrt(C)
        w_k = jax.random.normal(k3, (H, DQK, C), dtype=jnp.float32) / math.sqrt(C)
        w_v = jax.random.normal(k4, (H, DV, C), dtype=jnp.float32) / math.sqrt(C)
        w_o = jax.random.normal(k5, (DV * H, C), dtype=jnp.float32) / math.sqrt(C)
        return {'x_q': x_q, 'w_q': w_q, 'w_k': w_k, 'w_v': w_v, 'w_o': w_o}
    _L1_attn_all = _L1_attn_setup()
    _L1_attn_in = {k: v for k, v in _L1_attn_all.items() if k in ('w_q', 'w_k', 'w_v', 'w_o')}
    del _L1_attn_all

    def _L1_ffn_setup():
        import jax, jax.numpy as jnp
        import numpy as np
        QMAX = 127.0

        def _ste_round(v):
            return v + jax.lax.stop_gradient(jnp.round(v) - v)

        def _act_fake_quant(x, clip_factor):
            scale = jax.nn.sigmoid(clip_factor) * jnp.max(jnp.abs(x)) / QMAX
            return jnp.clip(_ste_round(x / scale), -QMAX - 1.0, QMAX) * scale

        def _weight_fake_quant(w):
            scale = jnp.max(jnp.abs(w), axis=1, keepdims=True) / QMAX
            return jnp.clip(_ste_round(w / scale), -QMAX - 1.0, QMAX) * scale
        key = jax.random.key(seed)
        k1, k2, k3, k4 = jax.random.split(key, 4)
        B, S, H, I = (8, 2048, 256, 704)
        return {'x': jax.random.normal(k1, (B, S, H), dtype=jnp.float32), 'clip_x': jnp.full((1,), 4.0, dtype=jnp.float32), 'clip_down': jnp.full((1,), 4.0, dtype=jnp.float32), 'w_gate': jax.random.normal(k2, (I, H), dtype=jnp.float32) * 0.02, 'w_up': jax.random.normal(k3, (I, H), dtype=jnp.float32) * 0.02, 'w_down': jax.random.normal(k4, (H, I), dtype=jnp.float32) * 0.02}
    _L1_ffn_all = _L1_ffn_setup()
    _L1_ffn_in = {k: v for k, v in _L1_ffn_all.items() if k in ('clip_x', 'clip_down', 'w_gate', 'w_up', 'w_down')}
    del _L1_ffn_all
    return {'x': x, 'x_txt': x_txt, 'L0_tok_W': _L0_tok_in['W'], 'L0_tok_b': _L0_tok_in['b'], 'L0_tok_pos_embedding': _L0_tok_in['pos_embedding'], 'L0_tok_cls_token': _L0_tok_in['cls_token'], 'L0_txt_embeddings': _L0_txt_in['embeddings'], 'L0_attn_w_attn': _L0_attn_in['w_attn'], 'L0_attn_b_attn': _L0_attn_in['b_attn'], 'L0_attn_w_proj': _L0_attn_in['w_proj'], 'L0_attn_b_proj': _L0_attn_in['b_proj'], 'L0_ffn_hasher_w': _L0_ffn_in['hasher_w'], 'L0_ffn_keys': _L0_ffn_in['keys'], 'L0_ffn_values_down': _L0_ffn_in['values_down'], 'L0_ffn_values_up': _L0_ffn_in['values_up'], 'L0_ffn_scale': _L0_ffn_in['scale'], 'L1_attn_w_q': _L1_attn_in['w_q'], 'L1_attn_w_k': _L1_attn_in['w_k'], 'L1_attn_w_v': _L1_attn_in['w_v'], 'L1_attn_w_o': _L1_attn_in['w_o'], 'L1_ffn_clip_x': _L1_ffn_in['clip_x'], 'L1_ffn_clip_down': _L1_ffn_in['clip_down'], 'L1_ffn_w_gate': _L1_ffn_in['w_gate'], 'L1_ffn_w_up': _L1_ffn_in['w_up'], 'L1_ffn_w_down': _L1_ffn_in['w_down']}

def reference(x, x_txt, L0_tok_W, L0_tok_b, L0_tok_pos_embedding, L0_tok_cls_token, L0_txt_embeddings, L0_attn_w_attn, L0_attn_b_attn, L0_attn_w_proj, L0_attn_b_proj, L0_ffn_hasher_w, L0_ffn_keys, L0_ffn_values_down, L0_ffn_values_up, L0_ffn_scale, L1_attn_w_q, L1_attn_w_k, L1_attn_w_v, L1_attn_w_o, L1_ffn_clip_x, L1_ffn_clip_down, L1_ffn_w_gate, L1_ffn_w_up, L1_ffn_w_down):
    import jax
    import jax.numpy as jnp

    def _L0_tok_ref(x, W, b, pos_embedding, cls_token):
        import jax, jax.numpy as jnp
        import numpy as np
        IMG, P, C, D = (96, 16, 3, 256)
        G = IMG // P
        NP = G * G
        K = P * P * C
        bsz = x.shape[0]
        patches = x.reshape(bsz, C, G, P, G, P).transpose(0, 2, 4, 1, 3, 5)
        patches = patches.reshape(bsz, NP, K)
        proj = jnp.einsum('bnk,dk->bnd', patches, W) + b
        cls = jnp.broadcast_to(cls_token, (bsz, 1, D))
        out = jnp.concatenate([cls, proj], axis=1) + pos_embedding
        return out

    def _L0_txt_ref(X, embeddings):
        import jax, jax.numpy as jnp
        import numpy as np
        VOCAB = 50257
        D_MODEL = 256
        return jnp.take(embeddings, X, axis=0)

    def _L0_attn_ref(hidden_states, w_attn, b_attn, w_proj, b_proj):
        import jax, jax.numpy as jnp
        import numpy as np
        N_EMBD = 256
        N_HEAD = 16
        SEQ = 512
        BATCH = 2
        NEG = -1000000000.0
        B, S, E = hidden_states.shape
        H = N_HEAD
        D = E // H
        qkv = hidden_states @ w_attn.T + b_attn
        q, k, v = jnp.split(qkv, 3, axis=-1)
        split = lambda t: t.reshape(B, S, H, D).transpose(0, 2, 1, 3)
        q, k, v = (split(q), split(k), split(v))
        w = jnp.einsum('bhnd,bhmd->bhnm', q, k) * jax.lax.rsqrt(float(D))
        mask = jnp.tril(jnp.ones((S, S), dtype=jnp.float32))
        w = jnp.where(mask > 0, w, NEG)
        w = jax.nn.softmax(w, axis=-1)
        attn = jnp.einsum('bhnm,bhmd->bhnd', w, v)
        attn = attn.transpose(0, 2, 1, 3).reshape(B, S, E)
        return attn @ w_proj.T + b_proj

    def _L0_ffn_ref(x, hasher_w, keys, values_down, values_up, scale):
        import jax, jax.numpy as jnp
        import numpy as np
        TOP_K = 4
        h = jnp.einsum('btd,pd->btp', x, hasher_w)
        sim = jnp.einsum('btp,np->btn', h, keys)
        vals, idx = jax.lax.top_k(sim, TOP_K)
        w = jax.nn.softmax(vals, axis=-1)
        out = jnp.zeros_like(x)
        for k in range(TOP_K):
            ik = idx[..., k]
            vd = values_down[ik]
            vu = values_up[ik]
            proj = jax.nn.silu(jnp.einsum('btd,btdp->btp', x, vd))
            o = jnp.einsum('btp,btpd->btd', proj, vu)
            out = out + o * w[..., k:k + 1]
        return x + out * scale

    def _L1_attn_ref(x_q, w_q, w_k, w_v, w_o):
        import jax, jax.numpy as jnp
        import numpy as np
        import math
        B, T, C = (4, 512, 256)
        H, DQK, DV = (16, 64, 64)
        q = jnp.einsum('ntc,hdc->nhtd', x_q, w_q)
        k = jnp.einsum('ntc,hdc->nhtd', x_q, w_k)
        v = jnp.einsum('ntc,hdc->nhtd', x_q, w_v)
        a = jnp.einsum('nhtd,nhsd->nhts', q, k) / math.sqrt(q.shape[3])
        t = a.shape[2]
        causal_forbidden = jnp.arange(t)[:, None] < jnp.arange(t)[None, :]
        a = jnp.where(causal_forbidden[None, None], -jnp.inf, a)
        a = jax.nn.softmax(a, axis=3)
        y = jnp.einsum('nhts,nhsd->nthd', a, v).reshape(a.shape[0], t, -1)
        return y @ w_o

    def _L1_ffn_ref(x, clip_x, clip_down, w_gate, w_up, w_down):
        import jax, jax.numpy as jnp
        import numpy as np
        QMAX = 127.0

        def _ste_round(v):
            return v + jax.lax.stop_gradient(jnp.round(v) - v)

        def _act_fake_quant(x, clip_factor):
            scale = jax.nn.sigmoid(clip_factor) * jnp.max(jnp.abs(x)) / QMAX
            return jnp.clip(_ste_round(x / scale), -QMAX - 1.0, QMAX) * scale

        def _weight_fake_quant(w):
            scale = jnp.max(jnp.abs(w), axis=1, keepdims=True) / QMAX
            return jnp.clip(_ste_round(w / scale), -QMAX - 1.0, QMAX) * scale
        xq = _act_fake_quant(x, clip_x[0])
        gate = jnp.einsum('bsh,ih->bsi', xq, _weight_fake_quant(w_gate))
        up = jnp.einsum('bsh,ih->bsi', xq, _weight_fake_quant(w_up))
        h = _act_fake_quant(jax.nn.silu(gate) * up, clip_down[0])
        return jnp.einsum('bsi,hi->bsh', h, _weight_fake_quant(w_down))
    h = _L0_tok_ref(x, L0_tok_W, L0_tok_b, L0_tok_pos_embedding, L0_tok_cls_token)
    h = jnp.concatenate([h, _L0_txt_ref(x_txt, L0_txt_embeddings)], axis=1)
    h = h + _L0_attn_ref(_layernorm(h, axis=-1), L0_attn_w_attn, L0_attn_b_attn, L0_attn_w_proj, L0_attn_b_proj)
    h = h + _L0_ffn_ref(_layernorm(h, axis=-1), L0_ffn_hasher_w, L0_ffn_keys, L0_ffn_values_down, L0_ffn_values_up, L0_ffn_scale)
    h = h + _L1_attn_ref(_layernorm(h, axis=-1), L1_attn_w_q, L1_attn_w_k, L1_attn_w_v, L1_attn_w_o)
    h = h + _L1_ffn_ref(_layernorm(h, axis=-1), L1_ffn_clip_x, L1_ffn_clip_down, L1_ffn_w_gate, L1_ffn_w_up, L1_ffn_w_down)
    return h

_drawn_inputs = setup_inputs


def setup_inputs(seed=0):
    import zlib

    import numpy as np

    out = dict(_drawn_inputs(seed))
    spreads = {'L0_attn_b_attn': (0.0, 0.1), 'L0_attn_b_proj': (0.0, 0.1)}
    factors = {'L0_tok_b': 6.996,
     'L0_ffn_hasher_w': 8.0,
     'L0_ffn_keys': 8.0,
     'L0_ffn_values_down': 8.0,
     'L0_ffn_values_up': 8.0,
     'L1_ffn_w_gate': 3.963,
     'L1_ffn_w_up': 3.726,
     'L1_ffn_w_down': 3.878}
    for name, (base, spread) in spreads.items():
        noise = np.random.default_rng([zlib.crc32(name.encode()), seed]).standard_normal(out[name].shape)
        drawn = base * np.exp(spread * noise) if base else spread * noise
        out[name] = jnp.asarray(drawn.astype(out[name].dtype))
    for name, factor in factors.items():
        out[name] = (out[name] * factor).astype(out[name].dtype)
    return out
```

```python
from contextlib import ExitStack

import concourse.bass as bass
from concourse import mybir

ALU = mybir.AluOpType
ACT = mybir.ActivationFunctionType
AX = mybir.AxisListType
F32 = mybir.dt.float32
BF16 = mybir.dt.bfloat16
I32 = mybir.dt.int32
U32 = mybir.dt.uint32

P = 128
B = 32
S = 114
NIMG = 37
NTXT = 77
D = 256
KC = D // P
PAIR = 2 * S
NPAIR = B // 2
HEADS = 16
UNITS = 8
QCOLS = 4 * S
MASKED = -1.0e30
EPS = 1.0e-5
TOK_K = 768 // P
TOK_G = 3
EXPERTS = 64
EDIM = 32
ETILES = EXPERTS * EDIM // P
TOPK = 4
INNER = 704
ITILES = (INNER + P - 1) // P
IROWS = [min(P, INNER - P * m) for m in range(ITILES)]
QMAX = 127.0
ROUND = 12582912.0
E_CONST = 2.718281828459045


class Pair:

    def __init__(self, p0, i=None):
        self.p0, self.i = p0, i
        self.first = i is None and p0 == 0
        self.last = i is None and p0 == NPAIR - 1

    def val(self, a, c):
        n = a * self.p0 + c
        return n if self.i is None else self.i * (2 * a) + n

    def shift(self, n):
        return Pair(self.p0 + n, self.i)


def run_slots(eng, slot):
    slot(Pair(0))
    with eng.Fori(0, (NPAIR - 2) // 2) as i:
        slot(Pair(1, i))
        slot(Pair(2, i))
    slot(Pair(NPAIR - 1))


def rows_of(H, p, s):
    b = p.val(2, s)
    if isinstance(b, int):
        return H[0:S, b, :]
    return H[0:S, bass.ds(b, 1), :].rearrange("p a d -> p (a d)")


class Banks:

    def __init__(self, front, first, middle, last):
        self.front, self.first, self.middle, self.last = front, first, middle, last

    def uses(self, p):
        return self.front if p is None else self.first if p.first else self.last if p.last else self.middle

    def at(self, p, use):
        names = [u for _, u in self.uses(p)]
        k = names.index(use)
        if p is None:
            return k % 2, k // 2
        if p.first:
            n = len(self.front) + k
            return n % 2, n // 2
        a = len(self.middle)
        c = len(self.front) + len(self.first) - a + k
        whole = a * p.p0 + c
        return whole % 2, whole // 2 if p.i is None else p.i * a + whole // 2

    def step(self, p, t):
        return [u for at, u in self.uses(p) if at == t]


def consts_on_chip(nc, sb, sem):
    c = {
        "ident": sb("ident", [P, P], F32), "identb": sb("identb", [P, P], BF16),
        "mask": sb("mask", [P, 4, S], BF16), "neghalf": sb("neghalf", [P, 2], F32),
        "eps": sb("eps", [P, 2], F32), "minus1": sb("minus1", [P, 2], F32), "ones": sb("ones", [P, P], F32), "e": sb("e_const", [P, 8], F32),
        "iota": sb("iota", [P, EXPERTS], F32), "sel": sb("sel", [P, ETILES, P], BF16),
    }
    return c


def build_consts(pool, c, made, dve_unused=None):
    n = 0
    for name, value in (("ident", 0.0), ("identb", 0.0), ("mask", 0.0), ("neghalf", -0.5), ("minus1", -1.0), ("eps", EPS), ("ones", 1.0),
                        ("e", E_CONST), ("sel", 0.0)):
        pool.memset(c[name][:], value).then_inc(made, 1)
        n += 1
    pool.iota(c["iota"][:], pattern=[[1, EXPERTS]], base=0, channel_multiplier=0,
              allow_small_or_imprecise_dtypes=True).then_inc(made, 1)
    n += 1
    pool.wait_ge(made, n)
    for name in ("ident", "identb"):
        pool.affine_select(out=c[name][:], in_=c[name][:], compare_op=ALU.not_equal, fill=1.0, base=0,
                           pattern=[[-1, P]], channel_multiplier=1).then_inc(made, 1)
        n += 1
    pool.affine_select(out=c["mask"][:], in_=c["mask"][:], compare_op=ALU.is_ge, fill=MASKED, base=0,
                       pattern=[[0, 4], [-1, S]], channel_multiplier=1).then_inc(made, 1)
    n += 1
    v = c["sel"][:].rearrange("p j (q r) -> p j q r", r=EDIM)
    for base in (0, -EXPERTS):
        pool.affine_select(out=v, in_=v, compare_op=ALU.not_equal, fill=1.0, base=base,
                           pattern=[[-(P // EDIM), ETILES], [-1, P // EDIM], [0, EDIM]],
                           channel_multiplier=1).then_inc(made, 1)
        n += 1
        pool.wait_ge(made, n)
    return n


def after_constants(eng, c):
    eng.wait_ge(c["made"], 1)


class Norm:

    def __init__(self, name, c, H, sb, sem):
        self.c, self.H = c, H
        self.stats = sb(name + "stats", [P, 2, 6], F32)
        self.mv = sb(name + "mv", [P, 2, 2], F32)
        self.vareps = sb(name + "vareps", [P, 2], F32)
        self.rstd = sb(name + "rstd", [P, 2], F32)
        self.stats_done, self.mv_done = sem(name + "stats_done"), sem(name + "mv_done")
        self.vareps_done, self.rstd_done = sem(name + "vareps_done"), sem(name + "rstd_done")

    def moments(self, dve, q):
        for s in range(2):
            dve.bn_stats(self.stats[0:S, s, :], rows_of(self.H, q, s)).then_inc(self.stats_done, 1)

    def wait_moments(self, dve, q):
        dve.wait_ge(self.stats_done, q.val(2, 2))

    def aggregate(self, dve, q):
        for s in range(2):
            dve.bn_aggr(self.mv[0:S, s, :], self.stats[0:S, s, :]).then_inc(self.mv_done, 1)

    def root(self, pool, q):
        pool.wait_ge(self.mv_done, q.val(2, 2))
        pool.tensor_tensor(self.vareps[0:S, :], self.mv[0:S, :, 1], self.c["eps"][0:S, :], ALU.add).then_inc(self.vareps_done, 1)
        pool.wait_ge(self.vareps_done, q.val(1, 1))
        pool.tensor_tensor(self.rstd[0:S, :], self.vareps[0:S, :], self.c["neghalf"][0:S, :],
                           ALU.pow).then_inc(self.rstd_done, 1)

    def rows(self, dve, q, dst, ready):
        dve.wait_ge(self.rstd_done, q.val(1, 1))
        for s in range(2):
            dve.tensor_scalar(dst(s), rows_of(self.H, q, s), self.mv[0:S, s, 0:1], self.rstd[0:S, s:s + 1],
                              ALU.subtract, ALU.mult).then_inc(ready, 1)


def attention(nc, name, H, c, w, HD, sb, psum, sem):
    ident, identb, mask, ones = c["ident"], c["identb"], c["mask"], c["ones"]
    ROW = 32 if HD == 16 else 64
    HPT = P // ROW
    QT = HEADS // HPT
    VN = HEADS * HD
    KO = VN // P
    VW = HD + 1
    bias = HD == 16
    SCALE = float(HD) ** -0.5

    norm = Norm(name, c, H, sb, sem)
    xn = sb(name + "xn", [P, 2, D], F32)
    xT = sb(name + "xT", [P, KC, 2, S], F32)
    qkT = [sb(name + f"qkT{k}", [P, 2 * QT, 2, S], F32) for k in range(2)]
    v = [[sb(name + f"v{k}{s}", [P, HEADS, VW], F32) for s in range(2)] for k in range(2)]
    E = [sb(name + f"E{k}", [P, 4, S], F32) for k in range(4)]
    rmax = [sb(name + f"rmax{k}", [P, 4], F32) for k in range(2)]
    pT = [sb(name + f"pT{k}", [P, 4, S], F32) for k in range(2)]
    rsum = [sb(name + f"rsum{k}", [P, 4], F32) for k in range(2)]
    on = [sb(name + f"on{s}", [P, VN], F32) for s in range(2)]
    oT = [sb(name + f"oT{s}", [P, KO, S], F32) for s in range(2)]

    psS = [psum(name + f"psS{k}", [P, 512], F32) for k in range(2)]
    psT = [psum(name + f"psT{k}", [P, 512], F32) for k in range(2)]
    psO = [psum(name + f"psO{k}", [P, 512], F32) for k in range(2)]
    psM = [psum(name + f"psM{k}", [P, 512], F32) for k in range(2)]

    xn_done, ones_done = sem(name + "xn_done"), sem(name + "ones_done")
    scores_done, max_done, sub_done, exp_done = (sem(name + n) for n in ("scores_done", "max_done", "sub_done", "exp_done"))
    turned, pT_done, pv_done, rsum_done, on_done = (sem(name + n) for n in ("turned", "pT_done", "pv_done", "rsum_done", "on_done"))
    filled = [sem(name + f"filled{k}") for k in range(2)]
    copied = [sem(name + f"copied{k}") for k in range(2)]

    VH = [(s, h) for s in range(2) for h in range(max(1, VN // 512))] if VN > D else [(None, 0)]
    OC = [(a, min(a + 4, KO)) for a in range(0, KO, 4)]
    front = [(2, ("xT",))] + [(3 + 4 * j // QT, ("qk", j)) for j in range(QT)]
    front += [(7 if n >= len(VH) // 2 else 6, ("v", s, h)) for n, (s, h) in enumerate(VH)]
    tail1 = [(4, ("oT", 1, a)) for a in range(len(OC))] + [(5, ("proj", 1))]
    tail0 = [(7, ("oT", 0, a)) for a in range(len(OC))] + [(7, ("proj", 0))]

    def merged(*parts):
        return sorted((x for part in parts for x in part), key=lambda x: x[0])

    banks = Banks(front, merged(front, tail0), merged(front, tail1, tail0), merged(tail1, tail0))
    after = [(0, ("oT", 1, a)) for a in range(len(OC))] + [(0, ("proj", 1))]
    END = Pair(NPAIR)

    def bank_of(p, use):
        if p is END:
            whole = sum(map(len, (banks.front, banks.first, banks.last))) + (NPAIR - 2) * len(banks.middle)
            whole += [u for _, u in after].index(use)
            return whole % 2, whole // 2
        return banks.at(p, use)

    def before(p):
        return None if p.first else p.shift(-1)

    def wait_copied(eng, p, use):
        k, n = bank_of(p, use)
        eng.wait_ge(copied[k], n + 1)

    def head_place(i, r):
        if HPT == 4:
            return i, ROW * r
        return 4 * (r // 2) + i, ROW * (r % 2)

    def whose(p, use):
        if use[0] in ("xT", "qk", "v"):
            return p.shift(1)
        return p.shift(-1) if use[1] == 1 else p

    block = nc.Block()
    with block:
        @block.tensor
        def _(pe):
            def bank_free(p, use):
                k, n = bank_of(p, use)
                if not isinstance(n, int) or n > 0:
                    pe.wait_ge(copied[k], n)
                return psM[k], filled[k]

            def scores(p, u):
                k, s, r = u % 2, u // 4, u % 4
                if u == 0:
                    for j in (QT - 2, QT - 1):
                        wait_copied(pe, before(p), ("qk", j))
                if not (p.first and u < 2):
                    pe.wait_ge(sub_done, p.val(8, u - 1))
                pe.matmul(psS[k][0:S, 0:QCOLS], identb[0:S, 0:S], mask[0:S].rearrange("p a k -> p (a k)"),
                          start=True, stop=False, skip_group_check=True)
                qk = qkT[p.p0 % 2]
                for i in range(4):
                    tile, row = head_place(i, r)
                    ps = slice(row, row + HD)
                    m = pe.matmul(psS[k][0:S, i * S:(i + 1) * S], qk[ps, tile, s, :], qk[ps, QT + tile, s, :],
                                  start=False, stop=(i == 3), skip_group_check=True)
                m.then_inc(scores_done, 1)

            def turn(p, u):
                k = u % 2
                pe.wait_ge(exp_done, p.val(8, u + 1))
                for i in range(4):
                    m = pe.transpose(psT[k][0:S, i * S:(i + 1) * S], E[u % 4][0:S, i, :], ident[0:S, 0:S])
                m.then_inc(turned, 1)

            def weigh(p, u):
                k, s, r = u % 2, u // 4, u % 4
                if u == 0:
                    for x in VH[-2:]:
                        wait_copied(pe, before(p), ("v", *x))
                pe.wait_ge(pT_done, p.val(8, u + 1))
                if not (p.first and u < 2):
                    pe.wait_ge(on_done, p.val(8, u - 1))
                for i in range(4):
                    tile, row = head_place(i, r)
                    m = pe.matmul(psO[k][0:S, i * VW:(i + 1) * VW], pT[k][0:S, i, :],
                                  v[p.p0 % 2][s][0:S, HPT * tile + row // ROW, :], start=True, stop=True)
                m.then_inc(pv_done, 1)

            def shared(p, use, q):
                kind = use[0]
                bank, done = bank_free(p, use)
                if kind == "xT":
                    pe.wait_ge(xn_done, q.val(2, 2))
                    for kc in range(KC):
                        for s in range(2):
                            m = pe.transpose(bank[:, (2 * kc + s) * S:(2 * kc + s + 1) * S],
                                             xn[0:S, s, kc * P:(kc + 1) * P], ident[0:S, 0:S])
                elif kind == "qk":
                    if use[1] == 0:
                        wait_copied(pe, p, ("xT",))
                    for half in range(2):
                        tile = 2 * use[1] + half
                        for kc in range(KC):
                            m = pe.matmul(bank[:, half * PAIR:(half + 1) * PAIR],
                                          w["qk"][:, kc, tile * P:(tile + 1) * P],
                                          xT[:, kc].rearrange("p s k -> p (s k)"), start=(kc == 0), stop=(kc == KC - 1))
                elif kind == "v":
                    both = [(0, 0, D), (1, 0, D)] if use[1] is None else [(use[1], 512 * use[2], 512)]
                    for n, (s, a, width) in enumerate(both):
                        out = bank[0:S, n * width:(n + 1) * width]
                        for kc in range(KC):
                            m = pe.matmul(out, xT[:, kc, s, :], w["v"][:, kc, a:a + width], start=(kc == 0),
                                          stop=(kc == KC - 1 and not bias))
                        if bias:
                            m = pe.matmul(out, ones[0:1, 0:S], w["vb"][0:1, :], start=False, stop=True)
                elif kind == "oT":
                    if use[2] == 0:
                        pe.wait_ge(on_done, q.val(8, 4 * use[1] + 4))
                    a, b = OC[use[2]]
                    for n in range(a, b):
                        m = pe.transpose(bank[:, (n - a) * S:(n - a + 1) * S], on[use[1]][0:S, n * P:(n + 1) * P],
                                         ident[0:S, 0:S])
                else:
                    for a in range(len(OC)):
                        wait_copied(pe, p, ("oT", use[1], a))
                    for n in range(KO):
                        m = pe.matmul(bank[0:S, 0:D], oT[use[1]][:, n, :], w["o"][:, n, :], start=(n == 0),
                                      stop=(n == KO - 1 and not bias))
                    if bias:
                        m = pe.matmul(bank[0:S, 0:D], ones[0:1, 0:S], w["ob"][0:1, :], start=False, stop=True)
                m.then_inc(done, 1)

            for q in w["loaded"]:
                pe.wait_ge(q, 16)
            pe.wait_ge(ones_done, 4)
            for _, use in banks.front:
                shared(None, use, Pair(0))

            def slot(p):
                for t in range(UNITS):
                    scores(p, t)
                    for use in banks.step(p, t):
                        shared(p, use, whose(p, use))
                    if t >= 2:
                        turn(p, t - 2)
                    elif not p.first:
                        turn(p.shift(-1), t + 6)
                    if t >= 3:
                        weigh(p, t - 3)
                    elif not p.first:
                        weigh(p.shift(-1), t + 5)

            run_slots(pe, slot)
            last = Pair(NPAIR - 1)
            for t in range(3):
                if t < 2:
                    turn(last, t + 6)
                weigh(last, t + 5)
            for _, use in after:
                shared(END, use, last)

        @block.scalar
        def _(act):
            def copy_out(p, use, q):
                if use[0] == "proj":
                    return
                k, n = bank_of(p, use)
                act.wait_ge(filled[k], n + 1)
                bank = psM[k]
                if use[0] == "xT":
                    m = act.activation(xT[:].rearrange("p c s k -> p (c s k)"), bank[:, 0:2 * PAIR], ACT.Copy)
                elif use[0] == "qk":
                    dst = qkT[q.p0 % 2]
                    if bias:
                        for half in range(2):
                            tile = 2 * use[1] + half
                            m = act.activation(dst[:, tile].rearrange("p s k -> p (s k)"),
                                               bank[:, half * PAIR:(half + 1) * PAIR], ACT.Identity,
                                               bias=w["qkb"][:, tile:tile + 1])
                    else:
                        m = act.activation(dst[:, 2 * use[1]:2 * use[1] + 2].rearrange("p t s k -> p (t s k)"),
                                           bank[:, 0:2 * PAIR], ACT.Copy)
                elif use[0] == "v":
                    if use[1] is None:
                        for s in range(2):
                            m = act.activation(v[q.p0 % 2][s][0:S, :, 0:HD],
                                               bank[0:S, s * D:(s + 1) * D].rearrange("p (h d) -> p h d", d=HD), ACT.Copy)
                    else:
                        hp = 512 // HD
                        m = act.activation(v[q.p0 % 2][use[1]][0:S, use[2] * hp:(use[2] + 1) * hp, 0:HD],
                                           bank[0:S, :].rearrange("p (h d) -> p h d", d=HD), ACT.Copy)
                else:
                    a, b = OC[use[2]]
                    m = act.activation(oT[use[1]][:, a:b, :].rearrange("p c k -> p (c k)"), bank[:, 0:(b - a) * S], ACT.Copy)
                m.then_inc(copied[k], 1)

            def pT_copy(p, u):
                act.wait_ge(turned, p.val(8, u + 1))
                act.activation(pT[u % 2][0:S].rearrange("p a k -> p (a k)"), psT[u % 2][0:S, 0:QCOLS],
                               ACT.Copy).then_inc(pT_done, 1)

            def exps(p, u):
                act.wait_ge(sub_done, p.val(8, u + 1))
                e = E[u % 4][0:S].rearrange("p a k -> p (a k)")
                act.activation(e, e, ACT.Exp, scale=SCALE).then_inc(exp_done, 1)

            for q in w["loaded"]:
                act.wait_ge(q, 16)
            for _, use in banks.front:
                copy_out(None, use, Pair(0))

            def slot(p):
                for t in range(UNITS):
                    exps(p, t)
                    for use in banks.step(p, t):
                        copy_out(p, use, whose(p, use))
                    if t >= 2:
                        pT_copy(p, t - 2)
                    elif not p.first:
                        pT_copy(p.shift(-1), t + 6)

            run_slots(act, slot)
            last = Pair(NPAIR - 1)
            for t in range(2):
                pT_copy(last, t + 6)
            for _, use in after:
                copy_out(END, use, last)

        @block.gpsimd
        def _(pool):
            norm.root(pool, Pair(0))

            def slot(p):
                if not p.last:
                    norm.root(pool, p.shift(1))

            run_slots(pool, slot)

        @block.vector
        def _(dve):
            def rows(p, q):
                if p is not None:
                    k, n = bank_of(before(p), ("xT",))
                    dve.wait_ge(filled[k], n + 1)
                norm.rows(dve, q, lambda s: xn[0:S, s, :], xn_done)

            def scores(p, u):
                k = u % 2
                bank = psS[k][0:S, 0:QCOLS].rearrange("p (h k) -> p h k", h=4)
                dve.wait_ge(scores_done, p.val(8, u + 1))
                dve.tensor_reduce(rmax[k][0:S, :], bank, AX.X, ALU.max).then_inc(max_done, 1)
                dve.wait_ge(max_done, p.val(8, u + 1))
                dve.tensor_tensor(E[u % 4][0:S], bank, rmax[k][0:S, :].unsqueeze(2).to_broadcast([S, 4, S]),
                                  ALU.subtract).then_inc(sub_done, 1)

            def normalise(p, u):
                k, s, r = u % 2, u // 4, u % 4
                dve.wait_ge(pv_done, p.val(8, u + 1))
                o = psO[k][0:S, 0:4 * VW].rearrange("p (h d) -> p h d", d=VW)
                dve.reciprocal(rsum[k][0:S, :].unsqueeze(2), o[:, :, HD:VW]).then_inc(rsum_done, 1)
                tile, row = head_place(0, r)
                h0 = HPT * tile + row // ROW
                dst = on[s][0:S, :].rearrange("p (h d) -> p h d", d=HD)[:, h0:h0 + 3 * HPT + 1:HPT, :]
                dve.wait_ge(rsum_done, p.val(8, u + 1))
                dve.tensor_tensor(dst, o[:, :, 0:HD], rsum[k][0:S, :].unsqueeze(2).to_broadcast([S, 4, HD]),
                                  ALU.mult).then_inc(on_done, 1)

            def residual(p, use, q):
                k, n = bank_of(p, use)
                dve.wait_ge(filled[k], n + 1)
                h = rows_of(H, q, use[1])
                dve.tensor_tensor(h, psM[k][0:S, 0:D], h, ALU.add).then_inc(copied[k], 1)

            for k in range(2):
                for s in range(2):
                    dve.memset(v[k][s][0:S, :, HD:VW], 1.0).then_inc(ones_done, 1)
            norm.moments(dve, Pair(0))
            norm.wait_moments(dve, Pair(0))
            norm.aggregate(dve, Pair(0))
            rows(None, Pair(0))

            def slot(p):
                for t in range(UNITS):
                    if t == 2 and not p.last:
                        rows(p, p.shift(1))
                    if t == 1 and not p.last:
                        norm.wait_moments(dve, p.shift(1))
                    scores(p, t)
                    if t == 0 and not p.last:
                        norm.moments(dve, p.shift(1))
                    if t == 1 and not p.last:
                        norm.aggregate(dve, p.shift(1))
                    for use in banks.step(p, t):
                        if use[0] == "proj":
                            residual(p, use, whose(p, use))
                    if t >= 3:
                        normalise(p, t - 3)
                    elif not p.first:
                        normalise(p.shift(-1), t + 5)

            run_slots(dve, slot)
            last = Pair(NPAIR - 1)
            for t in range(3):
                normalise(last, t + 5)
            for _, use in after:
                if use[0] == "proj":
                    residual(END, use, last)


def experts(nc, name, H, c, w, sb, psum, sem):
    ident, identb, sel = c["ident"], c["identb"], c["sel"]
    norm = Norm(name, c, H, sb, sem)
    xn = [sb(name + f"xn{k}", [P, 2, D], F32) for k in range(2)]
    xT = [sb(name + f"xT{k}", [P, KC, 2, S], F32) for k in range(2)]
    hT = sb(name + "hT", [EDIM, 2, S], F32)
    sim = sb(name + "sim", [P, 2, EXPERTS], F32)
    top = sb(name + "top", [P, 2, 8], F32)
    at = sb(name + "at", [P, 2, 8], U32)
    atf = sb(name + "atf", [P, 2, 8], F32)
    diff = sb(name + "diff", [P, 2, TOPK], F32)
    ew = sb(name + "ew", [P, 2, TOPK], F32)
    esum = sb(name + "esum", [P, 2, 1], F32)
    erecip = sb(name + "erecip", [P, 2, 1], F32)
    gate = sb(name + "gate", [P, 2, TOPK], F32)
    hit = sb(name + "hit", [P, 2, EXPERTS, TOPK], F32)
    wrow = sb(name + "wrow", [P, 2, EXPERTS], F32)
    wparts = sb(name + "wparts", [P, 2, 2, EXPERTS], BF16)
    wT = [sb(name + f"wT{k}", [P, 2, S], BF16) for k in range(2)]
    act_s = [sb(name + f"silu{k}", [P, 2, S], F32) for k in range(2)]
    hid = [sb(name + f"hid{k}", [P, 2, S], F32) for k in range(4)]
    step = [sb(name + f"step{s}", [P, D], F32) for s in range(2)]

    psD = [psum(name + f"psD{k}", [P, 512], F32) for k in range(2)]
    psW = [psum(name + f"psW{k}", [P, 512], F32) for k in range(2)]
    psU = [psum(name + f"psU{k}", [P, 512], F32) for k in range(2)]
    psM = [psum(name + f"psM{k}", [P, 512], F32) for k in range(2)]

    xn_done, down_done, spread_done, silu_done, hid_done, up_done, h_step, h_done = (sem(name + n) for n in (
        "xn_done", "down_done", "spread_done", "silu_done", "hid_done", "up_done", "h_step", "h_done"))
    top_done, at_done, pool_step, gate_done, gates_read, w_step, wparts_done = (sem(name + n) for n in (
        "top_done", "at_done", "pool_step", "gate_done", "gates_read", "w_step", "wparts_done"))
    filled = [sem(name + f"filled{k}") for k in range(2)]
    copied = [sem(name + f"copied{k}") for k in range(2)]

    front = [(3, ("xT",)), (5, ("hash",)), (7, ("sim",)), (14, ("wT",))]
    banks = Banks(front, front, front, [])
    NT = ETILES

    def before(p):
        return None if p.first else p.shift(-1)

    def wait_copied(eng, p, use):
        k, n = banks.at(p, use)
        eng.wait_ge(copied[k], n + 1)

    block = nc.Block()
    with block:
        @block.tensor
        def _(pe):
            def shared(p, use, q):
                k, n = banks.at(p, use)
                bank = psM[k]
                if not isinstance(n, int) or n > 0:
                    pe.wait_ge(copied[k], n)
                if use[0] == "xT":
                    pe.wait_ge(xn_done, q.val(2, 2))
                    for kc in range(KC):
                        for s in range(2):
                            m = pe.transpose(bank[:, (2 * kc + s) * S:(2 * kc + s + 1) * S],
                                             xn[q.p0 % 2][0:S, s, kc * P:(kc + 1) * P], ident[0:S, 0:S])
                elif use[0] == "hash":
                    wait_copied(pe, p, ("xT",))
                    for kc in range(KC):
                        m = pe.matmul(bank[0:EDIM, 0:PAIR], w["hash"][:, kc, :],
                                      xT[q.p0 % 2][:, kc].rearrange("p s k -> p (s k)"), start=(kc == 0), stop=(kc == KC - 1))
                elif use[0] == "sim":
                    wait_copied(pe, p, ("hash",))
                    for s in range(2):
                        m = pe.matmul(bank[0:S, s * EXPERTS:(s + 1) * EXPERTS], hT[:, s, :], w["keys"][:, :],
                                      start=True, stop=True)
                else:
                    pe.wait_ge(wparts_done, q.val(2, 2))
                    out = bank[:, :].bitcast(BF16)
                    for s in range(2):
                        m = pe.transpose(out[:, s * S:(s + 1) * S],
                                         wparts[0:S, s].rearrange("p a e -> p (a e)"), identb[0:S, 0:S])
                m.then_inc(filled[k], 1)

            def down(p, j):
                if j == 0:
                    wait_copied(pe, before(p), ("xT",))
                    wait_copied(pe, before(p), ("wT",))
                k = j % 2
                if not (p.first and j < 2):
                    pe.wait_ge(silu_done, p.val(NT, j - 1))
                for kc in range(KC):
                    m = pe.matmul(psD[k][:, 0:PAIR], w["down"][:, kc, j * P:(j + 1) * P],
                                  xT[p.p0 % 2][:, kc].rearrange("p s k -> p (s k)"), start=(kc == 0), stop=(kc == KC - 1))
                m.then_inc(down_done, 1)
                if not (p.first and j < 2):
                    pe.wait_ge(hid_done, p.val(NT, j - 1))
                pe.matmul(psW[k][:, 0:PAIR], sel[:, j, :], wT[p.p0 % 2][:].rearrange("p s k -> p (s k)"),
                          start=True, stop=True).then_inc(spread_done, 1)

            def up(p, j):
                if j == 0 and not p.first:
                    pe.wait_ge(h_step, p.val(2, 0))
                pe.wait_ge(hid_done, p.val(NT, j + 1))
                for s in range(2):
                    m = pe.matmul(psU[s][0:S, 0:D], hid[j % 4][:, s, :], w["up"][:, j, :], start=(j == 0),
                                  stop=(j == NT - 1))
                m.then_inc(up_done, 1)

            for q in w["loaded"]:
                pe.wait_ge(q, 16)
            for _, use in banks.front:
                shared(None, use, Pair(0))

            def slot(p):
                for t in range(NT):
                    down(p, t)
                    for use in banks.step(p, t):
                        shared(p, use, p.shift(1))
                    if t >= 2:
                        up(p, t - 2)
                    elif not p.first:
                        up(p.shift(-1), t + NT - 2)

            run_slots(pe, slot)
            for t in range(2):
                up(Pair(NPAIR - 1), t + NT - 2)

        @block.scalar
        def _(act):
            def copy_out(p, use, q):
                if use[0] == "sim":
                    return
                k, n = banks.at(p, use)
                act.wait_ge(filled[k], n + 1)
                if use[0] == "xT":
                    m = act.activation(xT[q.p0 % 2][:].rearrange("p c s k -> p (c s k)"), psM[k][:, 0:2 * PAIR], ACT.Copy)
                elif use[0] == "hash":
                    m = act.activation(hT[:].rearrange("p s k -> p (s k)"), psM[k][0:EDIM, 0:PAIR], ACT.Copy)
                else:
                    m = act.activation(wT[q.p0 % 2][:].rearrange("p s k -> p (s k)"),
                                       psM[k][:, :].bitcast(BF16)[:, 0:PAIR], ACT.Copy)
                m.then_inc(copied[k], 1)

            def silu(p, j):
                act.wait_ge(down_done, p.val(NT, j + 1))
                if not (p.first and j < 2):
                    act.wait_ge(hid_done, p.val(NT, j - 1))
                act.activation(act_s[j % 2][:].rearrange("p s k -> p (s k)"), psD[j % 2][:, 0:PAIR],
                               ACT.Silu).then_inc(silu_done, 1)

            for _, use in banks.front:
                copy_out(None, use, Pair(0))

            def slot(p):
                for t in range(NT):
                    silu(p, t)
                    for use in banks.step(p, t):
                        copy_out(p, use, p.shift(1))

            run_slots(act, slot)

        @block.gpsimd
        def _(pool):
            def gates(q):
                pool.wait_ge(top_done, q.val(2, 2))
                if not q.first:
                    pool.wait_ge(gates_read, q.val(4, 0))
                pool.tensor_tensor(diff[0:S], top[0:S, :, 0:TOPK], top[0:S, :, 0:1].to_broadcast([S, 2, TOPK]),
                                   ALU.subtract).then_inc(pool_step, 1)
                pool.wait_ge(pool_step, q.val(5, 1))
                pool.tensor_tensor(ew[0:S], c["e"][0:S, :].rearrange("p (s k) -> p s k", s=2), diff[0:S],
                                   ALU.pow).then_inc(pool_step, 1)
                pool.wait_ge(pool_step, q.val(5, 2))
                pool.tensor_tensor(diff[0:S, :, 0:2], ew[0:S, :, 0:2], ew[0:S, :, 2:4], ALU.add).then_inc(pool_step, 1)
                pool.wait_ge(pool_step, q.val(5, 3))
                pool.tensor_tensor(esum[0:S], diff[0:S, :, 0:1], diff[0:S, :, 1:2], ALU.add).then_inc(pool_step, 1)
                pool.wait_ge(pool_step, q.val(5, 4))
                pool.tensor_tensor(erecip[0:S], esum[0:S], c["minus1"][0:S, :].unsqueeze(2), ALU.pow).then_inc(pool_step, 1)
                pool.wait_ge(at_done, q.val(2, 2))
                pool.wait_ge(pool_step, q.val(5, 5))
                pool.tensor_tensor(gate[0:S], ew[0:S], erecip[0:S].to_broadcast([S, 2, TOPK]), ALU.mult).then_inc(gate_done, 1)
                pool.tensor_copy(atf[0:S], at[0:S]).then_inc(gate_done, 1)

            norm.root(pool, Pair(0))
            gates(Pair(0))

            def slot(p):
                if not p.last:
                    norm.root(pool, p.shift(1))
                    gates(p.shift(1))

            run_slots(pool, slot)

        @block.vector
        def _(dve):
            def rows(p, q):
                norm.rows(dve, q, lambda s: xn[q.p0 % 2][0:S, s, :], xn_done)

            def find_top(p, q):
                k, n = banks.at(p, ("sim",))
                dve.wait_ge(filled[k], n + 1)
                dve.tensor_copy(sim[0:S].rearrange("p s e -> p (s e)"), psM[k][0:S, 0:2 * EXPERTS]).then_inc(copied[k], 1)
                after_constants(dve, c)
                dve.wait_ge(copied[k], n + 1)
                for s in range(2):
                    dve.max(top[0:S, s, :], sim[0:S, s, :]).then_inc(top_done, 1)
                after_constants(dve, c)
                dve.wait_ge(top_done, q.val(2, 2))
                for s in range(2):
                    dve.max_index(at[0:S, s, :], top[0:S, s, :], sim[0:S, s, :]).then_inc(at_done, 1)

            def spread_gates(q):
                dve.wait_ge(gate_done, q.val(2, 2))
                shape = [S, EXPERTS, TOPK]
                for s in range(2):
                    dve.tensor_tensor(hit[0:S, s], c["iota"][0:S, :].unsqueeze(2).to_broadcast(shape),
                                      atf[0:S, s, 0:TOPK].unsqueeze(1).to_broadcast(shape),
                                      ALU.is_equal).then_inc(gates_read, 1)
                dve.wait_ge(gates_read, q.val(4, 2))
                for s in range(2):
                    dve.tensor_tensor(hit[0:S, s], hit[0:S, s], gate[0:S, s, :].unsqueeze(1).to_broadcast(shape),
                                      ALU.mult).then_inc(gates_read, 1)
                dve.wait_ge(gates_read, q.val(4, 4))
                dve.tensor_reduce(wrow[0:S], hit[0:S], AX.X, ALU.add).then_inc(w_step, 1)
                dve.wait_ge(w_step, q.val(2, 1))
                dve.tensor_copy(wparts[0:S, :, 0, :], wrow[0:S]).then_inc(w_step, 1)
                dve.wait_ge(w_step, q.val(2, 2))
                for s in range(2):
                    dve.tensor_tensor(wparts[0:S, s, 1, :], wrow[0:S, s, :], wparts[0:S, s, 0, :],
                                      ALU.subtract).then_inc(wparts_done, 1)

            def weigh(p, j):
                k = j % 2
                dve.wait_ge(spread_done, p.val(NT, j + 1))
                dve.wait_ge(silu_done, p.val(NT, j + 1))
                if not (p.first and j < 4):
                    dve.wait_ge(up_done, p.val(NT, j - 3))
                dve.tensor_tensor(hid[j % 4][:].rearrange("p s k -> p (s k)"), act_s[k][:].rearrange("p s k -> p (s k)"),
                                  psW[k][:, 0:PAIR], ALU.mult).then_inc(hid_done, 1)

            def residual(p):
                dve.wait_ge(up_done, p.val(NT, NT))
                for s in range(2):
                    dve.scalar_tensor_tensor(step[s][0:S, :], psU[s][0:S, 0:D], w["scale"][0:S, 0:1], xn[p.p0 % 2][0:S, s, :],
                                             ALU.mult, ALU.add).then_inc(h_step, 1)
                dve.wait_ge(h_step, p.val(2, 2))
                for s in range(2):
                    h = rows_of(H, p, s)
                    dve.tensor_tensor(h, h, step[s][0:S, :], ALU.add).then_inc(h_done, 1)

            for q in w["loaded"]:
                dve.wait_ge(q, 16)
            norm.moments(dve, Pair(0))
            norm.wait_moments(dve, Pair(0))
            norm.aggregate(dve, Pair(0))
            rows(None, Pair(0))
            find_top(None, Pair(0))
            spread_gates(Pair(0))

            def slot(p):
                for t in range(NT):
                    if t == 1 and not p.last:
                        norm.wait_moments(dve, p.shift(1))
                    if t == 2 and not p.first:
                        dve.wait_ge(h_done, p.val(2, 0))
                    weigh(p, t)
                    if t == 1 and not p.first:
                        residual(p.shift(-1))
                    if not p.last:
                        if t == 0:
                            norm.moments(dve, p.shift(1))
                        if t == 1:
                            norm.aggregate(dve, p.shift(1))
                        if t == 2:
                            rows(p, p.shift(1))
                        if t == 7:
                            find_top(p, p.shift(1))
                        if t == 12:
                            spread_gates(p.shift(1))

            run_slots(dve, slot)
            residual(Pair(NPAIR - 1))


def quant_ffn(nc, name, H, c, w, out, sb, psum, sem):
    ident, identb = c["ident"], c["identb"]
    block_sems = {}
    norm = Norm(name, c, H, sb, sem)
    xs = sb(name + "xs", [P, B, D], F32)
    wrange = sb(name + "wrange", [P, 2 * ITILES + KC], F32)
    wscale = sb(name + "wscale", [P, 2 * ITILES + KC], F32)
    wrecip = sb(name + "wrecip", [P, 2 * ITILES + KC], F32)
    rounded = sb(name + "rounded", [P, INNER], F32)
    gq = [sb(name + f"gq{k}", [P, INNER], BF16) for k in range(2)]
    guT = sb(name + "guT", [P, 2, KC, INNER], BF16)
    dT = sb(name + "dT", [P, ITILES, D], BF16)
    xabs = sb(name + "xabs", [P, NPAIR], F32)
    aabs = sb(name + "aabs", [P, 2, NPAIR], F32)
    tmp = sb(name + "tmp", [P, 16], F32)
    sig = sb(name + "sig", [P, 2, 4], F32)
    gsc = sb(name + "gsc", [P, 2 * ITILES], F32)
    downscale = sb(name + "downscale", [P, D], F32)
    diag = sb(name + "diag", [P, KC, P], F32)
    xq = [sb(name + f"xq{k}", [P, 2, D], BF16) for k in range(2)]
    xr = sb(name + "xr", [P, 2, D], F32)
    xqT = [sb(name + f"xqT{k}", [P, KC, 2, S], BF16) for k in range(2)]
    sg = [sb(name + f"sg{k}", [P, 2, S], F32) for k in range(2)]
    a = sb(name + "a", [P, ITILES, B * S], F32)
    ar = [sb(name + f"ar{k}", [P, ITILES, S], F32) for k in range(2)]
    aq = [sb(name + f"aq{k}", [P, ITILES, S], BF16) for k in range(2)]
    step = [xr[:, k, :] for k in range(2)]
    bank = [psum(name + f"ps{k}", [P, 512], F32) for k in range(8)]

    chain = sem(name + "weights_step")
    w_filled, w_copied = sem(name + "w_filled"), sem(name + "w_copied")
    xs_done, xabs_done = sem(name + "xs_done"), sem(name + "xabs_done")
    gmax_done, sig_step, sig_done = sem(name + "gmax_done"), sem(name + "sig_step"), sem(name + "sig_done")
    diag_done, spread_done = sem(name + "diag_done"), sem(name + "spread_done")
    xr_done, xq_done, xT_filled, xT_copied = (sem(name + n) for n in ("xr_done", "xq_done", "xT_filled", "xT_copied"))
    gu_done, sg_done, a_done, aabs_done = (sem(name + n) for n in ("gu_done", "sg_done", "a_done", "aabs_done"))
    ar_done, aq_step, aq_done, down_done, step_done, h_done, out_done = (sem(name + n) for n in (
        "ar_done", "aq_step", "aq_done", "down_done", "step_done", "h_done", "out_done"))

    NROWT = 2 * ITILES + KC
    tiles = [(w["gate"][0:IROWS[m], m, :], IROWS[m], D) for m in range(ITILES)]
    tiles += [(w["up"][0:IROWS[m], m, :], IROWS[m], D) for m in range(ITILES)]
    tiles += [(w["down"][:, m, :], P, INNER) for m in range(KC)]

    def columns(p):
        n = p.val(PAIR, 0)
        return bass.ds(n, PAIR) if not isinstance(n, int) else slice(n, n + PAIR)

    with nc.Block() as block:
        @block.gpsimd
        def _(pool):
            norm.root(pool, Pair(0))

            def slot(p):
                if not p.last:
                    norm.root(pool, p.shift(1))

            run_slots(pool, slot)
            for k in range(2):
                pool.tensor_scalar(sig[:, k, 0:1], w["clip"][:, k:k + 1], -1.0, None, ALU.mult).then_inc(sig_step, 1)
            pool.wait_ge(sig_step, 2)
            pool.tensor_tensor(sig[:, :, 1:2], c["e"][:, 0:2].unsqueeze(2), sig[:, :, 0:1], ALU.pow).then_inc(sig_step, 1)
            pool.wait_ge(sig_step, 3)
            pool.tensor_scalar(sig[:, :, 2:3], sig[:, :, 1:2], 1.0, None, ALU.add).then_inc(sig_done, 1)

        @block.vector
        def _(dve):
            for q in w["loaded"]:
                dve.wait_ge(q, 16)
            n = 0
            dve.memset(wrange[:], 1.0).then_inc(chain, 1)
            n += 1
            dve.wait_ge(chain, n)
            for k, (src, r, width) in enumerate(tiles):
                dve.tensor_reduce(wrange[0:r, k:k + 1], src, AX.X, ALU.max, apply_absolute_value=True).then_inc(chain, 1)
                n += 1
            dve.wait_ge(chain, n)
            dve.tensor_scalar(wscale[:], wrange[:], 1.0 / QMAX, None, ALU.mult).then_inc(chain, 1)
            n += 1
            dve.wait_ge(chain, n)
            dve.reciprocal(wrecip[:], wscale[:]).then_inc(chain, 1)
            n += 1
            dve.wait_ge(chain, n)
            for k, (src, r, width) in enumerate(tiles):
                dve.wait_ge(chain, n)
                dve.tensor_scalar(rounded[0:r, 0:width], src, wrecip[0:r, k:k + 1], ROUND, ALU.mult, ALU.add).then_inc(chain, 1)
                n += 1
                dve.wait_ge(chain, n)
                if k >= 2:
                    dve.wait_ge(w_filled, k - 1)
                dve.tensor_scalar(gq[k % 2][0:r, 0:width], rounded[0:r, 0:width], ROUND, None,
                                  ALU.subtract).then_inc(chain, 1)
                n += 1

            norm.moments(dve, Pair(0))
            norm.wait_moments(dve, Pair(0))
            norm.aggregate(dve, Pair(0))

            def slot(p):
                norm.rows(dve, p, lambda s: rows_of(xs, p, s), xs_done)
                if not p.last:
                    norm.moments(dve, p.shift(1))
                    norm.wait_moments(dve, p.shift(1))
                dve.wait_ge(xs_done, p.val(2, 2))
                b = p.val(2, 0)
                both = xs[0:S, bass.ds(b, 2), :] if not isinstance(b, int) else xs[0:S, b:b + 2, :]
                col = p.val(1, 0)
                dst = xabs[0:S, bass.ds(col, 1)] if not isinstance(col, int) else xabs[0:S, col:col + 1]
                dve.tensor_reduce(dst, both, AX.XY, ALU.max, apply_absolute_value=True).then_inc(xabs_done, 1)
                if not p.last:
                    norm.aggregate(dve, p.shift(1))

            run_slots(dve, slot)

        @block.tensor
        def _(pe):
            for k, (src, r, width) in enumerate(tiles):
                pe.wait_ge(chain, 1 + NROWT + 2 + 2 * (k + 1))
                if k >= 2:
                    pe.wait_ge(w_copied, k - 1)
                o = bank[k % 2][:, :].bitcast(BF16)
                for j in range((width + P - 1) // P):
                    cols = min(P, width - j * P)
                    m = pe.transpose(o[0:cols, j * P:j * P + r], gq[k % 2][0:r, j * P:j * P + cols], identb[0:r, 0:r])
                m.then_inc(w_filled, 1)

        @block.scalar
        def _(act):
            for k, (src, r, width) in enumerate(tiles):
                act.wait_ge(w_filled, k + 1)
                o = bank[k % 2][:, :].bitcast(BF16)
                if k < 2 * ITILES:
                    which, m = k // ITILES, k % ITILES
                    x = act.activation(guT[:, which, :, m * P:m * P + r],
                                       o[:, 0:KC * P].rearrange("p (c r) -> p c r", r=P)[:, :, 0:r], ACT.Copy)
                else:
                    half = k - 2 * ITILES
                    full = INNER // P
                    act.activation(dT[:, 0:full, half * P:(half + 1) * P],
                                   o[:, 0:full * P].rearrange("p (c r) -> p c r", r=P), ACT.Copy)
                    x = act.activation(dT[0:IROWS[-1], full, half * P:(half + 1) * P],
                                       o[0:IROWS[-1], full * P:(full + 1) * P], ACT.Copy)
                x.then_inc(w_copied, 1)

    step_sem = sem(name + "scale_step")
    gcol = sb(name + "gcol", [P, 2], F32)
    gtmp = sb(name + "gtmp", [P, 2], F32)
    sigma = sb(name + "sigma", [P, 2], F32)
    qs = sb(name + "qs", [P, 2], F32)
    qr = sb(name + "qr", [P, 2], F32)

    def global_scale(k, parts, npart):
        with nc.Block() as block:
            base = 6 * k

            @block.vector
            def _(dve):
                dve.memset(gcol[:, k:k + 1], 0.0).then_inc(step_sem, 1)
                dve.wait_ge(step_sem, base + 1)
                dve.tensor_reduce(gcol[0:npart, k:k + 1], parts, AX.XY, ALU.max).then_inc(step_sem, 1)
                dve.reciprocal(sigma[:, k:k + 1], sig[:, k, 2:3]).then_inc(step_sem, 1)
                dve.wait_ge(gmax_done, k + 1)
                dve.wait_ge(step_sem, base + 3)
                dve.tensor_scalar(qs[:, k:k + 1], gtmp[:, k:k + 1], sigma[:, k:k + 1], 1.0 / QMAX, ALU.mult,
                                  ALU.mult).then_inc(step_sem, 1)
                dve.wait_ge(step_sem, base + 4)
                dve.reciprocal(qr[:, k:k + 1], qs[:, k:k + 1]).then_inc(step_sem, 1)
                if k == 0:
                    dve.tensor_scalar(gsc[:], wscale[:, 0:2 * ITILES], qs[:, 0:1], None, ALU.mult).then_inc(step_sem, 1)
                else:
                    for h in range(KC):
                        dve.tensor_scalar(diag[:, h, :], ident[:], wscale[:, 2 * ITILES + h:2 * ITILES + h + 1],
                                          qs[:, 1:2], ALU.mult, ALU.mult).then_inc(diag_done, 1)
                    dve.wait_ge(spread_done, 1)
                    dve.tensor_copy(downscale[:], bank[0][:, 0:D]).then_inc(step_sem, 1)

            @block.gpsimd
            def _(pool):
                pool.wait_ge(step_sem, base + 2)
                pool.partition_all_reduce(gtmp[:, k:k + 1], gcol[:, k:k + 1], P,
                                          bass.bass_isa.ReduceOp.max).then_inc(gmax_done, 1)

            @block.tensor
            def _(pe):
                if k == 1:
                    pe.wait_ge(diag_done, KC)
                    pe.matmul(bank[0][:, 0:D], c["ones"][:, :], diag[:].rearrange("p h k -> p (h k)"), start=True,
                              stop=True).then_inc(spread_done, 1)

    global_scale(0, xabs[0:S, :].unsqueeze(1), S)

    with nc.Block() as block:
        M = ITILES

        @block.vector
        def _(dve):
            def quantize(q):
                b = q.val(2, 0)
                x = xs[0:S, bass.ds(b, 2), :] if not isinstance(b, int) else xs[0:S, b:b + 2, :]
                dve.tensor_scalar(x, x, qr[0:S, 0:1], QMAX, ALU.mult, ALU.min).then_inc(xr_done, 1)
                dve.wait_ge(xr_done, q.val(2, 1))
                if not q.first:
                    dve.wait_ge(xq_done, q.val(1, 0))
                dve.tensor_scalar(xr[0:S], x, -QMAX - 1.0, ROUND, ALU.max, ALU.add).then_inc(xr_done, 1)
                if not (q.first or q.p0 == 1 and q.i is None):
                    dve.wait_ge(xT_filled, q.val(1, -1))
                dve.wait_ge(xr_done, q.val(2, 2))
                dve.tensor_scalar(xq[q.p0 % 2][0:S], xr[0:S], ROUND, None, ALU.subtract).then_inc(xq_done, 1)

            def product(p, m):
                r, k = IROWS[m], m % 2
                dve.wait_ge(sg_done, p.val(M, m + 1))
                dve.scalar_tensor_tensor(a[0:r, m, columns(p)], bank[3 + (p.p0 * M + m) % 4][0:r, PAIR:2 * PAIR],
                                         gsc[0:r, ITILES + m:ITILES + m + 1], sg[k][0:r].rearrange("p s k -> p (s k)"),
                                         ALU.mult, ALU.mult).then_inc(a_done, 1)

            def absmax(p):
                dve.wait_ge(a_done, p.val(M, M))
                full = INNER // P
                n = p.val(1, 0)
                cell = bass.ds(n, 1) if not isinstance(n, int) else slice(n, n + 1)
                dve.tensor_reduce(aabs[:, 0, cell], a[:, 0:full, columns(p)], AX.XY, ALU.max,
                                  apply_absolute_value=True).then_inc(aabs_done, 1)
                r = IROWS[-1]
                dve.tensor_reduce(aabs[0:r, 1, cell], a[0:r, full, columns(p)], AX.X, ALU.max,
                                  apply_absolute_value=True).then_inc(aabs_done, 1)

            dve.memset(aabs[:], 0.0).then_inc(aabs_done, 1)
            dve.wait_ge(aabs_done, 1)
            quantize(Pair(0))

            def slot(p):
                for m in range(M):
                    product(p, m)
                    if m == 1 and not p.last:
                        quantize(p.shift(1))
                    if m == 2 and not p.first:
                        absmax(p.shift(-1))

            run_slots(dve, slot)
            absmax(Pair(NPAIR - 1))

        @block.tensor
        def _(pe):
            def turn(q):
                k = q.p0 % 2
                pe.wait_ge(xq_done, q.val(1, 1))
                if not (q.first or q.p0 == 1 and q.i is None):
                    pe.wait_ge(xT_copied, q.val(1, -1))
                o = bank[k][:, :].bitcast(BF16)
                for kc in range(KC):
                    for s in range(2):
                        m = pe.transpose(o[:, (2 * kc + s) * S:(2 * kc + s + 1) * S], xq[k][0:S, s, kc * P:(kc + 1) * P],
                                         identb[0:S, 0:S])
                m.then_inc(xT_filled, 1)

            def gate_up(p, m):
                r = IROWS[m]
                if m == 0:
                    pe.wait_ge(xT_copied, p.val(1, 1))
                if not (p.first and m < 4):
                    pe.wait_ge(a_done, p.val(M, m - 3))
                for which in range(2):
                    for kc in range(KC):
                        x = pe.matmul(bank[3 + (p.p0 * M + m) % 4][0:r, which * PAIR:(which + 1) * PAIR],
                                      guT[:, which, kc, m * P:m * P + r],
                                      xqT[p.p0 % 2][:, kc].rearrange("p s k -> p (s k)"), start=(kc == 0), stop=(kc == KC - 1))
                x.then_inc(gu_done, 1)

            turn(Pair(0))

            def slot(p):
                for m in range(M):
                    gate_up(p, m)
                    if m == 3 and not p.last:
                        turn(p.shift(1))

            run_slots(pe, slot)

        @block.scalar
        def _(act):
            def copy_out(q):
                k = q.p0 % 2
                act.wait_ge(xT_filled, q.val(1, 1))
                act.activation(xqT[k][:].rearrange("p c s k -> p (c s k)"), bank[k][:, :].bitcast(BF16)[:, 0:2 * PAIR],
                               ACT.Copy).then_inc(xT_copied, 1)

            def silu(p, m):
                r, k = IROWS[m], m % 2
                act.wait_ge(gu_done, p.val(M, m + 1))
                if not (p.first and m < 2):
                    act.wait_ge(a_done, p.val(M, m - 1))
                act.activation(sg[k][0:r].rearrange("p s k -> p (s k)"), bank[3 + (p.p0 * M + m) % 4][0:r, 0:PAIR],
                               ACT.Silu, scale=gsc[0:r, m:m + 1]).then_inc(sg_done, 1)

            copy_out(Pair(0))

            def slot(p):
                for m in range(M):
                    silu(p, m)
                    if m == 4 and not p.last:
                        copy_out(p.shift(1))

            run_slots(act, slot)

    global_scale(1, aabs[:], P)

    with nc.Block() as block:
        def sample_cols(p, s):
            n = p.val(PAIR, s * S)
            return bass.ds(n, S) if not isinstance(n, int) else slice(n, n + S)

        parts = [(P, slice(0, INNER // P)), (IROWS[-1], slice(INNER // P, ITILES))]

        @block.vector
        def _(dve):
            def quantize(p, s):
                for n, (r, t) in enumerate(parts):
                    dve.tensor_scalar(ar[s][0:r, t], a[0:r, t, sample_cols(p, s)], qr[0:r, 1:2], QMAX, ALU.mult,
                                      ALU.min).then_inc(ar_done, 1)
                dve.wait_ge(ar_done, p.val(4, 2 * s + 2))
                for n, (r, t) in enumerate(parts):
                    dve.tensor_scalar(ar[s][0:r, t], ar[s][0:r, t], -QMAX - 1.0, ROUND, ALU.max, ALU.add).then_inc(aq_step, 1)

            def residual(p, s):
                dve.wait_ge(down_done, p.val(2, s + 1))
                dve.tensor_tensor(step[s][0:S, :], bank[s][0:S, 0:D], downscale[0:S, :], ALU.mult).then_inc(step_done, 1)
                dve.wait_ge(step_done, p.val(2, s + 1))
                h = rows_of(H, p, s)
                dve.tensor_tensor(h, h, step[s][0:S, :], ALU.add).then_inc(h_done, 1)

            def slot(p):
                for s in range(2):
                    if not p.first:
                        dve.wait_ge(aq_done, p.val(4, 2 * s - 2))
                        dve.wait_ge(h_done, p.val(2, s - 1))
                    quantize(p, s)
                    if s == 1:
                        residual(p, 0)
                    elif not p.first:
                        residual(p.shift(-1), 1)

            run_slots(dve, slot)
            residual(Pair(NPAIR - 1), 1)

        @block.scalar
        def _(act):
            def slot(p):
                for s in range(2):
                    act.wait_ge(aq_step, p.val(4, 2 * s + 2))
                    if not p.first:
                        act.wait_ge(down_done, p.val(2, s - 1))
                    for r, t in parts:
                        act.activation(aq[s][0:r, t], ar[s][0:r, t], ACT.Copy, bias=-ROUND).then_inc(aq_done, 1)

            run_slots(act, slot)

        @block.tensor
        def _(pe):
            def slot(p):
                for s in range(2):
                    pe.wait_ge(aq_done, p.val(4, 2 * s + 2))
                    if not p.first:
                        pe.wait_ge(step_done, p.val(2, s - 1))
                    for m in range(ITILES):
                        r = IROWS[m]
                        x = pe.matmul(bank[s][0:S, 0:D], aq[s][0:r, m, :], dT[0:r, m, :], start=(m == 0),
                                      stop=(m == ITILES - 1))
                    x.then_inc(down_done, 1)

            run_slots(pe, slot)

        @block.sync
        def _(sp):
            def slot(p):
                for s in range(2):
                    sp.wait_ge(h_done, p.val(2, s + 1))
                    b = p.val(2, s)
                    dst = out[bass.ds(b, 1), :, :].rearrange("a s d -> (a s) d") if not isinstance(b, int) else out[b, :, :]
                    sp.dma_start(dst, rows_of(H, p, s)).then_inc(out_done, 16)

            run_slots(sp, slot)
            sp.wait_ge(out_done, 16 * B)


def program(nc, t, out):
    with ExitStack() as whole:
        def opened(stack, make):
            return lambda *a: stack.enter_context(make(*a))

        sem = opened(whole, nc.semaphore)
        sb = opened(whole, nc.sbuf_tensor)
        c = consts_on_chip(nc, sb, sem)
        made = c["made"] = sem("made")
        H = sb("H", [P, B, D], F32)

        loads = []

        def weight(stack, name, shape, load_list):
            s = stack(name, shape, F32)
            q = sem("loaded_" + name)
            loads.append((s, t[name], q))
            load_list.append(q)
            return s

        l4, l3, l2, l1, l0 = [], [], [], [], []
        w4 = {"gate": weight(sb, "f1_gate", [P, ITILES, D], l4), "up": weight(sb, "f1_up", [P, ITILES, D], l4),
              "down": weight(sb, "f1_down", [P, KC, INNER], l4), "clip": weight(sb, "f1_clip", [P, 2], l4), "loaded": l4}
        with ExitStack() as s3:
            sb3 = opened(s3, nc.sbuf_tensor)
            w3 = {"qk": weight(sb3, "a1_qk", [P, KC, 2048], l3), "v": weight(sb3, "a1_v", [P, KC, 1024], l3),
                  "o": weight(sb3, "a1_o", [P, 8, D], l3), "loaded": l3}
            with ExitStack() as s2:
                sb2 = opened(s2, nc.sbuf_tensor)
                w2 = {"down": weight(sb2, "f0_down", [P, KC, EXPERTS * EDIM], l2), "up": weight(sb2, "f0_up", [P, ETILES, D], l2),
                      "hash": weight(sb2, "f0_hash", [P, KC, EDIM], l2), "keys": weight(sb2, "f0_keys", [EDIM, EXPERTS], l2),
                      "scale": weight(sb2, "f0_scale", [P, 1], l2), "loaded": l2}
                with ExitStack() as s1:
                    sb1 = opened(s1, nc.sbuf_tensor)
                    w1 = {"qk": weight(sb1, "a0_qk", [P, KC, 1024], l1), "v": weight(sb1, "a0_v", [P, KC, D], l1),
                          "o": weight(sb1, "a0_o", [P, KC, D], l1), "qkb": weight(sb1, "a0_qkb", [P, 8], l1),
                          "vb": weight(sb1, "a0_vb", [1, D], l1), "ob": weight(sb1, "a0_ob", [1, D], l1), "loaded": l1}
                    with ExitStack() as s0:
                        embed(nc, t, H, c, made, loads, opened(s0, nc.sbuf_tensor), opened(s0, nc.psum_tensor), sem)
                    with ExitStack() as s0:
                        attention(nc, "a0_", H, c, w1, 16, opened(s0, nc.sbuf_tensor), opened(s0, nc.psum_tensor),
                                  opened(s0, nc.semaphore))
                with ExitStack() as s0:
                    experts(nc, "f0_", H, c, w2, opened(s0, nc.sbuf_tensor), opened(s0, nc.psum_tensor),
                            opened(s0, nc.semaphore))
            with ExitStack() as s0:
                attention(nc, "a1_", H, c, w3, 64, opened(s0, nc.sbuf_tensor), opened(s0, nc.psum_tensor),
                          opened(s0, nc.semaphore))
        with ExitStack() as s0:
            quant_ffn(nc, "f1_", H, c, w4, out, opened(s0, nc.sbuf_tensor), opened(s0, nc.psum_tensor),
                      opened(s0, nc.semaphore))


def embed(nc, t, H, c, made, loads, sb, psum, sem):
    tiles = [(g, min(TOK_G, B - g)) for g in range(0, B, TOK_G)]
    patches = sb("patches", [P, TOK_K, B, NIMG], F32)
    W = sb("tok_W", [P, TOK_K, D], F32)
    pos = sb("tok_pos", [TOK_G * NIMG, D], F32)
    add = sb("tok_add", [TOK_G * NIMG, D], F32)
    rows = sb("tok_rows", [TOK_G * NIMG, len(tiles), D], F32)
    idx = sb("tok_idx", [NTXT, B], I32)
    ps = [psum(f"tok_ps{k}", [P, 512], F32) for k in range(2)]
    idx_in, W_in, pos_in, words_in, images_in = (sem(n) for n in ("idx_in", "W_in", "pos_in", "words_in", "images_in"))
    patches_in = [sem(f"patches_in{k}") for k in range(TOK_K)]
    pos_done, proj_done, rows_done = sem("pos_done"), sem("proj_done"), sem("rows_done")

    with nc.Block() as block:
        @block.sync
        def _(sp):
            sp.dma_start(idx[:], t["idx"]).then_inc(idx_in, 16)
            sp.dma_start(W[:], t["tok_W"]).then_inc(W_in, 16)
            for k in range(TOK_K):
                sp.dma_start(patches[:, k].rearrange("p b n -> p (b n)"), t["patches"][:, k, :]).then_inc(patches_in[k], 16)
            sp.dma_start(pos[:], t["tok_pos"]).then_inc(pos_in, 16)
            sp.dma_start(add[:], t["tok_add"]).then_inc(pos_in, 16)
            for s, src, q in reversed(loads):
                sp.dma_start(s[:], src).then_inc(q, 16)

        @block.gpsimd
        def _(pool):
            pool.wait_ge(idx_in, 16)
            for b in range(B):
                pool.indirect_dma_start(H[NIMG:S, b, :], None, t["emb"],
                                        bass.IndirectOffsetOnAxis(ap=idx[:, b:b + 1].bitcast(U32), axis=0)).then_inc(words_in, 16)
            build_consts(pool, c, made)
            pool.wait_ge(words_in, 16 * B)

        @block.tensor
        def _(pe):
            pe.wait_ge(W_in, 16)
            for q in patches_in:
                pe.wait_ge(q, 16)
            for n, (b, g) in enumerate(tiles):
                if n >= 2:
                    pe.wait_ge(rows_done, n - 1)
                for k in range(TOK_K):
                    m = pe.matmul(ps[n % 2][0:g * NIMG, 0:D], patches[:, k, b:b + g, :].rearrange("p b n -> p (b n)"),
                                  W[:, k, :], start=(k == 0), stop=(k == TOK_K - 1))
                m.then_inc(proj_done, 1)

        @block.vector
        def _(dve):
            dve.wait_ge(pos_in, 32)
            dve.tensor_tensor(pos[:], pos[:], add[:], ALU.add).then_inc(pos_done, 1)
            dve.wait_ge(pos_done, 1)
            for n, (b, g) in enumerate(tiles):
                r = g * NIMG
                dve.wait_ge(proj_done, n + 1)
                dve.tensor_tensor(rows[0:r, n, :], ps[n % 2][0:r, 0:D], pos[0:r, :], ALU.add).then_inc(rows_done, 1)

        @block.scalar
        def _(act):
            for n, (b, g) in enumerate(tiles):
                act.wait_ge(rows_done, n + 1)
                for k in range(g):
                    act.dma_start(H[0:NIMG, b + k, :], rows[k * NIMG:(k + 1) * NIMG, n, :]).then_inc(images_in, 16)
            act.wait_ge(images_in, 16 * B)


def kernel(x, x_txt, L0_tok_W, L0_tok_b, L0_tok_pos_embedding, L0_tok_cls_token, L0_txt_embeddings, L0_attn_w_attn,
           L0_attn_b_attn, L0_attn_w_proj, L0_attn_b_proj, L0_ffn_hasher_w, L0_ffn_keys, L0_ffn_values_down,
           L0_ffn_values_up, L0_ffn_scale, L1_attn_w_q, L1_attn_w_k, L1_attn_w_v, L1_attn_w_o, L1_ffn_clip_x,
           L1_ffn_clip_down, L1_ffn_w_gate, L1_ffn_w_up, L1_ffn_w_down):
    import numpy as np
    import concourse.bacc as bacc
    from concourse.bass_utils import run_bass_kernel_spmd

    def chunked(m):
        m = np.asarray(m)
        return m.reshape(-1, P, m.shape[1]).transpose(1, 0, 2)

    def on_partitions(v):
        return np.tile(np.asarray(v).reshape(1, -1), (P, 1))

    G, PX, C = 6, 16, 3
    img = np.asarray(x).reshape(B, C, G, PX, G, PX).transpose(1, 3, 5, 0, 2, 4).reshape(C * PX * PX, B, NIMG - 1)
    patches = np.zeros((C * PX * PX, B, NIMG), img.dtype)
    patches[:, :, 1:] = img
    tok_add = np.concatenate([np.asarray(L0_tok_cls_token)[0], np.tile(np.asarray(L0_tok_b)[None], (NIMG - 1, 1))])
    wa, ba = np.asarray(L0_attn_w_attn), np.asarray(L0_attn_b_attn)
    qk = np.zeros((2, HEADS, 32, D), wa.dtype)
    qk[:, :, 0:16] = wa[0:2 * D].reshape(2, HEADS, 16, D)
    qkb = np.zeros((2, HEADS, 32), ba.dtype)
    qkb[:, :, 0:16] = ba[0:2 * D].reshape(2, HEADS, 16)
    a1_qk = np.concatenate([np.asarray(L1_attn_w_q).reshape(-1, D), np.asarray(L1_attn_w_k).reshape(-1, D)])

    def rows_padded(m):
        m = np.asarray(m)
        padded = np.zeros((ITILES * P, D), m.dtype)
        padded[0:INNER] = m
        return chunked(padded)

    arrays = {
        "idx": np.asarray(x_txt).T,
        "emb": np.asarray(L0_txt_embeddings),
        "patches": chunked(patches.reshape(C * PX * PX, B * NIMG)),
        "tok_W": chunked(np.asarray(L0_tok_W).T),
        "tok_pos": np.tile(np.asarray(L0_tok_pos_embedding)[0], (TOK_G, 1)),
        "tok_add": np.tile(tok_add, (TOK_G, 1)),
        "a0_qk": chunked(qk.reshape(-1, D).T),
        "a0_qkb": qkb.reshape(-1, P).T,
        "a0_v": chunked(wa[2 * D:].T),
        "a0_vb": ba[2 * D:].reshape(1, D),
        "a0_o": chunked(np.asarray(L0_attn_w_proj).T),
        "a0_ob": np.asarray(L0_attn_b_proj).reshape(1, D),
        "f0_hash": chunked(np.asarray(L0_ffn_hasher_w).T),
        "f0_keys": np.asarray(L0_ffn_keys).T,
        "f0_down": chunked(np.asarray(L0_ffn_values_down).transpose(1, 0, 2).reshape(D, -1)),
        "f0_up": chunked(np.asarray(L0_ffn_values_up).reshape(-1, D)),
        "f0_scale": on_partitions(L0_ffn_scale),
        "a1_qk": chunked(a1_qk.T),
        "a1_v": chunked(np.asarray(L1_attn_w_v).reshape(-1, D).T),
        "a1_o": chunked(L1_attn_w_o),
        "f1_gate": rows_padded(L1_ffn_w_gate),
        "f1_up": rows_padded(L1_ffn_w_up),
        "f1_down": chunked(L1_ffn_w_down),
        "f1_clip": on_partitions(np.concatenate([np.asarray(L1_ffn_clip_x), np.asarray(L1_ffn_clip_down)])),
    }
    arrays = {n + "_dram": np.ascontiguousarray(a) for n, a in arrays.items()}
    nc = bacc.Bacc("TRN2", target_bir_lowering=False, num_devices=1)
    t = {n[:-5]: nc.dram_tensor(n, a.shape, mybir.dt.from_np(a.dtype), kind="ExternalInput").ap() for n, a in arrays.items()}
    out = nc.dram_tensor("out_dram", (B, S, D), F32, kind="ExternalOutput").ap()
    program(nc, t, out)
    r = run_bass_kernel_spmd(nc, [arrays], core_ids=[0])
    return r.results[0]["out_dram"]
```

```python
from contextlib import ExitStack

import concourse.bass as bass
from concourse import mybir

ALU = mybir.AluOpType
ACT = mybir.ActivationFunctionType
AX = mybir.AxisListType
F32 = mybir.dt.float32
BF16 = mybir.dt.bfloat16
I32 = mybir.dt.int32
U32 = mybir.dt.uint32

P = 128
B = 32
S = 114
NIMG = 37
NTXT = 77
D = 256
KC = D // P
PAIR = 2 * S
NPAIR = B // 2
HEADS = 16
MADE = 16
UNITS = 8
QCOLS = 4 * S
MASKED = -1.0e30
EPS = 1.0e-5
TOK_K = 768 // P
TOK_G = 3
EXPERTS = 64
EDIM = 32
ETILES = EXPERTS * EDIM // P
TOPK = 4
INNER = 704
ITILES = (INNER + P - 1) // P
IROWS = [min(P, INNER - P * m) for m in range(ITILES)]
QMAX = 127.0
ALL = slice(None)
ROUND = 12582912.0
E_CONST = 2.718281828459045


class Pair:

    def __init__(self, p0, i=None):
        self.p0, self.i = p0, i
        self.first = i is None and p0 == 0
        self.last = i is None and p0 == NPAIR - 1

    def val(self, a, c):
        n = a * self.p0 + c
        return n if self.i is None else self.i * (2 * a) + n

    def shift(self, n):
        return Pair(self.p0 + n, self.i)


def run_slots(eng, slot):
    slot(Pair(0))
    with eng.Fori(0, (NPAIR - 2) // 2) as i:
        slot(Pair(1, i))
        slot(Pair(2, i))
    slot(Pair(NPAIR - 1))


def rows_of(H, p, s):
    b = p.val(2, s)
    if isinstance(b, int):
        return H[0:S, b, :]
    return H[0:S, bass.ds(b, 1), :].rearrange("p a d -> p (a d)")


def pair_of(x, p):
    b = p.val(2, 0)
    return x[0:S, b:b + 2, :] if isinstance(b, int) else x[0:S, bass.ds(b, 2), :]


def cell(x, p):
    n = p.val(1, 0)
    return x[:, n:n + 1] if isinstance(n, int) else x[:, bass.ds(n, 1)]


class Banks:

    def __init__(self, front, first, middle, last, after=()):
        self.front, self.first, self.middle, self.last, self.after = front, first, middle, last, list(after)

    def uses(self, p):
        if p is None:
            return self.front
        if p.i is None and p.p0 == NPAIR:
            return self.after
        return self.first if p.first else self.last if p.last else self.middle

    def count(self, p, use, kinds=None):
        def of(uses):
            return sum(kinds is None or u[0] in kinds for _, u in uses)

        names = [u for _, u in self.uses(p)]
        k = of(self.uses(p)[:names.index(use)])
        if p is None:
            return 0, k
        if p.first:
            return 0, of(self.front) + k
        a = of(self.middle)
        if p.i is None and p.p0 == NPAIR:
            return 0, of(self.front) + of(self.first) + a * (NPAIR - 2) + of(self.last) + k
        return a, of(self.front) + of(self.first) - a + k

    def at(self, p, use):
        a, c = self.count(p, use)
        whole = c if a == 0 else a * p.p0 + c
        return whole % 2, whole // 2 if a == 0 or p.i is None else p.i * a + whole // 2

    def nth(self, p, use, kinds):
        a, c = self.count(p, use, kinds)
        return c + 1 if a == 0 else p.val(a, c + 1)

    def step(self, p, t):
        return [u for at, u in self.uses(p) if at == t]


def matmul3(pe, out, a, b, start, stop):
    (ah, al), (bh, bl) = a, b
    pe.matmul(out, ah, bh, start=start, stop=False, skip_group_check=True)
    pe.matmul(out, ah, bl, start=False, stop=False, skip_group_check=True)
    return pe.matmul(out, al, bh, start=False, stop=stop, skip_group_check=True)


def both(pair, *index):
    return tuple(x[index] for x in pair)


def consts_on_chip(nc, sb, sem):
    c = {
        "ident": sb("ident", [P, P], F32), "identb": sb("identb", [P, P], BF16),
        "mask": sb("mask", [P, 4, S], BF16), "neghalf": sb("neghalf", [P, 2], F32),
        "eps": sb("eps", [P, 2], F32), "round": sb("round", [P, 2], F32), "minus1": sb("minus1", [P, 2], F32), "ones": sb("ones", [P, P], F32), "e": sb("e_const", [P, 8], F32),
        "iota": sb("iota", [P, EXPERTS], F32), "sel": sb("sel", [P, ETILES, P], BF16),
    }
    return c


def build_consts(pool, c, made):
    n = 0
    for name, value in (("ident", 0.0), ("identb", 0.0), ("mask", 0.0), ("neghalf", -0.5), ("minus1", -1.0), ("round", ROUND), ("eps", EPS), ("ones", 1.0),
                        ("e", E_CONST), ("sel", 0.0)):
        pool.memset(c[name][:], value).then_inc(made, 1)
        n += 1
    pool.iota(c["iota"][:], pattern=[[1, EXPERTS]], base=0, channel_multiplier=0,
              allow_small_or_imprecise_dtypes=True).then_inc(made, 1)
    n += 1
    pool.wait_ge(made, n)
    for name in ("ident", "identb"):
        pool.affine_select(out=c[name][:], in_=c[name][:], compare_op=ALU.not_equal, fill=1.0, base=0,
                           pattern=[[-1, P]], channel_multiplier=1).then_inc(made, 1)
        n += 1
    pool.affine_select(out=c["mask"][:], in_=c["mask"][:], compare_op=ALU.is_ge, fill=MASKED, base=0,
                       pattern=[[0, 4], [-1, S]], channel_multiplier=1).then_inc(made, 1)
    n += 1
    v = c["sel"][:].rearrange("p j (q r) -> p j q r", r=EDIM)
    for base in (0, -EXPERTS):
        pool.affine_select(out=v, in_=v, compare_op=ALU.not_equal, fill=1.0, base=base,
                           pattern=[[-(P // EDIM), ETILES], [-1, P // EDIM], [0, EDIM]],
                           channel_multiplier=1).then_inc(made, 1)
        n += 1
        pool.wait_ge(made, n)
    return n


def after_constants(eng, c):
    eng.wait_ge(c["made"], 1)


class Norm:

    def __init__(self, name, c, H, sb, sem):
        self.c, self.H = c, H
        self.stats = sb(name + "stats", [P, 2, 6], F32)
        self.mv = sb(name + "mv", [P, 2, 2], F32)
        self.vareps = sb(name + "vareps", [P, 2], F32)
        self.rstd = sb(name + "rstd", [P, 2], F32)
        self.stats_done, self.mv_done = sem(name + "stats_done"), sem(name + "mv_done")
        self.vareps_done, self.rstd_done = sem(name + "vareps_done"), sem(name + "rstd_done")

    def moments(self, dve, q):
        for s in range(2):
            dve.bn_stats(self.stats[0:S, s, :], rows_of(self.H, q, s)).then_inc(self.stats_done, 1)

    def wait_moments(self, dve, q):
        dve.wait_ge(self.stats_done, q.val(2, 2))

    def aggregate(self, dve, q):
        for s in range(2):
            dve.bn_aggr(self.mv[0:S, s, :], self.stats[0:S, s, :]).then_inc(self.mv_done, 1)

    def root(self, pool, q):
        pool.wait_ge(self.mv_done, q.val(2, 2))
        pool.tensor_tensor(self.vareps[0:S, :], self.mv[0:S, :, 1], self.c["eps"][0:S, :], ALU.add).then_inc(self.vareps_done, 1)
        pool.wait_ge(self.vareps_done, q.val(1, 1))
        pool.tensor_tensor(self.rstd[0:S, :], self.vareps[0:S, :], self.c["neghalf"][0:S, :],
                           ALU.pow).then_inc(self.rstd_done, 1)

    def rows(self, dve, q, dst, ready):
        dve.wait_ge(self.rstd_done, q.val(1, 1))
        for s in range(2):
            dve.tensor_scalar(dst(s), rows_of(self.H, q, s), self.mv[0:S, s, 0:1], self.rstd[0:S, s:s + 1],
                              ALU.subtract, ALU.mult).then_inc(ready, 1)


def attention(nc, name, H, c, w, HD, sb, psum, sem, final=None):
    ident, identb, mask, ones = c["ident"], c["identb"], c["mask"], c["ones"]
    ROW = 32 if HD == 16 else 64
    HPT = P // ROW
    QT = HEADS // HPT
    VN = HEADS * HD
    KO = VN // P
    VW = HD + 1
    bias = HD == 16
    SCALE = float(HD) ** -0.5

    norm = Norm(name, c, H, sb, sem)
    xn = sb(name + "xn", [P, 2, D], F32)
    xT = [sb(name + f"xT_{h}", [P, KC, 2, S], BF16) for h in ("high", "low")]
    qkT = [[sb(name + f"qkT{k}_{h}", [P, 2 * QT, 2, S], BF16) for h in ("high", "low")] for k in range(2)]
    v = [[sb(name + f"v{k}{s}", [P, HEADS, VW], F32) for s in range(2)] for k in range(2)]
    E = [sb(name + f"E{k}", [P, 4, S], F32) for k in range(4)]
    rmax = [sb(name + f"rmax{k}", [P, 4], F32) for k in range(2)]
    pT = [sb(name + f"pT{k}", [P, 4, S], F32) for k in range(2)]
    rsum = [sb(name + f"rsum{k}", [P, 4], F32) for k in range(2)]
    on = [sb(name + f"on{s}", [P, VN], F32) for s in range(2)]
    oT = [[sb(name + f"oT{s}_{h}", [P, KO, S], BF16) for h in ("high", "low")] for s in range(2)]

    psS = [psum(name + f"psS{k}", [P, 512], F32) for k in range(2)]
    psT = [psum(name + f"psT{k}", [P, 512], F32) for k in range(2)]
    psO = [psum(name + f"psO{k}", [P, 512], F32) for k in range(2)]
    psM = [psum(name + f"psM{k}", [P, 512], F32) for k in range(2)]

    xn_done, ones_done = sem(name + "xn_done"), sem(name + "ones_done")
    scores_done, max_done, sub_done, exp_done = (sem(name + n) for n in ("scores_done", "max_done", "sub_done", "exp_done"))
    turned, pT_done, pv_done, rsum_done, on_done = (sem(name + n) for n in ("turned", "pT_done", "pv_done", "rsum_done", "on_done"))
    filled = [sem(name + f"filled{k}") for k in range(2)]
    copied = [sem(name + f"copied{k}") for k in range(2)]
    high_done = sem(name + "high_done")
    SPLIT = ("xT", "qk", "oT")

    VH = [(s, h) for s in range(2) for h in range(max(1, VN // 512))] if VN > D else [(None, 0)]
    OC = [(a, min(a + 4, KO)) for a in range(0, KO, 4)]
    front = [(1, ("xT",))] + [((2, 3, 4, 6)[4 * j // QT], ("qk", j)) for j in range(QT)]
    front += [(7, ("v", s, h)) for s, h in VH]
    turn0 = [(7, ("oT", 0, a)) for a in range(len(OC))]
    tail = [(0, ("proj", 0))] + [(3, ("oT", 1, a)) for a in range(len(OC))] + [(5, ("proj", 1))]

    def merged(*parts):
        return sorted((x for part in parts for x in part), key=lambda x: x[0])

    banks = Banks(front, front + turn0, merged(tail, front, turn0), tail + turn0, tail)
    END = Pair(NPAIR)
    LATE = (1, 2)
    bank_of = banks.at

    def before(p):
        return None if p.first else p.shift(-1)

    def wait_copied(eng, p, use):
        k, n = bank_of(p, use)
        eng.wait_ge(copied[k], n + 1)

    def head_place(i, r):
        if HPT == 4:
            return i, ROW * r
        return 4 * (r // 2) + i, ROW * (r % 2)

    def whose(p, use):
        if use[0] in ("xT", "qk", "v"):
            return p.shift(1)
        return p if use[:2] == ("oT", 0) else p.shift(-1)

    block = nc.Block()
    with block:
        @block.tensor
        def _(pe):
            def bank_free(p, use):
                k, n = bank_of(p, use)
                if not isinstance(n, int) or n > 0:
                    pe.wait_ge(copied[k], n)
                return psM[k], filled[k]

            def scores(p, u):
                k, s, r = u % 2, u // 4, u % 4
                if u == 0:
                    for j in (QT - 2, QT - 1):
                        wait_copied(pe, before(p), ("qk", j))
                if not (p.first and u < 2):
                    pe.wait_ge(sub_done, p.val(8, u - 1))
                pe.matmul(psS[k][0:S, 0:QCOLS], identb[0:S, 0:S], mask[0:S].rearrange("p a k -> p (a k)"),
                          start=True, stop=False, skip_group_check=True)
                qk = qkT[p.p0 % 2]
                for i in range(4):
                    tile, row = head_place(i, r)
                    ps = slice(row, row + HD)
                    m = matmul3(pe, psS[k][0:S, i * S:(i + 1) * S], both(qk, ps, tile, s), both(qk, ps, QT + tile, s),
                                start=False, stop=(i == 3))
                m.then_inc(scores_done, 1)

            def turn(p, u):
                k = u % 2
                pe.wait_ge(exp_done, p.val(8, u + 1))
                for i in range(4):
                    m = pe.transpose(psT[k][0:S, i * S:(i + 1) * S], E[u % 4][0:S, i, :], ident[0:S, 0:S])
                m.then_inc(turned, 1)

            def weigh(p, u):
                k, s, r = u % 2, u // 4, u % 4
                if u == 0:
                    for x in VH[-2:]:
                        wait_copied(pe, before(p), ("v", *x))
                pe.wait_ge(pT_done, p.val(8, u + 1))
                if not (p.first and u < 2):
                    pe.wait_ge(on_done, p.val(8, u - 1))
                for i in range(4):
                    tile, row = head_place(i, r)
                    m = pe.matmul(psO[k][0:S, i * VW:(i + 1) * VW], pT[k][0:S, i, :],
                                  v[p.p0 % 2][s][0:S, HPT * tile + row // ROW, :], start=True, stop=True)
                m.then_inc(pv_done, 1)

            def shared(p, use, q):
                kind = use[0]
                bank, done = bank_free(p, use)
                if kind == "xT":
                    pe.wait_ge(xn_done, q.val(2, 2))
                    for kc in range(KC):
                        for s in range(2):
                            m = pe.transpose(bank[:, (2 * kc + s) * S:(2 * kc + s + 1) * S],
                                             xn[0:S, s, kc * P:(kc + 1) * P], ident[0:S, 0:S])
                elif kind == "qk":
                    if use[1] == 0:
                        wait_copied(pe, p, ("xT",))
                    for half in range(2):
                        tile = 2 * use[1] + half
                        for kc in range(KC):
                            m = matmul3(pe, bank[:, half * PAIR:(half + 1) * PAIR],
                                        both(w["qk"], ALL, kc, slice(tile * P, (tile + 1) * P)),
                                        [x[:, kc].rearrange("p s k -> p (s k)") for x in xT],
                                        start=(kc == 0), stop=(kc == KC - 1))
                elif kind == "v":
                    parts = [(0, 0, D), (1, 0, D)] if use[1] is None else [(use[1], 512 * use[2], 512)]
                    for n, (s, a, width) in enumerate(parts):
                        out = bank[0:S, n * width:(n + 1) * width]
                        for kc in range(KC):
                            m = matmul3(pe, out, both(xT, ALL, kc, s), both(w["v"], ALL, kc, slice(a, a + width)),
                                        start=(kc == 0), stop=(kc == KC - 1 and not bias))
                        if bias:
                            m = pe.matmul(out, ones[0:1, 0:S], w["vb"][0:1, :], start=False, stop=True, skip_group_check=True)
                elif kind == "oT":
                    if use[2] == 0:
                        pe.wait_ge(on_done, q.val(8, 4 * use[1] + 4))
                    a, b = OC[use[2]]
                    for n in range(a, b):
                        m = pe.transpose(bank[:, (n - a) * S:(n - a + 1) * S], on[use[1]][0:S, n * P:(n + 1) * P],
                                         ident[0:S, 0:S])
                else:
                    for a in range(len(OC)):
                        wait_copied(pe, p if use[1] else p.shift(-1), ("oT", use[1], a))
                    for n in range(KO):
                        m = matmul3(pe, bank[0:S, 0:D], both(oT[use[1]], ALL, n), both(w["o"], ALL, n), start=(n == 0),
                                    stop=(n == KO - 1 and not bias))
                    if bias:
                        m = pe.matmul(bank[0:S, 0:D], ones[0:1, 0:S], w["ob"][0:1, :], start=False, stop=True,
                                      skip_group_check=True)
                m.then_inc(done, 1)

            def uses(p, t):
                for use in banks.step(p, t):
                    shared(p, use, whose(p, use))

            pe.wait_ge(ones_done, 4)
            for _, use in banks.front:
                shared(None, use, Pair(0))

            def slot(p):
                for t in range(UNITS):
                    scores(p, t)
                    if t not in LATE:
                        uses(p, t)
                    if t >= 2:
                        turn(p, t - 2)
                    elif not p.first:
                        turn(p.shift(-1), t + 6)
                    if t >= 3:
                        weigh(p, t - 3)
                    elif not p.first:
                        weigh(p.shift(-1), t + 5)
                    if t in LATE:
                        uses(p, t)

            run_slots(pe, slot)
            last = Pair(NPAIR - 1)
            for t in range(3):
                if t < 2:
                    turn(last, t + 6)
                weigh(last, t + 5)
            for _, use in banks.after:
                shared(END, use, last)

        @block.scalar
        def _(act):
            def copy_out(p, use, q):
                if use[0] == "proj":
                    return
                k, n = bank_of(p, use)
                act.wait_ge(filled[k], n + 1)
                bank = psM[k]
                if use[0] == "xT":
                    m = act.activation(xT[0][:].rearrange("p c s k -> p (c s k)"), bank[:, 0:2 * PAIR], ACT.Copy)
                elif use[0] == "qk":
                    dst = qkT[q.p0 % 2][0]
                    if bias:
                        for half in range(2):
                            tile = 2 * use[1] + half
                            m = act.activation(dst[:, tile].rearrange("p s k -> p (s k)"),
                                               bank[:, half * PAIR:(half + 1) * PAIR], ACT.Identity,
                                               bias=w["qkb"][:, tile:tile + 1])
                    else:
                        m = act.activation(dst[:, 2 * use[1]:2 * use[1] + 2].rearrange("p t s k -> p (t s k)"),
                                           bank[:, 0:2 * PAIR], ACT.Copy)
                elif use[0] == "v":
                    if use[1] is None:
                        for s in range(2):
                            m = act.activation(v[q.p0 % 2][s][0:S, :, 0:HD],
                                               bank[0:S, s * D:(s + 1) * D].rearrange("p (h d) -> p h d", d=HD), ACT.Copy)
                    else:
                        hp = 512 // HD
                        m = act.activation(v[q.p0 % 2][use[1]][0:S, use[2] * hp:(use[2] + 1) * hp, 0:HD],
                                           bank[0:S, :].rearrange("p (h d) -> p h d", d=HD), ACT.Copy)
                else:
                    a, b = OC[use[2]]
                    m = act.activation(oT[use[1]][0][:, a:b, :].rearrange("p c k -> p (c k)"), bank[:, 0:(b - a) * S],
                                       ACT.Copy)
                m.then_inc(high_done if use[0] in SPLIT else copied[k], 1)

            def pT_copy(p, u):
                act.wait_ge(turned, p.val(8, u + 1))
                act.activation(pT[u % 2][0:S].rearrange("p a k -> p (a k)"), psT[u % 2][0:S, 0:QCOLS],
                               ACT.Copy).then_inc(pT_done, 1)

            def exps(p, u):
                act.wait_ge(sub_done, p.val(8, u + 1))
                e = E[u % 4][0:S].rearrange("p a k -> p (a k)")
                act.activation(e, e, ACT.Exp, scale=SCALE).then_inc(exp_done, 1)

            for _, use in banks.front:
                copy_out(None, use, Pair(0))

            def slot(p):
                for t in range(UNITS):
                    uses = banks.step(p, t)
                    first = 0 if t in LATE else 1
                    for use in uses[:first]:
                        copy_out(p, use, whose(p, use))
                    exps(p, t)
                    if t not in LATE:
                        for use in uses[first:]:
                            copy_out(p, use, whose(p, use))
                    if t >= 2:
                        pT_copy(p, t - 2)
                    elif not p.first:
                        pT_copy(p.shift(-1), t + 6)
                    if t in LATE:
                        for use in uses:
                            copy_out(p, use, whose(p, use))

            run_slots(act, slot)
            last = Pair(NPAIR - 1)
            for t in range(2):
                pT_copy(last, t + 6)
            for _, use in banks.after:
                copy_out(END, use, last)

        @block.gpsimd
        def _(pool):
            norm.root(pool, Pair(0))

            def slot(p):
                if not p.last:
                    norm.root(pool, p.shift(1))
                if final and not p.first:
                    final["norm"].root(pool, p.shift(-1))

            run_slots(pool, slot)
            if final:
                final["norm"].root(pool, Pair(NPAIR - 1))

        @block.vector
        def _(dve):
            def rows(p, q):
                if p is not None:
                    k, n = bank_of(before(p), ("xT",))
                    dve.wait_ge(filled[k], n + 1)
                norm.rows(dve, q, lambda s: xn[0:S, s, :], xn_done)

            def scores(p, u):
                k = u % 2
                bank = psS[k][0:S, 0:QCOLS].rearrange("p (h k) -> p h k", h=4)
                dve.wait_ge(scores_done, p.val(8, u + 1))
                dve.tensor_reduce(rmax[k][0:S, :], bank, AX.X, ALU.max).then_inc(max_done, 1)
                dve.wait_ge(max_done, p.val(8, u + 1))
                dve.tensor_tensor(E[u % 4][0:S], bank, rmax[k][0:S, :].unsqueeze(2).to_broadcast([S, 4, S]),
                                  ALU.subtract).then_inc(sub_done, 1)

            def normalise(p, u):
                k, s, r = u % 2, u // 4, u % 4
                dve.wait_ge(pv_done, p.val(8, u + 1))
                o = psO[k][0:S, 0:4 * VW].rearrange("p (h d) -> p h d", d=VW)
                dve.reciprocal(rsum[k][0:S, :].unsqueeze(2), o[:, :, HD:VW]).then_inc(rsum_done, 1)
                tile, row = head_place(0, r)
                h0 = HPT * tile + row // ROW
                dst = on[s][0:S, :].rearrange("p (h d) -> p h d", d=HD)[:, h0:h0 + 3 * HPT + 1:HPT, :]
                dve.wait_ge(rsum_done, p.val(8, u + 1))
                dve.tensor_tensor(dst, o[:, :, 0:HD], rsum[k][0:S, :].unsqueeze(2).to_broadcast([S, 4, HD]),
                                  ALU.mult).then_inc(on_done, 1)

            def low_half(p, use, q):
                k, n = bank_of(p, use)
                bank = psM[k]
                dve.wait_ge(high_done, banks.nth(p, use, SPLIT))
                if use[0] == "xT":
                    high, low = (x[:].rearrange("p c s k -> p (c s k)") for x in xT)
                    m = dve.tensor_tensor(low, bank[:, 0:2 * PAIR], high, ALU.subtract)
                elif use[0] == "qk" and bias:
                    for half in range(2):
                        tile = 2 * use[1] + half
                        high, low = (x[:, tile].rearrange("p s k -> p (s k)") for x in qkT[q.p0 % 2])
                        m = dve.scalar_tensor_tensor(low, bank[:, half * PAIR:(half + 1) * PAIR], w["qkb"][:, tile:tile + 1],
                                                     high, ALU.add, ALU.subtract)
                elif use[0] == "qk":
                    high, low = (x[:, 2 * use[1]:2 * use[1] + 2].rearrange("p t s k -> p (t s k)") for x in qkT[q.p0 % 2])
                    m = dve.tensor_tensor(low, bank[:, 0:2 * PAIR], high, ALU.subtract)
                else:
                    a, b = OC[use[2]]
                    high, low = (x[:, a:b, :].rearrange("p c k -> p (c k)") for x in oT[use[1]])
                    m = dve.tensor_tensor(low, bank[:, 0:(b - a) * S], high, ALU.subtract)
                m.then_inc(copied[k], 1)

            def residual(p, use, q):
                k, n = bank_of(p, use)
                dve.wait_ge(filled[k], n + 1)
                h = rows_of(H, q, use[1])
                dve.tensor_tensor(h, psM[k][0:S, 0:D], h, ALU.add).then_inc(copied[k], 1)

            def shared(p, use, q):
                if use[0] in SPLIT:
                    low_half(p, use, q)
                elif use[0] == "proj":
                    residual(p, use, q)

            def uses(p, t):
                for use in banks.step(p, t):
                    shared(p, use, whose(p, use))

            def final_rows(q):
                final["norm"].rows(dve, q, lambda s: rows_of(final["x"], q, s), final["x_done"])
                dve.wait_ge(final["x_done"], q.val(2, 2))
                dve.tensor_reduce(cell(final["absmax"][0:S], q), pair_of(final["x"], q), AX.XY, ALU.max,
                                  apply_absolute_value=True).then_inc(final["absmax_done"], 1)

            for k in range(2):
                for s in range(2):
                    dve.memset(v[k][s][0:S, :, HD:VW], 1.0).then_inc(ones_done, 1)
            norm.moments(dve, Pair(0))
            norm.wait_moments(dve, Pair(0))
            norm.aggregate(dve, Pair(0))
            rows(None, Pair(0))
            for _, use in banks.front:
                shared(None, use, Pair(0))

            def slot(p):
                for t in range(UNITS):
                    if t == 1 and not p.last:
                        rows(p, p.shift(1))
                    if t == 0 and not p.last:
                        norm.moments(dve, p.shift(1))
                        norm.wait_moments(dve, p.shift(1))
                    if final and t == 6 and not p.first:
                        final["norm"].wait_moments(dve, p.shift(-1))
                    scores(p, t)
                    if final and t == 6 and not p.first:
                        final["norm"].aggregate(dve, p.shift(-1))
                    if t == 0 and not p.last:
                        norm.aggregate(dve, p.shift(1))
                    if t not in LATE:
                        uses(p, t)
                    if final and t == 5 and not p.first:
                        wait_copied(dve, p, ("proj", 1))
                    if t >= 3:
                        normalise(p, t - 3)
                    elif not p.first:
                        normalise(p.shift(-1), t + 5)
                    if t in LATE:
                        uses(p, t)
                    if final and t == 5 and not p.first:
                        final["norm"].moments(dve, p.shift(-1))
                if final and not p.first:
                    final_rows(p.shift(-1))

            run_slots(dve, slot)
            last = Pair(NPAIR - 1)
            for t in range(3):
                normalise(last, t + 5)
            for _, use in banks.after:
                shared(END, use, last)
            if final:
                wait_copied(dve, END, ("proj", 1))
                final["norm"].moments(dve, last)
                final["norm"].wait_moments(dve, last)
                final["norm"].aggregate(dve, last)
                final_rows(last)


def experts(nc, name, H, c, w, sb, psum, sem):
    ident, identb, sel = c["ident"], c["identb"], c["sel"]
    norm = Norm(name, c, H, sb, sem)
    xn = [sb(name + f"xn{k}", [P, 2, D], F32) for k in range(2)]
    xT = [[sb(name + f"xT{k}_{h}", [P, KC, 2, S], BF16) for h in ("high", "low")] for k in range(2)]
    hT = sb(name + "hT", [EDIM, 2, S], F32)
    sim = sb(name + "sim", [P, 2, EXPERTS], F32)
    top = sb(name + "top", [P, 2, 8], F32)
    at = sb(name + "at", [P, 2, 8], U32)
    atf = sb(name + "atf", [P, 2, 8], F32)
    diff = sb(name + "diff", [P, 2, TOPK], F32)
    ew = sb(name + "ew", [P, 2, TOPK], F32)
    esum = sb(name + "esum", [P, 2, 1], F32)
    erecip = sb(name + "erecip", [P, 2, 1], F32)
    gate = sb(name + "gate", [P, 2, TOPK], F32)
    hit = sb(name + "hit", [P, 2, EXPERTS, TOPK], F32)
    wrow = sb(name + "wrow", [P, 2, EXPERTS], F32)
    wparts = sb(name + "wparts", [P, 2, 2, EXPERTS], BF16)
    wT = [sb(name + f"wT{k}", [P, 2, S], BF16) for k in range(2)]
    act_s = [sb(name + f"silu{k}", [P, 2, S], F32) for k in range(2)]
    hid = [sb(name + f"hid{k}", [P, 2, S], F32) for k in range(2)]
    hid2 = [[sb(name + f"hid{k}_{h}", [P, 2, S], BF16) for h in ("high", "low")] for k in range(4)]
    step = [sb(name + f"step{s}", [P, D], F32) for s in range(2)]

    psD = [psum(name + f"psD{k}", [P, 512], F32) for k in range(2)]
    psW = [psum(name + f"psW{k}", [P, 512], F32) for k in range(2)]
    psU = [psum(name + f"psU{k}", [P, 512], F32) for k in range(2)]
    psM = [psum(name + f"psM{k}", [P, 512], F32) for k in range(2)]

    xn_done, down_done, spread_done, silu_done, up_done, h_step, h_done = (sem(name + n) for n in (
        "xn_done", "down_done", "spread_done", "silu_done", "up_done", "h_step", "h_done"))
    hid_done, hid_high, hid_low, high_done = (sem(name + n) for n in ("hid_done", "hid_high", "hid_low", "high_done"))
    top_done, at_done, pool_step, gate_done, gates_read, w_step, wparts_done = (sem(name + n) for n in (
        "top_done", "at_done", "pool_step", "gate_done", "gates_read", "w_step", "wparts_done"))
    filled = [sem(name + f"filled{k}") for k in range(2)]
    copied = [sem(name + f"copied{k}") for k in range(2)]

    front = [(3, ("xT",)), (5, ("hash",)), (7, ("sim",)), (14, ("wT",))]
    banks = Banks(front, front, front, [])
    NT = ETILES
    LAG = 3

    def before(p):
        return None if p.first else p.shift(-1)

    def wait_copied(eng, p, use):
        k, n = banks.at(p, use)
        eng.wait_ge(copied[k], n + 1)

    block = nc.Block()
    with block:
        @block.tensor
        def _(pe):
            def shared(p, use, q):
                k, n = banks.at(p, use)
                bank = psM[k]
                if not isinstance(n, int) or n > 0:
                    pe.wait_ge(copied[k], n)
                if use[0] == "xT":
                    pe.wait_ge(xn_done, q.val(2, 2))
                    for kc in range(KC):
                        for s in range(2):
                            m = pe.transpose(bank[:, (2 * kc + s) * S:(2 * kc + s + 1) * S],
                                             xn[q.p0 % 2][0:S, s, kc * P:(kc + 1) * P], ident[0:S, 0:S])
                elif use[0] == "hash":
                    wait_copied(pe, p, ("xT",))
                    for kc in range(KC):
                        m = matmul3(pe, bank[0:EDIM, 0:PAIR], both(w["hash"], ALL, kc),
                                    [x[:, kc].rearrange("p s k -> p (s k)") for x in xT[q.p0 % 2]],
                                    start=(kc == 0), stop=(kc == KC - 1))
                elif use[0] == "sim":
                    wait_copied(pe, p, ("hash",))
                    for s in range(2):
                        m = pe.matmul(bank[0:S, s * EXPERTS:(s + 1) * EXPERTS], hT[:, s, :], w["keys"][:, :],
                                      start=True, stop=True)
                else:
                    pe.wait_ge(wparts_done, q.val(2, 2))
                    out = bank[:, :].bitcast(BF16)
                    for s in range(2):
                        m = pe.transpose(out[:, s * S:(s + 1) * S],
                                         wparts[0:S, s].rearrange("p a e -> p (a e)"), identb[0:S, 0:S])
                m.then_inc(filled[k], 1)

            def down(p, j):
                if j == 0:
                    wait_copied(pe, before(p), ("xT",))
                    wait_copied(pe, before(p), ("wT",))
                k = j % 2
                if not (p.first and j < 2):
                    pe.wait_ge(silu_done, p.val(NT, j - 1))
                for kc in range(KC):
                    m = matmul3(pe, psD[k][:, 0:PAIR], both(w["down"], ALL, kc, slice(j * P, (j + 1) * P)),
                                [x[:, kc].rearrange("p s k -> p (s k)") for x in xT[p.p0 % 2]],
                                start=(kc == 0), stop=(kc == KC - 1))
                m.then_inc(down_done, 1)
                if not (p.first and j < 2):
                    pe.wait_ge(hid_done, p.val(NT, j - 1))
                pe.matmul(psW[k][:, 0:PAIR], sel[:, j, :], wT[p.p0 % 2][:].rearrange("p s k -> p (s k)"),
                          start=True, stop=True).then_inc(spread_done, 1)

            def up(p, j):
                if j == 0 and not p.first:
                    pe.wait_ge(h_step, p.val(2, 0))
                pe.wait_ge(hid_low, p.val(NT, j + 1))
                for s in range(2):
                    m = matmul3(pe, psU[s][0:S, 0:D], both(hid2[j % 4], ALL, s), both(w["up"], ALL, j), start=(j == 0),
                                stop=(j == NT - 1))
                m.then_inc(up_done, 1)

            for _, use in banks.front:
                shared(None, use, Pair(0))

            def slot(p):
                for t in range(NT):
                    down(p, t)
                    for use in banks.step(p, t):
                        shared(p, use, p.shift(1))
                    if t >= LAG:
                        up(p, t - LAG)
                    elif not p.first:
                        up(p.shift(-1), t + NT - LAG)

            run_slots(pe, slot)
            for t in range(LAG):
                up(Pair(NPAIR - 1), t + NT - LAG)

        @block.scalar
        def _(act):
            def copy_out(p, use, q):
                if use[0] == "sim":
                    return
                k, n = banks.at(p, use)
                act.wait_ge(filled[k], n + 1)
                if use[0] == "xT":
                    m = act.activation(xT[q.p0 % 2][0][:].rearrange("p c s k -> p (c s k)"), psM[k][:, 0:2 * PAIR], ACT.Copy)
                elif use[0] == "hash":
                    m = act.activation(hT[:].rearrange("p s k -> p (s k)"), psM[k][0:EDIM, 0:PAIR], ACT.Copy)
                else:
                    m = act.activation(wT[q.p0 % 2][:].rearrange("p s k -> p (s k)"),
                                       psM[k][:, :].bitcast(BF16)[:, 0:PAIR], ACT.Copy)
                m.then_inc(high_done if use[0] == "xT" else copied[k], 1)

            def high_half(p, j):
                act.wait_ge(hid_done, p.val(NT, j + 1))
                if not (p.first and j < 4):
                    act.wait_ge(up_done, p.val(NT, j - 3))
                act.activation(hid2[j % 4][0][:].rearrange("p s k -> p (s k)"), hid[j % 2][:].rearrange("p s k -> p (s k)"),
                               ACT.Copy).then_inc(hid_high, 1)

            def silu(p, j):
                act.wait_ge(down_done, p.val(NT, j + 1))
                if not (p.first and j < 2):
                    act.wait_ge(hid_done, p.val(NT, j - 1))
                act.activation(act_s[j % 2][:].rearrange("p s k -> p (s k)"), psD[j % 2][:, 0:PAIR],
                               ACT.Silu).then_inc(silu_done, 1)

            for _, use in banks.front:
                copy_out(None, use, Pair(0))

            def slot(p):
                for t in range(NT):
                    silu(p, t)
                    if t >= 1:
                        high_half(p, t - 1)
                    elif not p.first:
                        high_half(p.shift(-1), NT - 1)
                    for use in banks.step(p, t):
                        copy_out(p, use, p.shift(1))

            run_slots(act, slot)
            high_half(Pair(NPAIR - 1), NT - 1)

        @block.gpsimd
        def _(pool):
            def gates(q):
                pool.wait_ge(top_done, q.val(2, 2))
                if not q.first:
                    pool.wait_ge(gates_read, q.val(4, 0))
                pool.tensor_tensor(diff[0:S], top[0:S, :, 0:TOPK], top[0:S, :, 0:1].to_broadcast([S, 2, TOPK]),
                                   ALU.subtract).then_inc(pool_step, 1)
                pool.wait_ge(pool_step, q.val(5, 1))
                pool.tensor_tensor(ew[0:S], c["e"][0:S, :].rearrange("p (s k) -> p s k", s=2), diff[0:S],
                                   ALU.pow).then_inc(pool_step, 1)
                pool.wait_ge(pool_step, q.val(5, 2))
                pool.tensor_tensor(diff[0:S, :, 0:2], ew[0:S, :, 0:2], ew[0:S, :, 2:4], ALU.add).then_inc(pool_step, 1)
                pool.wait_ge(pool_step, q.val(5, 3))
                pool.tensor_tensor(esum[0:S], diff[0:S, :, 0:1], diff[0:S, :, 1:2], ALU.add).then_inc(pool_step, 1)
                pool.wait_ge(pool_step, q.val(5, 4))
                pool.tensor_tensor(erecip[0:S], esum[0:S], c["minus1"][0:S, :].unsqueeze(2), ALU.pow).then_inc(pool_step, 1)
                pool.wait_ge(at_done, q.val(2, 2))
                pool.wait_ge(pool_step, q.val(5, 5))
                pool.tensor_tensor(gate[0:S], ew[0:S], erecip[0:S].to_broadcast([S, 2, TOPK]), ALU.mult).then_inc(gate_done, 1)
                pool.tensor_copy(atf[0:S], at[0:S]).then_inc(gate_done, 1)

            norm.root(pool, Pair(0))
            gates(Pair(0))

            def slot(p):
                if not p.last:
                    norm.root(pool, p.shift(1))
                    gates(p.shift(1))

            run_slots(pool, slot)

        @block.vector
        def _(dve):
            def rows(p, q):
                norm.rows(dve, q, lambda s: xn[q.p0 % 2][0:S, s, :], xn_done)

            def find_top(p, q):
                k, n = banks.at(p, ("sim",))
                dve.wait_ge(filled[k], n + 1)
                dve.tensor_copy(sim[0:S].rearrange("p s e -> p (s e)"), psM[k][0:S, 0:2 * EXPERTS]).then_inc(copied[k], 1)
                after_constants(dve, c)
                dve.wait_ge(copied[k], n + 1)
                for s in range(2):
                    dve.max(top[0:S, s, :], sim[0:S, s, :]).then_inc(top_done, 1)
                after_constants(dve, c)
                dve.wait_ge(top_done, q.val(2, 2))
                for s in range(2):
                    dve.max_index(at[0:S, s, :], top[0:S, s, :], sim[0:S, s, :]).then_inc(at_done, 1)

            def spread_gates(q):
                dve.wait_ge(gate_done, q.val(2, 2))
                shape = [S, EXPERTS, TOPK]
                for s in range(2):
                    dve.tensor_tensor(hit[0:S, s], c["iota"][0:S, :].unsqueeze(2).to_broadcast(shape),
                                      atf[0:S, s, 0:TOPK].unsqueeze(1).to_broadcast(shape),
                                      ALU.is_equal).then_inc(gates_read, 1)
                dve.wait_ge(gates_read, q.val(4, 2))
                for s in range(2):
                    dve.tensor_tensor(hit[0:S, s], hit[0:S, s], gate[0:S, s, :].unsqueeze(1).to_broadcast(shape),
                                      ALU.mult).then_inc(gates_read, 1)
                dve.wait_ge(gates_read, q.val(4, 4))
                dve.tensor_reduce(wrow[0:S], hit[0:S], AX.X, ALU.add).then_inc(w_step, 1)
                dve.wait_ge(w_step, q.val(2, 1))
                dve.tensor_copy(wparts[0:S, :, 0, :], wrow[0:S]).then_inc(w_step, 1)
                dve.wait_ge(w_step, q.val(2, 2))
                for s in range(2):
                    dve.tensor_tensor(wparts[0:S, s, 1, :], wrow[0:S, s, :], wparts[0:S, s, 0, :],
                                      ALU.subtract).then_inc(wparts_done, 1)

            def weigh(p, j):
                k = j % 2
                dve.wait_ge(spread_done, p.val(NT, j + 1))
                dve.wait_ge(silu_done, p.val(NT, j + 1))
                if not (p.first and j < 2):
                    dve.wait_ge(hid_low, p.val(NT, j - 1))
                dve.tensor_tensor(hid[j % 2][:].rearrange("p s k -> p (s k)"), act_s[k][:].rearrange("p s k -> p (s k)"),
                                  psW[k][:, 0:PAIR], ALU.mult).then_inc(hid_done, 1)

            def low_half(p, j):
                dve.wait_ge(hid_high, p.val(NT, j + 1))
                high, low = (x[:].rearrange("p s k -> p (s k)") for x in hid2[j % 4])
                dve.tensor_tensor(low, hid[j % 2][:].rearrange("p s k -> p (s k)"), high, ALU.subtract).then_inc(hid_low, 1)

            def low_of_rows(p, q):
                k, _ = banks.at(p, ("xT",))
                dve.wait_ge(high_done, banks.nth(p, ("xT",), ("xT",)))
                high, low = (x[:].rearrange("p c s k -> p (c s k)") for x in xT[q.p0 % 2])
                dve.tensor_tensor(low, psM[k][:, 0:2 * PAIR], high, ALU.subtract).then_inc(copied[k], 1)

            def residual(p):
                dve.wait_ge(up_done, p.val(NT, NT))
                for s in range(2):
                    dve.scalar_tensor_tensor(step[s][0:S, :], psU[s][0:S, 0:D], w["scale"][0:S, 0:1], xn[p.p0 % 2][0:S, s, :],
                                             ALU.mult, ALU.add).then_inc(h_step, 1)
                dve.wait_ge(h_step, p.val(2, 2))
                for s in range(2):
                    h = rows_of(H, p, s)
                    dve.tensor_tensor(h, h, step[s][0:S, :], ALU.add).then_inc(h_done, 1)

            norm.moments(dve, Pair(0))
            norm.wait_moments(dve, Pair(0))
            norm.aggregate(dve, Pair(0))
            rows(None, Pair(0))
            low_of_rows(None, Pair(0))
            find_top(None, Pair(0))
            spread_gates(Pair(0))

            def slot(p):
                for t in range(NT):
                    if t == 1 and not p.last:
                        norm.wait_moments(dve, p.shift(1))
                    if t == LAG and not p.first:
                        dve.wait_ge(h_done, p.val(2, 0))
                    weigh(p, t)
                    if t == LAG - 1 and not p.first:
                        residual(p.shift(-1))
                    if t >= 1:
                        low_half(p, t - 1)
                    elif not p.first:
                        low_half(p.shift(-1), NT - 1)
                    if not p.last:
                        if t == 0:
                            norm.moments(dve, p.shift(1))
                        if t == 1:
                            norm.aggregate(dve, p.shift(1))
                        if t == 2:
                            rows(p, p.shift(1))
                        if t == 3:
                            low_of_rows(p, p.shift(1))
                        if t == 7:
                            find_top(p, p.shift(1))
                        if t == 12:
                            spread_gates(p.shift(1))

            run_slots(dve, slot)
            low_half(Pair(NPAIR - 1), NT - 1)
            residual(Pair(NPAIR - 1))


def quant_ffn(nc, name, H, c, w, out, sb, psum, sem):
    ident, identb = c["ident"], c["identb"]
    xs, xabs, guT, dT, wscale = w["x"], w["absmax"], w["guT"], w["dT"], w["scale"]
    aabs = sb(name + "aabs", [P, NPAIR], F32)
    sig = sb(name + "sig", [P, 2, 4], F32)
    gsc = sb(name + "gsc", [P, 2 * ITILES], F32)
    downscale = sb(name + "downscale", [P, D], F32)
    diag = sb(name + "diag", [P, KC, P], F32)
    xq = [sb(name + f"xq{k}", [P, 2, D], BF16) for k in range(2)]
    xr = sb(name + "xr", [P, 2, D], F32)
    xqT = [sb(name + f"xqT{k}", [P, KC, 2, S], BF16) for k in range(2)]
    sg = [sb(name + f"sg{k}", [P, 2, S], F32) for k in range(2)]
    a = sb(name + "a", [P, ITILES, B * S], F32)
    ar = [sb(name + f"ar{k}", [P, ITILES, S], F32) for k in range(2)]
    ac = [sb(name + f"ac{k}", [P, ITILES, S], BF16) for k in range(2)]
    aq = [sb(name + f"aq{k}", [P, ITILES, S], BF16) for k in range(2)]
    step = [xr[:, k, :] for k in range(2)]
    bank = [psum(name + f"ps{k}", [P, 512], F32) for k in range(8)]

    pad_done = sem(name + "pad_done")
    gmax_done, sig_step, sig_done = sem(name + "gmax_done"), sem(name + "sig_step"), sem(name + "sig_done")
    diag_done, spread_done = sem(name + "diag_done"), sem(name + "spread_done")
    xr_done, xq_done, xT_filled, xT_copied = (sem(name + n) for n in ("xr_done", "xq_done", "xT_filled", "xT_copied"))
    gu_done, sg_done, a_done, aabs_done = (sem(name + n) for n in ("gu_done", "sg_done", "a_done", "aabs_done"))
    ar_done, aq_step, aq_done, down_done, step_done, h_done, out_done = (sem(name + n) for n in (
        "ar_done", "aq_step", "aq_done", "down_done", "step_done", "h_done", "out_done"))

    def columns(p):
        n = p.val(PAIR, 0)
        return bass.ds(n, PAIR) if not isinstance(n, int) else slice(n, n + PAIR)

    step_sem = sem(name + "scale_step")
    gcol = sb(name + "gcol", [P, 2], F32)
    gtmp = sb(name + "gtmp", [P, 2], F32)
    sigma = sb(name + "sigma", [P, 2], F32)
    qs = sb(name + "qs", [P, 2], F32)
    qr = sb(name + "qr", [P, 2], F32)

    def global_scale(k, parts, npart):
        with nc.Block() as block:
            base = 6 * k

            @block.vector
            def _(dve):
                dve.memset(gcol[:, k:k + 1], 0.0).then_inc(step_sem, 1)
                dve.wait_ge(step_sem, base + 1)
                dve.tensor_reduce(gcol[0:npart, k:k + 1], parts, AX.XY, ALU.max).then_inc(step_sem, 1)
                dve.wait_ge(sig_done, 1)
                dve.reciprocal(sigma[:, k:k + 1], sig[:, k, 2:3]).then_inc(step_sem, 1)
                dve.wait_ge(gmax_done, k + 1)
                dve.wait_ge(step_sem, base + 3)
                dve.tensor_scalar(qs[:, k:k + 1], gtmp[:, k:k + 1], sigma[:, k:k + 1], 1.0 / QMAX, ALU.mult,
                                  ALU.mult).then_inc(step_sem, 1)
                dve.wait_ge(step_sem, base + 4)
                dve.reciprocal(qr[:, k:k + 1], qs[:, k:k + 1]).then_inc(step_sem, 1)
                if k == 0:
                    dve.tensor_scalar(gsc[:], wscale[:, 0:2 * ITILES], qs[:, 0:1], None, ALU.mult).then_inc(step_sem, 1)
                else:
                    for h in range(KC):
                        dve.tensor_scalar(diag[:, h, :], ident[:], wscale[:, 2 * ITILES + h:2 * ITILES + h + 1],
                                          qs[:, 1:2], ALU.mult, ALU.mult).then_inc(diag_done, 1)
                    dve.wait_ge(spread_done, 1)
                    dve.tensor_copy(downscale[:], bank[0][:, 0:D]).then_inc(step_sem, 1)

            @block.gpsimd
            def _(pool):
                if k == 0:
                    for n in range(2):
                        pool.tensor_scalar(sig[:, n, 0:1], w["clip"][:, n:n + 1], -1.0, None, ALU.mult).then_inc(sig_step, 1)
                    pool.wait_ge(sig_step, 2)
                    pool.tensor_tensor(sig[:, :, 1:2], c["e"][:, 0:2].unsqueeze(2), sig[:, :, 0:1], ALU.pow).then_inc(sig_step, 1)
                    pool.wait_ge(sig_step, 3)
                    pool.tensor_scalar(sig[:, :, 2:3], sig[:, :, 1:2], 1.0, None, ALU.add).then_inc(sig_done, 1)
                pool.wait_ge(step_sem, base + 2)
                pool.partition_all_reduce(gtmp[:, k:k + 1], gcol[:, k:k + 1], P,
                                          bass.bass_isa.ReduceOp.max).then_inc(gmax_done, 1)

            @block.tensor
            def _(pe):
                if k == 1:
                    pe.wait_ge(diag_done, KC)
                    pe.matmul(bank[0][:, 0:D], c["ones"][:, :], diag[:].rearrange("p h k -> p (h k)"), start=True,
                              stop=True).then_inc(spread_done, 1)

    global_scale(0, xabs[0:S, :].unsqueeze(1), S)

    with nc.Block() as block:
        M = ITILES

        @block.gpsimd
        def _(pool):
            pool.memset(a[IROWS[-1]:P, ITILES - 1, :], 0.0).then_inc(pad_done, 1)

        @block.vector
        def _(dve):
            def quantize(q):
                b = q.val(2, 0)
                x = xs[0:S, bass.ds(b, 2), :] if not isinstance(b, int) else xs[0:S, b:b + 2, :]
                dve.tensor_scalar(x, x, qr[0:S, 0:1], QMAX, ALU.mult, ALU.min).then_inc(xr_done, 1)
                dve.wait_ge(xr_done, q.val(2, 1))
                if not q.first:
                    dve.wait_ge(xq_done, q.val(1, 0))
                dve.tensor_scalar(xr[0:S], x, -QMAX - 1.0, ROUND, ALU.max, ALU.add).then_inc(xr_done, 1)
                if not (q.first or q.p0 == 1 and q.i is None):
                    dve.wait_ge(xT_filled, q.val(1, -1))
                dve.wait_ge(xr_done, q.val(2, 2))
                dve.tensor_scalar(xq[q.p0 % 2][0:S], xr[0:S], ROUND, None, ALU.subtract).then_inc(xq_done, 1)

            def product(p, m):
                r, k = IROWS[m], m % 2
                dve.wait_ge(sg_done, p.val(M, m + 1))
                dve.scalar_tensor_tensor(a[0:r, m, columns(p)], bank[3 + (p.p0 * M + m) % 4][0:r, PAIR:2 * PAIR],
                                         gsc[0:r, ITILES + m:ITILES + m + 1], sg[k][0:r].rearrange("p s k -> p (s k)"),
                                         ALU.mult, ALU.mult).then_inc(a_done, 1)

            def absmax(p):
                dve.wait_ge(a_done, p.val(M, M))
                dve.tensor_reduce(cell(aabs, p), a[:, :, columns(p)], AX.XY, ALU.max,
                                  apply_absolute_value=True).then_inc(aabs_done, 1)

            dve.wait_ge(pad_done, 1)
            quantize(Pair(0))

            def slot(p):
                for m in range(M):
                    product(p, m)
                    if m == 1 and not p.last:
                        quantize(p.shift(1))
                    if m == 2 and not p.first:
                        absmax(p.shift(-1))

            run_slots(dve, slot)
            absmax(Pair(NPAIR - 1))

        @block.tensor
        def _(pe):
            def turn(q):
                k = q.p0 % 2
                pe.wait_ge(xq_done, q.val(1, 1))
                if not (q.first or q.p0 == 1 and q.i is None):
                    pe.wait_ge(xT_copied, q.val(1, -1))
                o = bank[k][:, :].bitcast(BF16)
                for kc in range(KC):
                    for s in range(2):
                        m = pe.transpose(o[:, (2 * kc + s) * S:(2 * kc + s + 1) * S], xq[k][0:S, s, kc * P:(kc + 1) * P],
                                         identb[0:S, 0:S])
                m.then_inc(xT_filled, 1)

            def gate_up(p, m):
                r = IROWS[m]
                if m == 0:
                    pe.wait_ge(xT_copied, p.val(1, 1))
                if not (p.first and m < 4):
                    pe.wait_ge(a_done, p.val(M, m - 3))
                for which in range(2):
                    for kc in range(KC):
                        x = pe.matmul(bank[3 + (p.p0 * M + m) % 4][0:r, which * PAIR:(which + 1) * PAIR],
                                      guT[:, which, kc, m * P:m * P + r],
                                      xqT[p.p0 % 2][:, kc].rearrange("p s k -> p (s k)"), start=(kc == 0), stop=(kc == KC - 1))
                x.then_inc(gu_done, 1)

            turn(Pair(0))

            def slot(p):
                for m in range(M):
                    gate_up(p, m)
                    if m == 3 and not p.last:
                        turn(p.shift(1))

            run_slots(pe, slot)

        @block.scalar
        def _(act):
            def copy_out(q):
                k = q.p0 % 2
                act.wait_ge(xT_filled, q.val(1, 1))
                act.activation(xqT[k][:].rearrange("p c s k -> p (c s k)"), bank[k][:, :].bitcast(BF16)[:, 0:2 * PAIR],
                               ACT.Copy).then_inc(xT_copied, 1)

            def silu(p, m):
                r, k = IROWS[m], m % 2
                act.wait_ge(gu_done, p.val(M, m + 1))
                if not (p.first and m < 2):
                    act.wait_ge(a_done, p.val(M, m - 1))
                act.activation(sg[k][0:r].rearrange("p s k -> p (s k)"), bank[3 + (p.p0 * M + m) % 4][0:r, 0:PAIR],
                               ACT.Silu, scale=gsc[0:r, m:m + 1]).then_inc(sg_done, 1)

            copy_out(Pair(0))

            def slot(p):
                for m in range(M):
                    silu(p, m)
                    if m == 4 and not p.last:
                        copy_out(p.shift(1))

            run_slots(act, slot)

    global_scale(1, aabs[:].unsqueeze(1), P)

    with nc.Block() as block:
        def sample_cols(p, s):
            n = p.val(PAIR, s * S)
            return bass.ds(n, S) if not isinstance(n, int) else slice(n, n + S)

        @block.vector
        def _(dve):
            def clip(p, s):
                dve.wait_ge(ar_done, p.val(2, s + 1))
                dve.tensor_scalar(ac[s][:], ar[s][:], ROUND, QMAX, ALU.subtract, ALU.min).then_inc(aq_step, 1)
                dve.wait_ge(aq_step, p.val(2, s + 1))
                dve.tensor_scalar(aq[s][:], ac[s][:], -QMAX - 1.0, None, ALU.max).then_inc(aq_done, 1)

            def residual(p, s):
                dve.wait_ge(down_done, p.val(2, s + 1))
                dve.tensor_tensor(step[s][0:S, :], bank[s][0:S, 0:D], downscale[0:S, :], ALU.mult).then_inc(step_done, 1)
                dve.wait_ge(step_done, p.val(2, s + 1))
                h = rows_of(H, p, s)
                dve.tensor_tensor(h, h, step[s][0:S, :], ALU.add).then_inc(h_done, 1)

            def slot(p):
                for s in range(2):
                    if not p.first:
                        dve.wait_ge(aq_done, p.val(2, s - 1))
                        dve.wait_ge(down_done, p.val(2, s - 1))
                        dve.wait_ge(h_done, p.val(2, s - 1))
                    clip(p, s)
                    if s == 1:
                        residual(p, 0)
                    elif not p.first:
                        residual(p.shift(-1), 1)

            run_slots(dve, slot)
            residual(Pair(NPAIR - 1), 1)

        @block.scalar
        def _(act):
            def slot(p):
                for s in range(2):
                    if not p.first:
                        act.wait_ge(aq_step, p.val(2, s - 1))
                    act.activation(ar[s][:], a[:, :, sample_cols(p, s)], ACT.Identity, bias=c["round"][:, 0:1],
                                   scale=qr[:, 1:2]).then_inc(ar_done, 1)

            run_slots(act, slot)

        @block.tensor
        def _(pe):
            def slot(p):
                for s in range(2):
                    pe.wait_ge(aq_done, p.val(2, s + 1))
                    if not p.first:
                        pe.wait_ge(step_done, p.val(2, s - 1))
                    for m in range(ITILES):
                        r = IROWS[m]
                        x = pe.matmul(bank[s][0:S, 0:D], aq[s][0:r, m, :], dT[0:r, m, :], start=(m == 0),
                                      stop=(m == ITILES - 1))
                    x.then_inc(down_done, 1)

            run_slots(pe, slot)

        @block.sync
        def _(sp):
            def slot(p):
                for s in range(2):
                    sp.wait_ge(h_done, p.val(2, s + 1))
                    b = p.val(2, s)
                    dst = out[bass.ds(b, 1), :, :].rearrange("a s d -> (a s) d") if not isinstance(b, int) else out[b, :, :]
                    sp.dma_start(dst, rows_of(H, p, s)).then_inc(out_done, 16)

            run_slots(sp, slot)
            sp.wait_ge(out_done, 16 * B)


def program(nc, t, out):
    with ExitStack() as whole:
        def opened(stack, make):
            return lambda *a: stack.enter_context(make(*a))

        sem = opened(whole, nc.semaphore)
        sb = opened(whole, nc.sbuf_tensor)
        c = consts_on_chip(nc, sb, sem)
        made = c["made"] = sem("made")
        H = sb("H", [P, B, D], F32)
        f1 = {
            "x": sb("f1_x", [P, B, D], F32), "absmax": sb("f1_absmax", [P, NPAIR], F32),
            "guT": sb("f1_guT", [P, 2, KC, INNER], BF16), "dT": sb("f1_dT", [P, ITILES, D], BF16),
            "scale": sb("f1_scale", [P, 2 * ITILES + KC], F32), "clip": sb("f1_clip", [P, 2], F32),
        }
        plain, split = [("f1_clip", f1["clip"][:])], []

        def halves(sb, name, shape):
            pair = [sb(name + "_" + h, shape, BF16) for h in ("high", "low")]
            split.append((name, pair))
            return pair

        def small(sb, name, shape):
            x = sb(name, shape, F32)
            plain.append((name, x[:]))
            return x

        with ExitStack() as s3:
            sb3 = opened(s3, nc.sbuf_tensor)
            a1 = {"qk": halves(sb3, "a1_qk", [P, KC, 2048]), "v": halves(sb3, "a1_v", [P, KC, 1024]),
                  "o": halves(sb3, "a1_o", [P, 8, D])}
            with ExitStack() as s2:
                sb2 = opened(s2, nc.sbuf_tensor)
                f0 = {"down": halves(sb2, "f0_down", [P, KC, EXPERTS * EDIM]), "up": halves(sb2, "f0_up", [P, ETILES, D]),
                      "hash": halves(sb2, "f0_hash", [P, KC, EDIM]), "keys": small(sb2, "f0_keys", [EDIM, EXPERTS]),
                      "scale": small(sb2, "f0_scale", [P, 1])}
                with ExitStack() as s1:
                    sb1 = opened(s1, nc.sbuf_tensor)
                    a0 = {"qk": halves(sb1, "a0_qk", [P, KC, 1024]), "v": halves(sb1, "a0_v", [P, KC, D]),
                          "o": halves(sb1, "a0_o", [P, KC, D]), "qkb": small(sb1, "a0_qkb", [P, 8]),
                          "vb": small(sb1, "a0_vb", [1, D]), "ob": small(sb1, "a0_ob", [1, D])}
                    with ExitStack() as s0:
                        embed(nc, t, H, c, made, plain, split, f1, opened(s0, nc.sbuf_tensor), opened(s0, nc.psum_tensor), sem)
                    with ExitStack() as s0:
                        attention(nc, "a0_", H, c, a0, 16, opened(s0, nc.sbuf_tensor), opened(s0, nc.psum_tensor),
                                  opened(s0, nc.semaphore))
                with ExitStack() as s0:
                    experts(nc, "f0_", H, c, f0, opened(s0, nc.sbuf_tensor), opened(s0, nc.psum_tensor),
                            opened(s0, nc.semaphore))
            with ExitStack() as s0:
                own = opened(s0, nc.sbuf_tensor)
                final = {"norm": Norm("a1_final_", c, H, own, sem), "x": f1["x"], "absmax": f1["absmax"],
                         "x_done": sem("f1_x_done"), "absmax_done": sem("f1_absmax_done")}
                attention(nc, "a1_", H, c, a1, 64, own, opened(s0, nc.psum_tensor), opened(s0, nc.semaphore), final)
        with ExitStack() as s0:
            quant_ffn(nc, "f1_", H, c, f1, out, opened(s0, nc.sbuf_tensor), opened(s0, nc.psum_tensor),
                      opened(s0, nc.semaphore))


def embed(nc, t, H, c, made, plain, split, f1, sb, psum, sem):
    tiles = [(g, min(TOK_G, B - g)) for g in range(0, B, TOK_G)]
    NT, TW = len(tiles), TOK_K * TOK_G * NIMG
    W = sb("tok_W", [P, TOK_K, D], F32)
    pos = sb("tok_pos", [TOK_G * NIMG, D], F32)
    add = sb("tok_add", [TOK_G * NIMG, D], F32)
    rows = sb("tok_rows", [TOK_G * NIMG, NT, D], F32)
    idx = sb("tok_idx", [NTXT, B], I32)
    spare = f1["x"][:].rearrange("p b d -> p (b d)")
    patches = spare[:, 0:NT * TW].rearrange("p (t k n) -> p t k n", k=TOK_K, n=TOK_G * NIMG)
    ps = [psum(f"tok_ps{k}", [P, 512], F32) for k in range(4)]
    idx_in, W_in, pos_in, words_in, images_in, plain_in = (sem(n) for n in (
        "idx_in", "W_in", "pos_in", "words_in", "images_in", "plain_in"))
    patches_in = [sem(f"patches_in{k}") for k in range(NT)]
    pos_done, proj_done, rows_done = sem("pos_done"), sem("proj_done"), sem("rows_done")

    RING, CHUNK = 3, 768
    raw = [sb(f"raw{k}", [P, CHUNK], F32) for k in range(RING)]
    raw_in = [sem(f"raw_in{k}") for k in range(RING)]
    high_done, low_done = sem("high_done"), sem("low_done")
    chunks = []
    for name, pair in reversed(split):
        flat = [x[:].rearrange("p a n -> p (a n)") for x in pair]
        src = t[name].rearrange("p a n -> p (a n)")
        n = src.shape[1]
        for a in range(0, n, CHUNK):
            b = min(a + CHUNK, n)
            chunks.append((src[:, a:b], flat[0][:, a:b], flat[1][:, a:b], b - a))

    f1_in = sem("f1_in")
    quant = {n: sb("raw_" + n, shape, F32) for n, shape in (
        ("f1_gate", [P, ITILES, D]), ("f1_up", [P, ITILES, D]), ("f1_down", [P, KC, INNER]))}
    wtiles = [(quant[n][0:IROWS[m], m, :], IROWS[m], D) for n in ("f1_gate", "f1_up") for m in range(ITILES)]
    wtiles += [(quant["f1_down"][:, m, :], P, INNER) for m in range(KC)]
    NW = len(wtiles)
    wrange = sb("wrange", [P, NW], F32)
    wrecip = sb("wrecip", [P, NW], F32)
    rounded = spare[:, NT * TW:NT * TW + INNER]
    wq = [sb(f"wq{k}", [P, INNER], BF16) for k in range(2)]
    range_done, scale_done, recip_done = sem("range_done"), sem("scale_done"), sem("recip_done")
    wround_done, wq_done, w_filled, w_copied = sem("wround_done"), sem("wq_done"), sem("w_filled"), sem("w_copied")

    with nc.Block() as block:
        @block.sync
        def _(sp):
            sp.dma_start(idx[:], t["idx"]).then_inc(idx_in, 16)
            for n, q in quant.items():
                sp.dma_start(q[:], t[n]).then_inc(f1_in, 16)
            sp.dma_start(W[:], t["tok_W"]).then_inc(W_in, 16)
            sp.dma_start(pos[:], t["tok_pos"]).then_inc(pos_in, 16)
            sp.dma_start(add[:], t["tok_add"]).then_inc(pos_in, 16)
            for name, dst in plain:
                sp.dma_start(dst, t[name]).then_inc(plain_in, 16)
            for n in range(max(NT, len(chunks))):
                if n < NT:
                    sp.dma_start(patches[:, n].rearrange("p k n -> p (k n)"), t["patches"][n]).then_inc(patches_in[n], 16)
                if n < len(chunks):
                    if n >= RING:
                        sp.wait_ge(low_done, n - RING + 1)
                    sp.dma_start(raw[n % RING][:, 0:chunks[n][3]], chunks[n][0]).then_inc(raw_in[n % RING], 16)
            sp.wait_ge(plain_in, 16 * len(plain))

        @block.gpsimd
        def _(pool):
            build_consts(pool, c, made)
            pool.wait_ge(idx_in, 16)
            for b in range(B):
                pool.indirect_dma_start(H[NIMG:S, b, :], None, t["emb"],
                                        bass.IndirectOffsetOnAxis(ap=idx[:, b:b + 1].bitcast(U32), axis=0)).then_inc(words_in, 16)
            for n, (b, g) in enumerate(tiles):
                pool.wait_ge(rows_done, n + 1)
                for k in range(g):
                    pool.dma_start(H[0:NIMG, b + k, :], rows[k * NIMG:(k + 1) * NIMG, n, :]).then_inc(images_in, 16)
            pool.wait_ge(words_in, 16 * B)
            pool.wait_ge(images_in, 16 * B)

        @block.tensor
        def _(pe):
            def weight_tile(k):
                _, r, width = wtiles[k]
                pe.wait_ge(wq_done, k + 1)
                if k >= 2:
                    pe.wait_ge(w_copied, k - 1)
                o = ps[2 + k % 2][:, :].bitcast(BF16)
                for j in range((width + P - 1) // P):
                    cols = min(P, width - j * P)
                    m = pe.transpose(o[0:cols, j * P:j * P + r], wq[k % 2][0:r, j * P:j * P + cols], c["identb"][0:r, 0:r])
                m.then_inc(w_filled, 1)

            def patch_tile(n):
                r = tiles[n][1] * NIMG
                pe.wait_ge(patches_in[n], 16)
                if n >= 2:
                    pe.wait_ge(rows_done, n - 1)
                for k in range(TOK_K):
                    m = pe.matmul(ps[n % 2][0:r, 0:D], patches[:, n, k, 0:r], W[:, k, :], start=(k == 0),
                                  stop=(k == TOK_K - 1))
                m.then_inc(proj_done, 1)

            pe.wait_ge(W_in, 16)
            pe.wait_ge(made, MADE)
            for k in range(max(NW, NT)):
                if k < NW:
                    weight_tile(k)
                if k < NT:
                    patch_tile(k)

        @block.scalar
        def _(act):
            def copy_out(k):
                _, r, width = wtiles[k]
                act.wait_ge(w_filled, k + 1)
                o = ps[2 + k % 2][:, :].bitcast(BF16)
                if k < 2 * ITILES:
                    which, m = k // ITILES, k % ITILES
                    x = act.activation(f1["guT"][:, which, :, m * P:m * P + r],
                                       o[:, 0:KC * P].rearrange("p (c r) -> p c r", r=P)[:, :, 0:r], ACT.Copy)
                else:
                    half, full = k - 2 * ITILES, INNER // P
                    act.activation(f1["dT"][:, 0:full, half * P:(half + 1) * P],
                                   o[:, 0:full * P].rearrange("p (c r) -> p c r", r=P), ACT.Copy)
                    x = act.activation(f1["dT"][0:IROWS[-1], full, half * P:(half + 1) * P],
                                       o[0:IROWS[-1], full * P:(full + 1) * P], ACT.Copy)
                x.then_inc(w_copied, 1)

            for n in range(max(NW, len(chunks))):
                if n < NW:
                    copy_out(n)
                if n < len(chunks):
                    act.wait_ge(raw_in[n % RING], 16 * (n // RING + 1))
                    act.activation(chunks[n][1], raw[n % RING][:, 0:chunks[n][3]], ACT.Copy).then_inc(high_done, 1)

        @block.vector
        def _(dve):
            def weight_tile(k):
                src, r, width = wtiles[k]
                if k >= 1:
                    dve.wait_ge(wq_done, k)
                dve.tensor_scalar(rounded[0:r, 0:width], src, wrecip[0:r, k:k + 1], ROUND, ALU.mult,
                                  ALU.add).then_inc(wround_done, 1)
                dve.wait_ge(wround_done, k + 1)
                if k >= 2:
                    dve.wait_ge(w_filled, k - 1)
                dve.tensor_scalar(wq[k % 2][0:r, 0:width], rounded[0:r, 0:width], ROUND, None,
                                  ALU.subtract).then_inc(wq_done, 1)

            dve.memset(wrange[:], 1.0).then_inc(range_done, 1)
            dve.wait_ge(range_done, 1)
            dve.wait_ge(f1_in, 48)
            for k, (src, r, _) in enumerate(wtiles):
                dve.tensor_reduce(wrange[0:r, k:k + 1], src, AX.X, ALU.max, apply_absolute_value=True).then_inc(range_done, 1)
            dve.wait_ge(range_done, NW + 1)
            dve.tensor_scalar(f1["scale"][:], wrange[:], 1.0 / QMAX, None, ALU.mult).then_inc(scale_done, 1)
            dve.wait_ge(scale_done, 1)
            dve.reciprocal(wrecip[:], f1["scale"][:]).then_inc(recip_done, 1)
            dve.wait_ge(recip_done, 1)
            dve.wait_ge(pos_in, 32)
            dve.tensor_tensor(pos[:], pos[:], add[:], ALU.add).then_inc(pos_done, 1)
            dve.wait_ge(pos_done, 1)
            weight_tile(0)
            for n in range(max(NW, NT, len(chunks))):
                if n + 1 < NW:
                    weight_tile(n + 1)
                if n < len(chunks):
                    dve.wait_ge(high_done, n + 1)
                    dve.tensor_tensor(chunks[n][2], raw[n % RING][:, 0:chunks[n][3]], chunks[n][1],
                                      ALU.subtract).then_inc(low_done, 1)
                if n < NT:
                    r = tiles[n][1] * NIMG
                    dve.wait_ge(proj_done, n + 1)
                    dve.tensor_tensor(rows[0:r, n, :], ps[n % 2][0:r, 0:D], pos[0:r, :], ALU.add).then_inc(rows_done, 1)


def kernel(x, x_txt, L0_tok_W, L0_tok_b, L0_tok_pos_embedding, L0_tok_cls_token, L0_txt_embeddings, L0_attn_w_attn,
           L0_attn_b_attn, L0_attn_w_proj, L0_attn_b_proj, L0_ffn_hasher_w, L0_ffn_keys, L0_ffn_values_down,
           L0_ffn_values_up, L0_ffn_scale, L1_attn_w_q, L1_attn_w_k, L1_attn_w_v, L1_attn_w_o, L1_ffn_clip_x,
           L1_ffn_clip_down, L1_ffn_w_gate, L1_ffn_w_up, L1_ffn_w_down):
    import numpy as np
    import concourse.bacc as bacc
    from concourse.bass_utils import run_bass_kernel_spmd

    def chunked(m):
        m = np.asarray(m)
        return m.reshape(-1, P, m.shape[1]).transpose(1, 0, 2)

    def on_partitions(v):
        return np.tile(np.asarray(v).reshape(1, -1), (P, 1))

    G, PX, C = 6, 16, 3
    img = np.asarray(x).reshape(B, C, G, PX, G, PX).transpose(1, 3, 5, 0, 2, 4).reshape(C * PX * PX, B, NIMG - 1)
    patches = np.zeros((C * PX * PX, B, NIMG), img.dtype)
    patches[:, :, 1:] = img
    room = np.zeros((C * PX * PX, -(-B // TOK_G) * TOK_G, NIMG), img.dtype)
    room[:, 0:B] = patches
    patch_tiles = room.reshape(TOK_K, P, -1, TOK_G * NIMG).transpose(2, 1, 0, 3).reshape(-1, P, TOK_K * TOK_G * NIMG)
    tok_add = np.concatenate([np.asarray(L0_tok_cls_token)[0], np.tile(np.asarray(L0_tok_b)[None], (NIMG - 1, 1))])
    wa, ba = np.asarray(L0_attn_w_attn), np.asarray(L0_attn_b_attn)
    qk = np.zeros((2, HEADS, 32, D), wa.dtype)
    qk[:, :, 0:16] = wa[0:2 * D].reshape(2, HEADS, 16, D)
    qkb = np.zeros((2, HEADS, 32), ba.dtype)
    qkb[:, :, 0:16] = ba[0:2 * D].reshape(2, HEADS, 16)
    a1_qk = np.concatenate([np.asarray(L1_attn_w_q).reshape(-1, D), np.asarray(L1_attn_w_k).reshape(-1, D)])

    def rows_padded(m):
        m = np.asarray(m)
        padded = np.zeros((ITILES * P, D), m.dtype)
        padded[0:INNER] = m
        return chunked(padded)

    arrays = {
        "idx": np.asarray(x_txt).T,
        "emb": np.asarray(L0_txt_embeddings),
        "patches": patch_tiles,
        "tok_W": chunked(np.asarray(L0_tok_W).T),
        "tok_pos": np.tile(np.asarray(L0_tok_pos_embedding)[0], (TOK_G, 1)),
        "tok_add": np.tile(tok_add, (TOK_G, 1)),
        "a0_qk": chunked(qk.reshape(-1, D).T),
        "a0_qkb": qkb.reshape(-1, P).T,
        "a0_v": chunked(wa[2 * D:].T),
        "a0_vb": ba[2 * D:].reshape(1, D),
        "a0_o": chunked(np.asarray(L0_attn_w_proj).T),
        "a0_ob": np.asarray(L0_attn_b_proj).reshape(1, D),
        "f0_hash": chunked(np.asarray(L0_ffn_hasher_w).T),
        "f0_keys": np.asarray(L0_ffn_keys).T,
        "f0_down": chunked(np.asarray(L0_ffn_values_down).transpose(1, 0, 2).reshape(D, -1)),
        "f0_up": chunked(np.asarray(L0_ffn_values_up).reshape(-1, D)),
        "f0_scale": on_partitions(L0_ffn_scale),
        "a1_qk": chunked(a1_qk.T),
        "a1_v": chunked(np.asarray(L1_attn_w_v).reshape(-1, D).T),
        "a1_o": chunked(L1_attn_w_o),
        "f1_gate": rows_padded(L1_ffn_w_gate),
        "f1_up": rows_padded(L1_ffn_w_up),
        "f1_down": chunked(L1_ffn_w_down),
        "f1_clip": on_partitions(np.concatenate([np.asarray(L1_ffn_clip_x), np.asarray(L1_ffn_clip_down)])),
    }
    arrays = {n + "_dram": np.ascontiguousarray(a) for n, a in arrays.items()}
    nc = bacc.Bacc("TRN2", target_bir_lowering=False, num_devices=1)
    t = {n[:-5]: nc.dram_tensor(n, a.shape, mybir.dt.from_np(a.dtype), kind="ExternalInput").ap() for n, a in arrays.items()}
    out = nc.dram_tensor("out_dram", (B, S, D), F32, kind="ExternalOutput").ap()
    program(nc, t, out)
    r = run_bass_kernel_spmd(nc, [arrays], core_ids=[0])
    return r.results[0]["out_dram"]
```

```python
from contextlib import ExitStack

import concourse.bass as bass
from concourse import mybir

ALU = mybir.AluOpType
ACT = mybir.ActivationFunctionType
AX = mybir.AxisListType
F32 = mybir.dt.float32
BF16 = mybir.dt.bfloat16
F16 = mybir.dt.float16
I32 = mybir.dt.int32
U32 = mybir.dt.uint32

P = 128
B = 32
S = 114
NIMG = 37
NTXT = 77
D = 256
KC = D // P
PAIR = 2 * S
NPAIR = B // 2
HEADS = 16
MADE = 16
UNITS = 8
QCOLS = 4 * S
MASKED = -3.0e38
EPS = 1.0e-5
TOK_K = 768 // P
TOK_G = 3
EXPERTS = 64
EDIM = 32
ETILES = EXPERTS * EDIM // P
TOPK = 4
INNER = 704
ITILES = (INNER + P - 1) // P
IROWS = [min(P, INNER - P * m) for m in range(ITILES)]
QMAX = 127.0
ALL = slice(None)
ROUND = 12582912.0
E_CONST = 2.718281828459045


class Pair:

    def __init__(self, p0, i=None):
        self.p0, self.i = p0, i
        self.first = i is None and p0 == 0
        self.last = i is None and p0 == NPAIR - 1

    def val(self, a, c):
        n = a * self.p0 + c
        return n if self.i is None else self.i * (2 * a) + n

    def shift(self, n):
        return Pair(self.p0 + n, self.i)


def run_slots(eng, slot):
    slot(Pair(0))
    with eng.Fori(0, (NPAIR - 2) // 2) as i:
        slot(Pair(1, i))
        slot(Pair(2, i))
    slot(Pair(NPAIR - 1))


def rows_of(H, p, s):
    b = p.val(2, s)
    if isinstance(b, int):
        return H[0:S, b, :]
    return H[0:S, bass.ds(b, 1), :].rearrange("p a d -> p (a d)")


def pair_of(x, p):
    b = p.val(2, 0)
    return x[0:S, b:b + 2, :] if isinstance(b, int) else x[0:S, bass.ds(b, 2), :]


def cell(x, p):
    n = p.val(1, 0)
    return x[:, n:n + 1] if isinstance(n, int) else x[:, bass.ds(n, 1)]


PIECE = 512
F0_PIECES = {"down": (0, 8), "up": (8, 16)}
A1_PIECES = {"qk": (0, 8), "v": (8, 12), "o": (12, 16)}
TOP_EXP = 4
EXP_BITS = 0x7F800000
ONE_EXP = 1 << 23


def as_chunks(pair, pieces, width):
    a, b = pieces
    if width > PIECE:
        return [x[:, a:b, :].rearrange("p (k c) n -> p k (c n)", k=KC) for x in pair]
    return [x[:, a:b, :].rearrange("p a (b n) -> p (a b) n", n=width) for x in pair]


class Stream:

    def __init__(self, name, src, sb, sem):
        self.src = src
        self.raw = [sb(name + f"piece{k}", [P, PIECE], F32) for k in range(2)]
        self.raw_in = [sem(name + f"piece_in{k}") for k in range(2)]
        self.high_done, self.used = sem(name + "piece_high"), sem(name + "piece_used")

    @staticmethod
    def piece(x, q):
        n = q.val(1, 0)
        return x[:, n, :] if isinstance(n, int) else x[:, bass.ds(n, 1), :].rearrange("p a n -> p (a n)")

    def load(self, sp, q):
        if not (q.first or q.p0 == 1 and q.i is None):
            sp.wait_ge(self.used, q.val(1, -1))
        sp.dma_start(self.raw[q.p0 % 2][:], self.piece(self.src, q)).then_inc(self.raw_in[q.p0 % 2], 16)

    def wait_in(self, eng, q):
        n = 16 * (q.p0 // 2 + 1)
        eng.wait_ge(self.raw_in[q.p0 % 2], n if q.i is None else q.i * 16 + n)

    def high(self, act, q, pair, scale=None):
        self.wait_in(act, q)
        dst, raw = self.piece(pair[0], q), self.raw[q.p0 % 2][:]
        if scale is None:
            act.activation(dst, raw, ACT.Copy).then_inc(self.high_done, 1)
        else:
            act.activation(dst, raw, ACT.Identity, scale=scale).then_inc(self.high_done, 1)

    def low(self, dve, q, pair, scale=None):
        dve.wait_ge(self.high_done, q.val(1, 1))
        high, low, raw = self.piece(pair[0], q), self.piece(pair[1], q), self.raw[q.p0 % 2][:]
        if scale is None:
            dve.tensor_tensor(low, raw, high, ALU.subtract).then_inc(self.used, 1)
        else:
            dve.scalar_tensor_tensor(low, raw, scale, high, ALU.mult, ALU.subtract).then_inc(self.used, 1)

    def absmax(self, dve, q, dst):
        self.wait_in(dve, q)
        dve.tensor_reduce(cell(dst, q), self.raw[q.p0 % 2][:], AX.X, ALU.max,
                          apply_absolute_value=True).then_inc(self.used, 1)


def scale_weights(nc, w, sb, sem):
    own_max = sb("wmax", [P, 3], F32)
    all_max = sb("wmax_all", [P, 3], F32)
    least = sb("wmax_least", [P, 3], F32)
    exps = sb("wexp", [P, 3], I32)
    scales = sb("wscales", [P, 3], F32)
    undo = sb("wundo", [P, 3], F32)
    step, reduced = sem("wscale_step"), sem("wscale_reduced")
    kinds = list(A1_PIECES.values())
    with nc.Block() as block:
        @block.vector
        def _(dve):
            n = 0
            for k, (a, b) in enumerate(kinds):
                dve.tensor_reduce(own_max[:, k:k + 1], w["range"][:, a:b], AX.X, ALU.max).then_inc(step, 1)
                n += 1
            dve.memset(least[:, 0:1], 1.0e-15).then_inc(step, 1)
            dve.memset(least[:, 1:3], 1.0e-30).then_inc(step, 1)
            n += 2
            dve.wait_ge(reduced, 1)
            dve.wait_ge(step, n)
            dve.tensor_tensor(all_max[:], all_max[:], least[:], ALU.max).then_inc(step, 1)
            dve.wait_ge(step, n + 1)
            dve.tensor_scalar(exps[:], all_max[:].bitcast(I32), EXP_BITS, None, ALU.bitwise_and).then_inc(step, 1)
            dve.wait_ge(step, n + 2)
            dve.tensor_scalar(scales[:].bitcast(I32), exps[:], -1.0, float((254 + TOP_EXP) * ONE_EXP), ALU.mult,
                              ALU.add).then_inc(step, 1)
            dve.tensor_scalar(undo[:].bitcast(I32), exps[:], float(-TOP_EXP * ONE_EXP), None, ALU.add).then_inc(step, 1)
            dve.wait_ge(step, n + 4)
            for k, (a, b) in enumerate(kinds):
                dve.tensor_copy(w["scales"][:, a:b], scales[:, k:k + 1].to_broadcast([P, b - a])).then_inc(step, 1)
            dve.tensor_scalar(w["exp_scale"][:], undo[:, 0:1], undo[:, 0:1], 64 ** -0.5, ALU.mult, ALU.mult).then_inc(step, 1)
            dve.tensor_tensor(w["out_scale"][:], undo[:, 1:2], undo[:, 2:3], ALU.mult).then_inc(step, 1)

        @block.gpsimd
        def _(pool):
            pool.wait_ge(step, 3)
            pool.partition_all_reduce(all_max[:], own_max[:], P, bass.bass_isa.ReduceOp.max).then_inc(reduced, 1)


class Banks:

    def __init__(self, front, first, middle, last, after=()):
        self.front, self.first, self.middle, self.last, self.after = front, first, middle, last, list(after)

    def uses(self, p):
        if p is None:
            return self.front
        if p.i is None and p.p0 == NPAIR:
            return self.after
        return self.first if p.first else self.last if p.last else self.middle

    def count(self, p, use, kinds=None):
        def of(uses):
            return sum(kinds is None or u[0] in kinds for _, u in uses)

        names = [u for _, u in self.uses(p)]
        k = of(self.uses(p)[:names.index(use)])
        if p is None:
            return 0, k
        if p.first:
            return 0, of(self.front) + k
        a = of(self.middle)
        if p.i is None and p.p0 == NPAIR:
            return 0, of(self.front) + of(self.first) + a * (NPAIR - 2) + of(self.last) + k
        return a, of(self.front) + of(self.first) - a + k

    def at(self, p, use):
        a, c = self.count(p, use)
        whole = c if a == 0 else a * p.p0 + c
        return whole % 2, whole // 2 if a == 0 or p.i is None else p.i * a + whole // 2

    def nth(self, p, use, kinds):
        a, c = self.count(p, use, kinds)
        return c + 1 if a == 0 else p.val(a, c + 1)

    def step(self, p, t):
        return [u for at, u in self.uses(p) if at == t]


def matmul3(pe, out, a, b, start, stop):
    (ah, al), (bh, bl) = a, b
    pe.matmul(out, ah, bh, start=start, stop=False, skip_group_check=True)
    pe.matmul(out, ah, bl, start=False, stop=False, skip_group_check=True)
    return pe.matmul(out, al, bh, start=False, stop=stop, skip_group_check=True)


def both(pair, *index):
    return tuple(x[index] for x in pair)


def consts_on_chip(nc, sb, sem):
    c = {
        "ident": sb("ident", [P, P], F32), "identb": sb("identb", [P, P], BF16),
        "mask": sb("mask", [P, 4, S], BF16), "neghalf": sb("neghalf", [P, 2], F32),
        "eps": sb("eps", [P, 2], F32), "round": sb("round", [P, 2], F32), "minus1": sb("minus1", [P, 2], F32),
        "ones": sb("ones", [P, P], F32), "e": sb("e_const", [P, 8], F32),
        "iota": sb("iota", [P, EXPERTS], F32), "sel": sb("sel", [P, ETILES, P], BF16),
    }
    return c


def build_consts(pool, c, made):
    n = 0
    for name, value in (("ident", 0.0), ("identb", 0.0), ("mask", 0.0), ("neghalf", -0.5), ("minus1", -1.0),
                        ("round", ROUND), ("eps", EPS), ("ones", 1.0), ("e", E_CONST), ("sel", 0.0)):
        pool.memset(c[name][:], value).then_inc(made, 1)
        n += 1
    pool.iota(c["iota"][:], pattern=[[1, EXPERTS]], base=0, channel_multiplier=0,
              allow_small_or_imprecise_dtypes=True).then_inc(made, 1)
    n += 1
    pool.wait_ge(made, n)
    for name in ("ident", "identb"):
        pool.affine_select(out=c[name][:], in_=c[name][:], compare_op=ALU.not_equal, fill=1.0, base=0,
                           pattern=[[-1, P]], channel_multiplier=1).then_inc(made, 1)
        n += 1
    pool.affine_select(out=c["mask"][:], in_=c["mask"][:], compare_op=ALU.is_ge, fill=MASKED, base=0,
                       pattern=[[0, 4], [-1, S]], channel_multiplier=1).then_inc(made, 1)
    n += 1
    v = c["sel"][:].rearrange("p j (q r) -> p j q r", r=EDIM)
    for base in (0, -EXPERTS):
        pool.affine_select(out=v, in_=v, compare_op=ALU.not_equal, fill=1.0, base=base,
                           pattern=[[-(P // EDIM), ETILES], [-1, P // EDIM], [0, EDIM]],
                           channel_multiplier=1).then_inc(made, 1)
        n += 1
        pool.wait_ge(made, n)
    return n


def after_constants(eng, c):
    eng.wait_ge(c["made"], 1)


class Norm:

    def __init__(self, name, c, H, sb, sem):
        self.c, self.H = c, H
        self.stats = sb(name + "stats", [P, 2, 6], F32)
        self.mv = sb(name + "mv", [P, 2, 2], F32)
        self.vareps = sb(name + "vareps", [P, 2], F32)
        self.rstd = sb(name + "rstd", [P, 2], F32)
        self.stats_done, self.mv_done = sem(name + "stats_done"), sem(name + "mv_done")
        self.vareps_done, self.rstd_done = sem(name + "vareps_done"), sem(name + "rstd_done")

    def moments(self, dve, q):
        for s in range(2):
            dve.bn_stats(self.stats[0:S, s, :], rows_of(self.H, q, s)).then_inc(self.stats_done, 1)

    def wait_moments(self, dve, q):
        dve.wait_ge(self.stats_done, q.val(2, 2))

    def aggregate(self, dve, q):
        for s in range(2):
            dve.bn_aggr(self.mv[0:S, s, :], self.stats[0:S, s, :]).then_inc(self.mv_done, 1)

    def root(self, pool, q):
        pool.wait_ge(self.mv_done, q.val(2, 2))
        pool.tensor_tensor(self.vareps[0:S, :], self.mv[0:S, :, 1], self.c["eps"][0:S, :], ALU.add).then_inc(self.vareps_done, 1)
        pool.wait_ge(self.vareps_done, q.val(1, 1))
        pool.tensor_tensor(self.rstd[0:S, :], self.vareps[0:S, :], self.c["neghalf"][0:S, :],
                           ALU.pow).then_inc(self.rstd_done, 1)

    def rows(self, dve, q, dst, ready):
        dve.wait_ge(self.rstd_done, q.val(1, 1))
        for s in range(2):
            dve.tensor_scalar(dst(s), rows_of(self.H, q, s), self.mv[0:S, s, 0:1], self.rstd[0:S, s:s + 1],
                              ALU.subtract, ALU.mult).then_inc(ready, 1)


def attention(nc, name, H, c, w, HD, sb, psum, sem, final=None, late=None):
    ident, identb, mask = c["ident"], c["identb"], c["mask"]
    ROW = 32 if HD == 16 else 64
    HPT = P // ROW
    QT = HEADS // HPT
    VN = HEADS * HD
    KO = VN // P
    VW = HD + 1
    bias = HD == 16
    SCALE = float(HD) ** -0.5

    norm = Norm(name, c, H, sb, sem)
    xn = sb(name + "xn", [P, 2, D], F32)
    HALF = BF16 if HD == 16 else F16
    xT = [sb(name + f"xT_{h}", [P, KC, 2, S], HALF) for h in ("high", "low")]
    qkT = [[sb(name + f"qkT{k}_{h}", [P, 2 * QT, 2, S], HALF) for h in ("high", "low")] for k in range(2)]
    v = [[sb(name + f"v{k}{s}", [P, HEADS, VW], F32) for s in range(2)] for k in range(2)]
    E = [sb(name + f"E{k}", [P, 4, S], F32) for k in range(4)]
    rmax = [sb(name + f"rmax{k}", [P, 4], F32) for k in range(2)]
    pT = [sb(name + f"pT{k}", [P, 4, S], F32) for k in range(2)]
    rsum = [sb(name + f"rsum{k}", [P, 4], F32) for k in range(2)]
    on = [sb(name + f"on{s}", [P, VN], F32) for s in range(2)]
    oT = [[sb(name + f"oT{s}_{h}", [P, KO, S], HALF) for h in ("high", "low")] for s in range(2)]

    psS = [psum(name + f"psS{k}", [P, 512], F32) for k in range(2)]
    psT = [psum(name + f"psT{k}", [P, 512], F32) for k in range(2)]
    psO = [psum(name + f"psO{k}", [P, 512], F32) for k in range(2)]
    psM = [psum(name + f"psM{k}", [P, 512], F32) for k in range(2)]

    xn_done, ones_done = sem(name + "xn_done"), sem(name + "ones_done")
    scores_done, max_done, sub_done, exp_done = (sem(name + n) for n in ("scores_done", "max_done", "sub_done", "exp_done"))
    turned, pT_done, pv_done, rsum_done, on_done = (sem(name + n) for n in ("turned", "pT_done", "pv_done", "rsum_done", "on_done"))
    filled = [sem(name + f"filled{k}") for k in range(2)]
    copied = [sem(name + f"copied{k}") for k in range(2)]
    high_done = sem(name + "high_done")
    SPLIT = ("xT", "qk", "oT")

    VH = [(s, h) for s in range(2) for h in range(max(1, VN // 512))] if VN > D else [(None, 0)]
    OC = [(a, min(a + 4, KO)) for a in range(0, KO, 4)]
    QK_STEPS = (2.5, 3, 4, 6)
    V_STEPS = (0, 0, 1, 1)
    front = [(1.5, ("xT",))] + [(QK_STEPS[4 * j // QT], ("qk", j)) for j in range(QT)]
    values = [(V_STEPS[n], ("v", s, h)) for n, (s, h) in enumerate(VH)]
    turn0 = [(7, ("oT", 0, a)) for a in range(len(OC))]
    tail = [(1, ("proj", 0))] + [(3, ("oT", 1, a)) for a in range(len(OC))] + [(5, ("proj", 1))]

    def merged(*parts):
        return sorted((x for part in parts for x in part), key=lambda x: x[0])

    banks = Banks(front, merged(values, front, turn0), merged(values, tail, front, turn0), merged(values, tail, turn0), tail)
    END = Pair(NPAIR)
    bank_of = banks.at

    def before(p):
        return None if p.first else p.shift(-1)

    def wait_copied(eng, p, use):
        k, n = bank_of(p, use)
        eng.wait_ge(copied[k], n + 1)

    def head_place(i, r):
        if HPT == 4:
            return i, ROW * r
        return 4 * (r // 2) + i, ROW * (r % 2)

    def whose(p, use):
        if use[0] in ("xT", "qk"):
            return p.shift(1)
        return p if use[0] == "v" or use[:2] == ("oT", 0) else p.shift(-1)

    if late:
        split = Stream(name + "next_", late["split_src"], sb, sem)
        look = Stream(name + "after_", late["look_src"], sb, sem)

    block = nc.Block()
    with block:
        @block.sync
        def _(sp):
            if late:
                split.load(sp, Pair(0))
                look.load(sp, Pair(0))

                def slot(p):
                    if not p.last:
                        split.load(sp, p.shift(1))
                        look.load(sp, p.shift(1))

                run_slots(sp, slot)

        @block.tensor
        def _(pe):
            def bank_free(p, use):
                k, n = bank_of(p, use)
                if not isinstance(n, int) or n > 0:
                    pe.wait_ge(copied[k], n)
                return psM[k], filled[k]

            def scores(p, u):
                k, s, r = u % 2, u // 4, u % 4
                if u == 0:
                    for j in (QT - 2, QT - 1):
                        wait_copied(pe, before(p), ("qk", j))
                if not (p.first and u < 2):
                    pe.wait_ge(sub_done, p.val(8, u - 1))
                pe.matmul(psS[k][0:S, 0:QCOLS], identb[0:S, 0:S], mask[0:S].rearrange("p a k -> p (a k)"),
                          start=True, stop=False, skip_group_check=True)
                qk = qkT[p.p0 % 2]
                for i in range(4):
                    tile, row = head_place(i, r)
                    ps = slice(row, row + HD)
                    m = matmul3(pe, psS[k][0:S, i * S:(i + 1) * S], both(qk, ps, tile, s), both(qk, ps, QT + tile, s),
                                start=False, stop=(i == 3))
                m.then_inc(scores_done, 1)

            def turn(p, u):
                k = u % 2
                pe.wait_ge(exp_done, p.val(8, u + 1))
                for i in range(4):
                    m = pe.transpose(psT[k][0:S, i * S:(i + 1) * S], E[u % 4][0:S, i, :], ident[0:S, 0:S])
                m.then_inc(turned, 1)

            def weigh(p, u):
                k, s, r = u % 2, u // 4, u % 4
                if u == 0:
                    for x in VH[-2:]:
                        wait_copied(pe, p, ("v", *x))
                pe.wait_ge(pT_done, p.val(8, u + 1))
                if not (p.first and u < 2):
                    pe.wait_ge(on_done, p.val(8, u - 1))
                for i in range(4):
                    tile, row = head_place(i, r)
                    m = pe.matmul(psO[k][0:S, i * VW:(i + 1) * VW], pT[k][0:S, i, :],
                                  v[p.p0 % 2][s][0:S, HPT * tile + row // ROW, :], start=True, stop=True)
                m.then_inc(pv_done, 1)

            def shared(p, use, q):
                kind = use[0]
                bank, done = bank_free(p, use)
                if kind == "xT":
                    pe.wait_ge(xn_done, q.val(2, 2))
                    for kc in range(KC):
                        for s in range(2):
                            m = pe.transpose(bank[:, (2 * kc + s) * S:(2 * kc + s + 1) * S],
                                             xn[0:S, s, kc * P:(kc + 1) * P], ident[0:S, 0:S])
                elif kind == "qk":
                    if use[1] == 0:
                        wait_copied(pe, p, ("xT",))
                    for half in range(2):
                        tile = 2 * use[1] + half
                        for kc in range(KC):
                            m = matmul3(pe, bank[:, half * PAIR:(half + 1) * PAIR],
                                        both(w["qk"], ALL, kc, slice(tile * P, (tile + 1) * P)),
                                        [x[:, kc].rearrange("p s k -> p (s k)") for x in xT],
                                        start=(kc == 0), stop=(kc == KC - 1))
                elif kind == "v":
                    parts = [(0, 0, D), (1, 0, D)] if use[1] is None else [(use[1], 512 * use[2], 512)]
                    for n, (s, a, width) in enumerate(parts):
                        out = bank[0:S, n * width:(n + 1) * width]
                        for kc in range(KC):
                            m = matmul3(pe, out, both(xT, ALL, kc, s), both(w["v"], ALL, kc, slice(a, a + width)),
                                        start=(kc == 0), stop=(kc == KC - 1 and not bias))
                        if bias:
                            m = pe.matmul(out, w["ones"][:, 0:S], w["biases"][:, 0:D], start=False, stop=True, skip_group_check=True)
                elif kind == "oT":
                    if use[2] == 0:
                        pe.wait_ge(on_done, q.val(8, 4 * use[1] + 4))
                    a, b = OC[use[2]]
                    for n in range(a, b):
                        m = pe.transpose(bank[:, (n - a) * S:(n - a + 1) * S], on[use[1]][0:S, n * P:(n + 1) * P],
                                         ident[0:S, 0:S])
                else:
                    for a in range(len(OC)):
                        wait_copied(pe, p if use[1] else p.shift(-1), ("oT", use[1], a))
                    for n in range(KO):
                        m = matmul3(pe, bank[0:S, 0:D], both(oT[use[1]], ALL, n), both(w["o"], ALL, n), start=(n == 0),
                                    stop=(n == KO - 1 and not bias))
                    if bias:
                        m = pe.matmul(bank[0:S, 0:D], w["ones"][:, 0:S], w["biases"][:, D:2 * D], start=False, stop=True,
                                      skip_group_check=True)
                m.then_inc(done, 1)

            def uses(p, t):
                for use in banks.step(p, t):
                    shared(p, use, whose(p, use))

            pe.wait_ge(ones_done, 4)
            for _, use in banks.front:
                shared(None, use, Pair(0))

            def slot(p):
                for t in range(UNITS):
                    scores(p, t)
                    uses(p, t)
                    if t >= 2:
                        turn(p, t - 2)
                    elif not p.first:
                        turn(p.shift(-1), t + 6)
                    if t >= 3:
                        weigh(p, t - 3)
                    elif not p.first:
                        weigh(p.shift(-1), t + 5)
                    uses(p, t + 0.5)

            run_slots(pe, slot)
            last = Pair(NPAIR - 1)
            for t in range(3):
                if t < 2:
                    turn(last, t + 6)
                weigh(last, t + 5)
            for _, use in banks.after:
                shared(END, use, last)

        @block.scalar
        def _(act):
            def copy_out(p, use, q):
                if use[0] == "proj":
                    return
                k, n = bank_of(p, use)
                act.wait_ge(filled[k], n + 1)
                bank = psM[k]
                if use[0] == "xT":
                    m = act.activation(xT[0][:].rearrange("p c s k -> p (c s k)"), bank[:, 0:2 * PAIR], ACT.Copy)
                elif use[0] == "qk":
                    dst = qkT[q.p0 % 2][0]
                    if bias:
                        for half in range(2):
                            tile = 2 * use[1] + half
                            m = act.activation(dst[:, tile].rearrange("p s k -> p (s k)"),
                                               bank[:, half * PAIR:(half + 1) * PAIR], ACT.Identity,
                                               bias=w["qkb"][:, tile:tile + 1])
                    else:
                        m = act.activation(dst[:, 2 * use[1]:2 * use[1] + 2].rearrange("p t s k -> p (t s k)"),
                                           bank[:, 0:2 * PAIR], ACT.Copy)
                elif use[0] == "v":
                    if use[1] is None:
                        for s in range(2):
                            m = act.activation(v[q.p0 % 2][s][0:S, :, 0:HD],
                                               bank[0:S, s * D:(s + 1) * D].rearrange("p (h d) -> p h d", d=HD), ACT.Copy)
                    else:
                        hp = 512 // HD
                        m = act.activation(v[q.p0 % 2][use[1]][0:S, use[2] * hp:(use[2] + 1) * hp, 0:HD],
                                           bank[0:S, :].rearrange("p (h d) -> p h d", d=HD), ACT.Copy)
                else:
                    a, b = OC[use[2]]
                    m = act.activation(oT[use[1]][0][:, a:b, :].rearrange("p c k -> p (c k)"), bank[:, 0:(b - a) * S],
                                       ACT.Copy)
                m.then_inc(high_done if use[0] in SPLIT else copied[k], 1)

            def pT_copy(p, u):
                act.wait_ge(turned, p.val(8, u + 1))
                act.activation(pT[u % 2][0:S].rearrange("p a k -> p (a k)"), psT[u % 2][0:S, 0:QCOLS],
                               ACT.Copy).then_inc(pT_done, 1)

            def exps(p, u):
                act.wait_ge(sub_done, p.val(8, u + 1))
                e = E[u % 4][0:S].rearrange("p a k -> p (a k)")
                act.activation(e, e, ACT.Exp, scale=w["exp_scale"][0:S, 0:1] if "exp_scale" in w else SCALE).then_inc(exp_done, 1)

            for _, use in banks.front:
                copy_out(None, use, Pair(0))

            def slot(p):
                for t in range(UNITS):
                    uses = banks.step(p, t)
                    for use in uses[:1]:
                        copy_out(p, use, whose(p, use))
                    exps(p, t)
                    for use in uses[1:]:
                        copy_out(p, use, whose(p, use))
                    if t >= 2:
                        pT_copy(p, t - 2)
                    elif not p.first:
                        pT_copy(p.shift(-1), t + 6)
                    for use in banks.step(p, t + 0.5):
                        copy_out(p, use, whose(p, use))
                    if late and t == 4:
                        split.high(act, p, late["split"])

            run_slots(act, slot)
            last = Pair(NPAIR - 1)
            for t in range(2):
                pT_copy(last, t + 6)
            for _, use in banks.after:
                copy_out(END, use, last)

        @block.gpsimd
        def _(pool):
            norm.root(pool, Pair(0))

            def slot(p):
                if not p.last:
                    norm.root(pool, p.shift(1))
                if final and not p.first:
                    final["norm"].root(pool, p.shift(-1))

            run_slots(pool, slot)
            if final:
                final["norm"].root(pool, Pair(NPAIR - 1))

        @block.vector
        def _(dve):
            def rows(p, q):
                if p is not None:
                    k, n = bank_of(before(p), ("xT",))
                    dve.wait_ge(filled[k], n + 1)
                norm.rows(dve, q, lambda s: xn[0:S, s, :], xn_done)

            def scores(p, u):
                k = u % 2
                bank = psS[k][0:S, 0:QCOLS].rearrange("p (h k) -> p h k", h=4)
                dve.wait_ge(scores_done, p.val(8, u + 1))
                dve.tensor_reduce(rmax[k][0:S, :], bank, AX.X, ALU.max).then_inc(max_done, 1)
                dve.wait_ge(max_done, p.val(8, u + 1))
                dve.tensor_tensor(E[u % 4][0:S], bank, rmax[k][0:S, :].unsqueeze(2).to_broadcast([S, 4, S]),
                                  ALU.subtract).then_inc(sub_done, 1)

            def normalise(p, u):
                k, s, r = u % 2, u // 4, u % 4
                dve.wait_ge(pv_done, p.val(8, u + 1))
                o = psO[k][0:S, 0:4 * VW].rearrange("p (h d) -> p h d", d=VW)
                dve.reciprocal(rsum[k][0:S, :].unsqueeze(2), o[:, :, HD:VW]).then_inc(rsum_done, 1)
                tile, row = head_place(0, r)
                h0 = HPT * tile + row // ROW
                dst = on[s][0:S, :].rearrange("p (h d) -> p h d", d=HD)[:, h0:h0 + 3 * HPT + 1:HPT, :]
                dve.wait_ge(rsum_done, p.val(8, u + 1))
                dve.tensor_tensor(dst, o[:, :, 0:HD], rsum[k][0:S, :].unsqueeze(2).to_broadcast([S, 4, HD]),
                                  ALU.mult).then_inc(on_done, 1)

            def low_half(p, use, q):
                k, n = bank_of(p, use)
                bank = psM[k]
                dve.wait_ge(high_done, banks.nth(p, use, SPLIT))
                if use[0] == "xT":
                    high, low = (x[:].rearrange("p c s k -> p (c s k)") for x in xT)
                    m = dve.tensor_tensor(low, bank[:, 0:2 * PAIR], high, ALU.subtract)
                elif use[0] == "qk" and bias:
                    for half in range(2):
                        tile = 2 * use[1] + half
                        high, low = (x[:, tile].rearrange("p s k -> p (s k)") for x in qkT[q.p0 % 2])
                        m = dve.scalar_tensor_tensor(low, bank[:, half * PAIR:(half + 1) * PAIR], w["qkb"][:, tile:tile + 1],
                                                     high, ALU.add, ALU.subtract)
                elif use[0] == "qk":
                    high, low = (x[:, 2 * use[1]:2 * use[1] + 2].rearrange("p t s k -> p (t s k)") for x in qkT[q.p0 % 2])
                    m = dve.tensor_tensor(low, bank[:, 0:2 * PAIR], high, ALU.subtract)
                else:
                    a, b = OC[use[2]]
                    high, low = (x[:, a:b, :].rearrange("p c k -> p (c k)") for x in oT[use[1]])
                    m = dve.tensor_tensor(low, bank[:, 0:(b - a) * S], high, ALU.subtract)
                m.then_inc(copied[k], 1)

            def residual(p, use, q):
                k, n = bank_of(p, use)
                dve.wait_ge(filled[k], n + 1)
                h = rows_of(H, q, use[1])
                if "out_scale" in w:
                    dve.scalar_tensor_tensor(h, psM[k][0:S, 0:D], w["out_scale"][0:S, 0:1], h, ALU.mult,
                                             ALU.add).then_inc(copied[k], 1)
                else:
                    dve.tensor_tensor(h, psM[k][0:S, 0:D], h, ALU.add).then_inc(copied[k], 1)

            def shared(p, use, q):
                if use[0] in SPLIT:
                    low_half(p, use, q)
                elif use[0] == "proj":
                    residual(p, use, q)

            def uses(p, t):
                for use in banks.step(p, t):
                    shared(p, use, whose(p, use))

            def final_rows(q):
                final["norm"].rows(dve, q, lambda s: rows_of(final["x"], q, s), final["x_done"])
                dve.wait_ge(final["x_done"], q.val(2, 2))
                dve.tensor_reduce(cell(final["absmax"][0:S], q), pair_of(final["x"], q), AX.XY, ALU.max,
                                  apply_absolute_value=True).then_inc(final["absmax_done"], 1)

            for k in range(2):
                for s in range(2):
                    dve.memset(v[k][s][0:S, :, HD:VW], 1.0).then_inc(ones_done, 1)
            norm.moments(dve, Pair(0))
            norm.wait_moments(dve, Pair(0))
            norm.aggregate(dve, Pair(0))
            rows(None, Pair(0))
            for _, use in banks.front:
                shared(None, use, Pair(0))

            def slot(p):
                for t in range(UNITS):
                    if t == 1 and not p.last:
                        rows(p, p.shift(1))
                    if t == 0 and not p.last:
                        norm.moments(dve, p.shift(1))
                        norm.wait_moments(dve, p.shift(1))
                    if final and t == 6 and not p.first:
                        final["norm"].wait_moments(dve, p.shift(-1))
                    scores(p, t)
                    if final and t == 6 and not p.first:
                        final["norm"].aggregate(dve, p.shift(-1))
                    if t == 0 and not p.last:
                        norm.aggregate(dve, p.shift(1))
                    uses(p, t)
                    if final and t == 5 and not p.first:
                        wait_copied(dve, p, ("proj", 1))
                    if t >= 3:
                        normalise(p, t - 3)
                    elif not p.first:
                        normalise(p.shift(-1), t + 5)
                    uses(p, t + 0.5)
                    if late and t == 5:
                        split.low(dve, p, late["split"])
                    if late and t == 6:
                        look.absmax(dve, p, late["range"])
                    if final and t == 5 and not p.first:
                        final["norm"].moments(dve, p.shift(-1))
                if final and not p.first:
                    final_rows(p.shift(-1))

            run_slots(dve, slot)
            last = Pair(NPAIR - 1)
            for t in range(3):
                normalise(last, t + 5)
            for _, use in banks.after:
                shared(END, use, last)
            if final:
                wait_copied(dve, END, ("proj", 1))
                final["norm"].moments(dve, last)
                final["norm"].wait_moments(dve, last)
                final["norm"].aggregate(dve, last)
                final_rows(last)


def experts(nc, name, H, c, w, sb, psum, sem, late):
    ident, identb, sel = c["ident"], c["identb"], c["sel"]
    norm = Norm(name, c, H, sb, sem)
    xn = [sb(name + f"xn{k}", [P, 2, D], F32) for k in range(2)]
    xT = [[sb(name + f"xT{k}_{h}", [P, KC, 2, S], BF16) for h in ("high", "low")] for k in range(2)]
    hT = sb(name + "hT", [EDIM, 2, S], F32)
    sim = sb(name + "sim", [P, 2, EXPERTS], F32)
    top = sb(name + "top", [P, 2, 8], F32)
    at = sb(name + "at", [P, 2, 8], U32)
    atf = sb(name + "atf", [P, 2, 8], F32)
    diff = sb(name + "diff", [P, 2, TOPK], F32)
    ew = sb(name + "ew", [P, 2, TOPK], F32)
    esum = sb(name + "esum", [P, 2, 1], F32)
    erecip = sb(name + "erecip", [P, 2, 1], F32)
    gate = sb(name + "gate", [P, 2, TOPK], F32)
    hit = sb(name + "hit", [P, 2, EXPERTS, TOPK], F32)
    wrow = sb(name + "wrow", [P, 2, EXPERTS], F32)
    wparts = sb(name + "wparts", [P, 2, 2, EXPERTS], BF16)
    wT = [sb(name + f"wT{k}", [P, 2, S], BF16) for k in range(2)]
    act_s = [sb(name + f"silu{k}", [P, 2, S], F32) for k in range(2)]
    hid = [sb(name + f"hid{k}", [P, 2, S], F32) for k in range(2)]
    hid2 = [[sb(name + f"hid{k}_{h}", [P, 2, S], BF16) for h in ("high", "low")] for k in range(4)]

    psD = [psum(name + f"psD{k}", [P, 512], F32) for k in range(2)]
    psW = [psum(name + f"psW{k}", [P, 512], F32) for k in range(2)]
    psU = [psum(name + f"psU{k}", [P, 512], F32) for k in range(2)]
    psM = [psum(name + f"psM{k}", [P, 512], F32) for k in range(2)]

    xn_done, added, down_done, spread_done, silu_done, up_done, h_done = (sem(name + n) for n in (
        "xn_done", "added", "down_done", "spread_done", "silu_done", "up_done", "h_done"))
    hid_done, hid_high, hid_low, high_done = (sem(name + n) for n in ("hid_done", "hid_high", "hid_low", "high_done"))
    top_done, at_done, pool_step, gate_done, gates_read, w_step, wparts_done = (sem(name + n) for n in (
        "top_done", "at_done", "pool_step", "gate_done", "gates_read", "w_step", "wparts_done"))
    filled = [sem(name + f"filled{k}") for k in range(2)]
    copied = [sem(name + f"copied{k}") for k in range(2)]

    front = [(3, ("xT",)), (5, ("hash",)), (7, ("sim",)), (15, ("wT",))]
    banks = Banks(front, front, front, [])
    NT = ETILES
    LAG = 3
    split = Stream(name + "next_", late["src"], sb, sem)
    scale_now = sb(name + "scale_now", [P, 1], F32)
    scale_set = sem(name + "scale_set")

    def before(p):
        return None if p.first else p.shift(-1)

    def wait_copied(eng, p, use):
        k, n = banks.at(p, use)
        eng.wait_ge(copied[k], n + 1)

    block = nc.Block()
    with block:
        @block.sync
        def _(sp):
            split.load(sp, Pair(0))

            def slot(p):
                if not p.last:
                    split.load(sp, p.shift(1))

            run_slots(sp, slot)

        @block.tensor
        def _(pe):
            def shared(p, use, q):
                k, n = banks.at(p, use)
                bank = psM[k]
                if not isinstance(n, int) or n > 0:
                    pe.wait_ge(copied[k], n)
                if use[0] == "xT":
                    pe.wait_ge(xn_done, q.val(2, 2))
                    for kc in range(KC):
                        for s in range(2):
                            m = pe.transpose(bank[:, (2 * kc + s) * S:(2 * kc + s + 1) * S],
                                             xn[q.p0 % 2][0:S, s, kc * P:(kc + 1) * P], ident[0:S, 0:S])
                elif use[0] == "hash":
                    wait_copied(pe, p, ("xT",))
                    for kc in range(KC):
                        m = matmul3(pe, bank[0:EDIM, 0:PAIR], both(w["hash"], ALL, kc),
                                    [x[:, kc].rearrange("p s k -> p (s k)") for x in xT[q.p0 % 2]],
                                    start=(kc == 0), stop=(kc == KC - 1))
                elif use[0] == "sim":
                    wait_copied(pe, p, ("hash",))
                    for s in range(2):
                        m = pe.matmul(bank[0:S, s * EXPERTS:(s + 1) * EXPERTS], hT[:, s, :], w["keys"][:, :],
                                      start=True, stop=True)
                else:
                    pe.wait_ge(wparts_done, q.val(2, 2))
                    out = bank[:, :].bitcast(BF16)
                    for s in range(2):
                        m = pe.transpose(out[:, s * S:(s + 1) * S],
                                         wparts[0:S, s].rearrange("p a e -> p (a e)"), identb[0:S, 0:S])
                m.then_inc(filled[k], 1)

            def down(p, j):
                if j == 0:
                    wait_copied(pe, before(p), ("xT",))
                    wait_copied(pe, before(p), ("wT",))
                k = j % 2
                if not (p.first and j < 2):
                    pe.wait_ge(silu_done, p.val(NT, j - 1))
                for kc in range(KC):
                    m = matmul3(pe, psD[k][:, 0:PAIR], both(w["down"], ALL, kc, slice(j * P, (j + 1) * P)),
                                [x[:, kc].rearrange("p s k -> p (s k)") for x in xT[p.p0 % 2]],
                                start=(kc == 0), stop=(kc == KC - 1))
                m.then_inc(down_done, 1)
                if not (p.first and j < 2):
                    pe.wait_ge(hid_done, p.val(NT, j - 1))
                pe.matmul(psW[k][:, 0:PAIR], sel[:, j, :], wT[p.p0 % 2][:].rearrange("p s k -> p (s k)"),
                          start=True, stop=True).then_inc(spread_done, 1)

            def up(p, j):
                if j == 0 and not p.first:
                    pe.wait_ge(h_done, p.val(2, 0))
                pe.wait_ge(hid_low, p.val(NT, j + 1))
                for s in range(2):
                    m = matmul3(pe, psU[s][0:S, 0:D], both(hid2[j % 4], ALL, s), both(w["up"], ALL, j), start=(j == 0),
                                stop=(j == NT - 1))
                m.then_inc(up_done, 1)

            for _, use in banks.front:
                shared(None, use, Pair(0))

            def slot(p):
                for t in range(NT):
                    down(p, t)
                    for use in banks.step(p, t):
                        shared(p, use, p.shift(1))
                    if t >= LAG:
                        up(p, t - LAG)
                    elif not p.first:
                        up(p.shift(-1), t + NT - LAG)

            run_slots(pe, slot)
            for t in range(LAG):
                up(Pair(NPAIR - 1), t + NT - LAG)

        @block.scalar
        def _(act):
            def copy_out(p, use, q):
                if use[0] == "sim":
                    return
                k, n = banks.at(p, use)
                act.wait_ge(filled[k], n + 1)
                if use[0] == "xT":
                    m = act.activation(xT[q.p0 % 2][0][:].rearrange("p c s k -> p (c s k)"), psM[k][:, 0:2 * PAIR], ACT.Copy)
                elif use[0] == "hash":
                    m = act.activation(hT[:].rearrange("p s k -> p (s k)"), psM[k][0:EDIM, 0:PAIR], ACT.Copy)
                else:
                    m = act.activation(wT[q.p0 % 2][:].rearrange("p s k -> p (s k)"),
                                       psM[k][:, :].bitcast(BF16)[:, 0:PAIR], ACT.Copy)
                m.then_inc(high_done if use[0] == "xT" else copied[k], 1)

            def high_half(p, j):
                act.wait_ge(hid_done, p.val(NT, j + 1))
                if not (p.first and j < 4):
                    act.wait_ge(up_done, p.val(NT, j - 3))
                act.activation(hid2[j % 4][0][:].rearrange("p s k -> p (s k)"), hid[j % 2][:].rearrange("p s k -> p (s k)"),
                               ACT.Copy).then_inc(hid_high, 1)

            def silu(p, j):
                act.wait_ge(down_done, p.val(NT, j + 1))
                if not (p.first and j < 2):
                    act.wait_ge(hid_done, p.val(NT, j - 1))
                act.activation(act_s[j % 2][:].rearrange("p s k -> p (s k)"), psD[j % 2][:, 0:PAIR],
                               ACT.Silu).then_inc(silu_done, 1)

            for _, use in banks.front:
                copy_out(None, use, Pair(0))

            def slot(p):
                for t in range(NT):
                    silu(p, t)
                    if t >= 1:
                        high_half(p, t - 1)
                    elif not p.first:
                        high_half(p.shift(-1), NT - 1)
                    for use in banks.step(p, t):
                        copy_out(p, use, p.shift(1))
                    if t == 10:
                        act.wait_ge(scale_set, p.val(1, 1))
                        split.high(act, p, late["split"], scale_now[:, 0:1])

            run_slots(act, slot)
            high_half(Pair(NPAIR - 1), NT - 1)

        @block.gpsimd
        def _(pool):
            def gates(q):
                pool.wait_ge(top_done, q.val(2, 2))
                if not q.first:
                    pool.wait_ge(gates_read, q.val(4, 0))
                pool.tensor_tensor(diff[0:S], top[0:S, :, 0:TOPK], top[0:S, :, 0:1].to_broadcast([S, 2, TOPK]),
                                   ALU.subtract).then_inc(pool_step, 1)
                pool.wait_ge(pool_step, q.val(5, 1))
                pool.tensor_tensor(ew[0:S], c["e"][0:S, :].rearrange("p (s k) -> p s k", s=2), diff[0:S],
                                   ALU.pow).then_inc(pool_step, 1)
                pool.wait_ge(pool_step, q.val(5, 2))
                pool.wait_ge(at_done, q.val(2, 2))
                pool.tensor_tensor(diff[0:S, :, 0:2], ew[0:S, :, 0:2], ew[0:S, :, 2:4], ALU.add).then_inc(pool_step, 1)
                pool.tensor_copy(atf[0:S], at[0:S]).then_inc(gate_done, 1)
                pool.wait_ge(pool_step, q.val(5, 3))
                pool.tensor_tensor(esum[0:S], diff[0:S, :, 0:1], diff[0:S, :, 1:2], ALU.add).then_inc(pool_step, 1)
                pool.wait_ge(pool_step, q.val(5, 4))
                pool.tensor_tensor(erecip[0:S], esum[0:S], c["minus1"][0:S, :].unsqueeze(2), ALU.pow).then_inc(pool_step, 1)
                pool.wait_ge(pool_step, q.val(5, 5))
                pool.tensor_tensor(gate[0:S], ew[0:S], erecip[0:S].to_broadcast([S, 2, TOPK]), ALU.mult).then_inc(gate_done, 1)

            norm.root(pool, Pair(0))
            gates(Pair(0))

            def slot(p):
                if not p.last:
                    norm.root(pool, p.shift(1))
                    gates(p.shift(1))

            run_slots(pool, slot)

        @block.vector
        def _(dve):
            def rows(q):
                if not (q.first or q.p0 == 1 and q.i is None):
                    dve.wait_ge(added, q.val(2, -2))
                norm.rows(dve, q, lambda s: xn[q.p0 % 2][0:S, s, :], xn_done)

            def add_rows(q):
                dve.wait_ge(xn_done, q.val(2, 2))
                for s in range(2):
                    h = rows_of(H, q, s)
                    dve.tensor_tensor(h, h, xn[q.p0 % 2][0:S, s, :], ALU.add).then_inc(added, 1)

            def find_top(p, q):
                k, n = banks.at(p, ("sim",))
                dve.wait_ge(filled[k], n + 1)
                dve.tensor_copy(sim[0:S].rearrange("p s e -> p (s e)"), psM[k][0:S, 0:2 * EXPERTS]).then_inc(copied[k], 1)
                after_constants(dve, c)
                dve.wait_ge(copied[k], n + 1)
                for s in range(2):
                    dve.max(top[0:S, s, :], sim[0:S, s, :]).then_inc(top_done, 1)
                after_constants(dve, c)
                dve.wait_ge(top_done, q.val(2, 2))
                for s in range(2):
                    dve.max_index(at[0:S, s, :], top[0:S, s, :], sim[0:S, s, :]).then_inc(at_done, 1)

            shape = [S, EXPERTS, TOPK]

            def find_hits(q):
                dve.wait_ge(gate_done, q.val(2, 1))
                for s in range(2):
                    dve.tensor_tensor(hit[0:S, s], c["iota"][0:S, :].unsqueeze(2).to_broadcast(shape),
                                      atf[0:S, s, 0:TOPK].unsqueeze(1).to_broadcast(shape),
                                      ALU.is_equal).then_inc(gates_read, 1)

            def gate_hits(q):
                dve.wait_ge(gate_done, q.val(2, 2))
                dve.wait_ge(gates_read, q.val(4, 2))
                for s in range(2):
                    dve.tensor_tensor(hit[0:S, s], hit[0:S, s], gate[0:S, s, :].unsqueeze(1).to_broadcast(shape),
                                      ALU.mult).then_inc(gates_read, 1)

            def sum_hits(q):
                dve.wait_ge(gates_read, q.val(4, 4))
                dve.tensor_reduce(wrow[0:S], hit[0:S], AX.X, ALU.add).then_inc(w_step, 1)
                dve.wait_ge(w_step, q.val(2, 1))
                dve.tensor_copy(wparts[0:S, :, 0, :], wrow[0:S]).then_inc(w_step, 1)

            def low_gates(q):
                dve.wait_ge(w_step, q.val(2, 2))
                for s in range(2):
                    dve.tensor_tensor(wparts[0:S, s, 1, :], wrow[0:S, s, :], wparts[0:S, s, 0, :],
                                      ALU.subtract).then_inc(wparts_done, 1)

            def weigh(p, j):
                k = j % 2
                dve.wait_ge(spread_done, p.val(NT, j + 1))
                dve.wait_ge(silu_done, p.val(NT, j + 1))
                if not (p.first and j < 2):
                    dve.wait_ge(hid_low, p.val(NT, j - 1))
                dve.tensor_tensor(hid[j % 2][:].rearrange("p s k -> p (s k)"), act_s[k][:].rearrange("p s k -> p (s k)"),
                                  psW[k][:, 0:PAIR], ALU.mult).then_inc(hid_done, 1)

            def low_half(p, j):
                dve.wait_ge(hid_high, p.val(NT, j + 1))
                high, low = (x[:].rearrange("p s k -> p (s k)") for x in hid2[j % 4])
                dve.tensor_tensor(low, hid[j % 2][:].rearrange("p s k -> p (s k)"), high, ALU.subtract).then_inc(hid_low, 1)

            def low_of_rows(p, q):
                k, _ = banks.at(p, ("xT",))
                dve.wait_ge(high_done, banks.nth(p, ("xT",), ("xT",)))
                high, low = (x[:].rearrange("p c s k -> p (c s k)") for x in xT[q.p0 % 2])
                dve.tensor_tensor(low, psM[k][:, 0:2 * PAIR], high, ALU.subtract).then_inc(copied[k], 1)

            def residual(p):
                dve.wait_ge(up_done, p.val(NT, NT))
                dve.wait_ge(added, p.val(2, 2))
                for s in range(2):
                    h = rows_of(H, p, s)
                    dve.scalar_tensor_tensor(h, psU[s][0:S, 0:D], w["scale"][0:S, 0:1], h, ALU.mult,
                                             ALU.add).then_inc(h_done, 1)

            norm.moments(dve, Pair(0))
            norm.wait_moments(dve, Pair(0))
            norm.aggregate(dve, Pair(0))
            rows(Pair(0))
            add_rows(Pair(0))
            low_of_rows(None, Pair(0))
            find_top(None, Pair(0))
            for part in (find_hits, gate_hits, sum_hits, low_gates):
                part(Pair(0))

            def slot(p):
                for t in range(NT):
                    if t == 0 and not p.last:
                        norm.moments(dve, p.shift(1))
                        norm.wait_moments(dve, p.shift(1))
                    weigh(p, t)
                    if t == LAG - 1 and not p.first:
                        residual(p.shift(-1))
                    if t >= 1:
                        low_half(p, t - 1)
                    elif not p.first:
                        low_half(p.shift(-1), NT - 1)
                    if t == 9:
                        if not p.first:
                            dve.wait_ge(split.used, p.val(1, 0))
                        dve.tensor_copy(scale_now[:], cell(late["scales"], p)).then_inc(scale_set, 1)
                    if t == 10:
                        dve.wait_ge(scale_set, p.val(1, 1))
                        split.low(dve, p, late["split"], scale_now[:, 0:1])
                    if not p.last:
                        if t == 0:
                            norm.aggregate(dve, p.shift(1))
                        if t == 1:
                            rows(p.shift(1))
                        if t == 5:
                            add_rows(p.shift(1))
                        if t == 3:
                            low_of_rows(p, p.shift(1))
                        if t == 7:
                            find_top(p, p.shift(1))
                        if t == 11:
                            find_hits(p.shift(1))
                        if t == 12:
                            gate_hits(p.shift(1))
                        if t == 13:
                            sum_hits(p.shift(1))
                            low_gates(p.shift(1))

            run_slots(dve, slot)
            low_half(Pair(NPAIR - 1), NT - 1)
            residual(Pair(NPAIR - 1))


def quant_ffn(nc, name, H, c, w, out, sb, psum, sem):
    ident, identb = c["ident"], c["identb"]
    xs, xabs, guT, dT, wscale = w["x"], w["absmax"], w["guT"], w["dT"], w["scale"]
    aabs = sb(name + "aabs", [P, NPAIR], F32)
    sig = sb(name + "sig", [P, 2, 4], F32)
    gsc = sb(name + "gsc", [P, 2 * ITILES], F32)
    downscale = sb(name + "downscale", [P, D], F32)
    diag = sb(name + "diag", [P, KC, P], F32)
    xq = [sb(name + f"xq{k}", [P, 2, D], BF16) for k in range(2)]
    xr = sb(name + "xr", [P, 2, D], F32)
    xc = sb(name + "xc", [P, 2, D], BF16)
    xqT = [sb(name + f"xqT{k}", [P, KC, 2, S], BF16) for k in range(2)]
    sg = [sb(name + f"sg{k}", [P, 2, S], F32) for k in range(3)]
    a = sb(name + "a", [P, ITILES, B * S], F32)
    ar = [sb(name + f"ar{k}", [P, ITILES, S], F32) for k in range(2)]
    ac = [sb(name + f"ac{k}", [P, ITILES, S], BF16) for k in range(2)]
    aq = [sb(name + f"aq{k}", [P, ITILES, S], BF16) for k in range(2)]
    bank = [psum(name + f"ps{k}", [P, 512], F32) for k in range(8)]

    pad_done = sem(name + "pad_done")
    gmax_done, sig_step, sig_done = sem(name + "gmax_done"), sem(name + "sig_step"), sem(name + "sig_done")
    diag_done, spread_done = sem(name + "diag_done"), sem(name + "spread_done")
    xr_done, xc_done, xq_done, xT_filled, xT_copied = (sem(name + n) for n in (
        "xr_done", "xc_done", "xq_done", "xT_filled", "xT_copied"))
    gu_done, sg_done, a_done, aabs_done = (sem(name + n) for n in ("gu_done", "sg_done", "a_done", "aabs_done"))
    ar_done, aq_step, aq_done, down_done, step_done, h_done, out_done = (sem(name + n) for n in (
        "ar_done", "aq_step", "aq_done", "down_done", "step_done", "h_done", "out_done"))

    def columns(p):
        n = p.val(PAIR, 0)
        return bass.ds(n, PAIR) if not isinstance(n, int) else slice(n, n + PAIR)

    step_sem = sem(name + "scale_step")
    gcol = sb(name + "gcol", [P, 2], F32)
    gtmp = sb(name + "gtmp", [P, 2], F32)
    sigma = sb(name + "sigma", [P, 2], F32)
    qs = sb(name + "qs", [P, 2], F32)
    qr = sb(name + "qr", [P, 2], F32)

    def global_scale(k, parts, npart):
        with nc.Block() as block:
            base = 6 * k

            @block.vector
            def _(dve):
                dve.memset(gcol[:, k:k + 1], 0.0).then_inc(step_sem, 1)
                dve.wait_ge(step_sem, base + 1)
                dve.tensor_reduce(gcol[0:npart, k:k + 1], parts, AX.XY, ALU.max).then_inc(step_sem, 1)
                dve.wait_ge(sig_done, 1)
                dve.reciprocal(sigma[:, k:k + 1], sig[:, k, 2:3]).then_inc(step_sem, 1)
                dve.wait_ge(gmax_done, k + 1)
                dve.wait_ge(step_sem, base + 3)
                dve.tensor_scalar(qs[:, k:k + 1], gtmp[:, k:k + 1], sigma[:, k:k + 1], 1.0 / QMAX, ALU.mult,
                                  ALU.mult).then_inc(step_sem, 1)
                dve.wait_ge(step_sem, base + 4)
                dve.reciprocal(qr[:, k:k + 1], qs[:, k:k + 1]).then_inc(step_sem, 1)
                if k == 0:
                    dve.tensor_scalar(gsc[:], wscale[:, 0:2 * ITILES], qs[:, 0:1], None, ALU.mult).then_inc(step_sem, 1)
                else:
                    for h in range(KC):
                        dve.tensor_scalar(diag[:, h, :], ident[:], wscale[:, 2 * ITILES + h:2 * ITILES + h + 1],
                                          qs[:, 1:2], ALU.mult, ALU.mult).then_inc(diag_done, 1)
                    dve.wait_ge(spread_done, 1)
                    dve.tensor_copy(downscale[:], bank[0][:, 0:D]).then_inc(step_sem, 1)

            @block.gpsimd
            def _(pool):
                if k == 0:
                    for n in range(2):
                        pool.tensor_scalar(sig[:, n, 0:1], w["clip"][:, n:n + 1], -1.0, None, ALU.mult).then_inc(sig_step, 1)
                    pool.wait_ge(sig_step, 2)
                    pool.tensor_tensor(sig[:, :, 1:2], c["e"][:, 0:2].unsqueeze(2), sig[:, :, 0:1], ALU.pow).then_inc(sig_step, 1)
                    pool.wait_ge(sig_step, 3)
                    pool.tensor_scalar(sig[:, :, 2:3], sig[:, :, 1:2], 1.0, None, ALU.add).then_inc(sig_done, 1)
                pool.wait_ge(step_sem, base + 2)
                pool.partition_all_reduce(gtmp[:, k:k + 1], gcol[:, k:k + 1], P,
                                          bass.bass_isa.ReduceOp.max).then_inc(gmax_done, 1)

            @block.tensor
            def _(pe):
                if k == 1:
                    pe.wait_ge(diag_done, KC)
                    pe.matmul(bank[0][:, 0:D], c["ones"][:, :], diag[:].rearrange("p h k -> p (h k)"), start=True,
                              stop=True).then_inc(spread_done, 1)

    global_scale(0, xabs[0:S, :].unsqueeze(1), S)

    with nc.Block() as block:
        M = ITILES

        @block.gpsimd
        def _(pool):
            pool.memset(a[IROWS[-1]:P, ITILES - 1, :], 0.0).then_inc(pad_done, 1)

        @block.vector
        def _(dve):
            def quantize(q):
                dve.wait_ge(xr_done, q.val(1, 1))
                if not q.first:
                    dve.wait_ge(xq_done, q.val(1, 0))
                dve.tensor_scalar(xc[0:S], xr[0:S], ROUND, QMAX, ALU.subtract, ALU.min).then_inc(xc_done, 1)
                if not (q.first or q.p0 == 1 and q.i is None):
                    dve.wait_ge(xT_filled, q.val(1, -1))
                dve.wait_ge(xc_done, q.val(1, 1))
                dve.tensor_scalar(xq[q.p0 % 2][0:S], xc[0:S], -QMAX - 1.0, None, ALU.max).then_inc(xq_done, 1)

            def product(p, m):
                r, k = IROWS[m], m % 3
                dve.wait_ge(sg_done, p.val(M, m + 1))
                dve.scalar_tensor_tensor(a[0:r, m, columns(p)], bank[2 + m][0:r, PAIR:2 * PAIR],
                                         gsc[0:r, ITILES + m:ITILES + m + 1], sg[k][0:r].rearrange("p s k -> p (s k)"),
                                         ALU.mult, ALU.mult).then_inc(a_done, 1)

            def absmax(p):
                dve.wait_ge(a_done, p.val(M, M))
                dve.tensor_reduce(cell(aabs, p), a[:, :, columns(p)], AX.XY, ALU.max,
                                  apply_absolute_value=True).then_inc(aabs_done, 1)

            dve.wait_ge(pad_done, 1)
            quantize(Pair(0))

            def slot(p):
                for m in range(M):
                    product(p, m)
                    if m == 1 and not p.last:
                        quantize(p.shift(1))
                    if m == 2 and not p.first:
                        absmax(p.shift(-1))

            run_slots(dve, slot)
            absmax(Pair(NPAIR - 1))

        @block.tensor
        def _(pe):
            def turn(q):
                k = q.p0 % 2
                pe.wait_ge(xq_done, q.val(1, 1))
                if not (q.first or q.p0 == 1 and q.i is None):
                    pe.wait_ge(xT_copied, q.val(1, -1))
                o = bank[k][:, :].bitcast(BF16)
                for kc in range(KC):
                    for s in range(2):
                        m = pe.transpose(o[:, (2 * kc + s) * S:(2 * kc + s + 1) * S], xq[k][0:S, s, kc * P:(kc + 1) * P],
                                         identb[0:S, 0:S])
                m.then_inc(xT_filled, 1)

            def gate_up(p, m):
                r = IROWS[m]
                if m == 0:
                    pe.wait_ge(xT_copied, p.val(1, 1))
                if not p.first:
                    pe.wait_ge(a_done, p.val(M, m - M + 1))
                for which in range(2):
                    for kc in range(KC):
                        x = pe.matmul(bank[2 + m][0:r, which * PAIR:(which + 1) * PAIR],
                                      guT[:, which, kc, m * P:m * P + r],
                                      xqT[p.p0 % 2][:, kc].rearrange("p s k -> p (s k)"), start=(kc == 0), stop=(kc == KC - 1))
                x.then_inc(gu_done, 1)

            turn(Pair(0))

            def slot(p):
                for m in range(M):
                    gate_up(p, m)
                    if m == 3 and not p.last:
                        turn(p.shift(1))

            run_slots(pe, slot)

        @block.scalar
        def _(act):
            def copy_out(q):
                k = q.p0 % 2
                act.wait_ge(xT_filled, q.val(1, 1))
                act.activation(xqT[k][:].rearrange("p c s k -> p (c s k)"), bank[k][:, :].bitcast(BF16)[:, 0:2 * PAIR],
                               ACT.Copy).then_inc(xT_copied, 1)

            def round_rows(q):
                if not q.first:
                    act.wait_ge(xc_done, q.val(1, 0))
                act.activation(xr[0:S], pair_of(xs, q), ACT.Identity, bias=c["round"][0:S, 0:1],
                               scale=qr[0:S, 0:1]).then_inc(xr_done, 1)

            def silu(p, m):
                r, k = IROWS[m], m % 3
                act.wait_ge(gu_done, p.val(M, m + 1))
                if not (p.first and m < 3):
                    act.wait_ge(a_done, p.val(M, m - 2))
                act.activation(sg[k][0:r].rearrange("p s k -> p (s k)"), bank[2 + m][0:r, 0:PAIR],
                               ACT.Silu, scale=gsc[0:r, m:m + 1]).then_inc(sg_done, 1)

            round_rows(Pair(0))
            copy_out(Pair(0))

            def slot(p):
                for m in range(M):
                    silu(p, m)
                    if m == 0 and not p.last:
                        round_rows(p.shift(1))
                    if m == 4 and not p.last:
                        copy_out(p.shift(1))

            run_slots(act, slot)

    global_scale(1, aabs[:].unsqueeze(1), P)

    with nc.Block() as block:
        def sample_cols(p, s):
            n = p.val(PAIR, s * S)
            return bass.ds(n, S) if not isinstance(n, int) else slice(n, n + S)

        @block.vector
        def _(dve):
            def clip_high(p, s):
                dve.wait_ge(ar_done, p.val(2, s + 1))
                if not p.first:
                    dve.wait_ge(aq_done, p.val(2, s - 1))
                dve.tensor_scalar(ac[s][:], ar[s][:], ROUND, QMAX, ALU.subtract, ALU.min).then_inc(aq_step, 1)

            def clip_low(p, s):
                dve.wait_ge(aq_step, p.val(2, s + 1))
                if not p.first:
                    dve.wait_ge(down_done, p.val(2, s - 1))
                dve.tensor_scalar(aq[s][:], ac[s][:], -QMAX - 1.0, None, ALU.max).then_inc(aq_done, 1)

            def rescale(p, s):
                dve.wait_ge(down_done, p.val(2, s + 1))
                dve.tensor_tensor(bank[s][0:S, 0:D], bank[s][0:S, 0:D], downscale[0:S, :], ALU.mult).then_inc(step_done, 1)

            def residual(p, s):
                dve.wait_ge(step_done, p.val(2, s + 1))
                h = rows_of(H, p, s)
                dve.tensor_tensor(h, h, bank[s][0:S, 0:D], ALU.add).then_inc(h_done, 1)

            def slot(p):
                for s in range(2):
                    clip_high(p, s)
                    if not p.first:
                        rescale(p.shift(-1), s)
                    clip_low(p, s)
                    if not p.first:
                        residual(p.shift(-1), s)

            run_slots(dve, slot)
            for s in range(2):
                rescale(Pair(NPAIR - 1), s)
                residual(Pair(NPAIR - 1), s)

        @block.scalar
        def _(act):
            def slot(p):
                for s in range(2):
                    if not p.first:
                        act.wait_ge(aq_step, p.val(2, s - 1))
                    act.activation(ar[s][:], a[:, :, sample_cols(p, s)], ACT.Identity, bias=c["round"][:, 0:1],
                                   scale=qr[:, 1:2]).then_inc(ar_done, 1)

            run_slots(act, slot)

        @block.tensor
        def _(pe):
            def slot(p):
                for s in range(2):
                    pe.wait_ge(aq_done, p.val(2, s + 1))
                    if not p.first:
                        pe.wait_ge(h_done, p.val(2, s - 1))
                    for m in range(ITILES):
                        r = IROWS[m]
                        x = pe.matmul(bank[s][0:S, 0:D], aq[s][0:r, m, :], dT[0:r, m, :], start=(m == 0),
                                      stop=(m == ITILES - 1))
                    x.then_inc(down_done, 1)

            run_slots(pe, slot)

        @block.sync
        def _(sp):
            def slot(p):
                for s in range(2):
                    sp.wait_ge(h_done, p.val(2, s + 1))
                    b = p.val(2, s)
                    dst = out[bass.ds(b, 1), :, :].rearrange("a s d -> (a s) d") if not isinstance(b, int) else out[b, :, :]
                    sp.dma_start(dst, rows_of(H, p, s)).then_inc(out_done, 16)

            run_slots(sp, slot)
            sp.wait_ge(out_done, 16 * B)


def program(nc, t, out):
    with ExitStack() as whole:
        def opened(stack, make):
            return lambda *a: stack.enter_context(make(*a))

        sem = opened(whole, nc.semaphore)
        sb = opened(whole, nc.sbuf_tensor)
        c = consts_on_chip(nc, sb, sem)
        made = c["made"] = sem("made")
        H = sb("H", [P, B, D], F32)
        f1 = {
            "x": sb("f1_x", [P, B, D], F32), "absmax": sb("f1_absmax", [P, NPAIR], F32),
            "guT": sb("f1_guT", [P, 2, KC, INNER], BF16), "dT": sb("f1_dT", [P, ITILES, D], BF16),
            "scale": sb("f1_scale", [P, 2 * ITILES + KC], F32), "clip": sb("f1_clip", [P, 2], F32),
        }
        plain, split = [("f1_clip", f1["clip"][:])], []

        def halves(sb, name, shape):
            pair = [sb(name + "_" + h, shape, BF16) for h in ("high", "low")]
            split.append((name, pair))
            return pair

        def small(sb, name, shape):
            x = sb(name, shape, F32)
            plain.append((name, x[:]))
            return x

        with ExitStack() as s3:
            sb3 = opened(s3, nc.sbuf_tensor)
            a1_late = [sb3("a1_late_" + h, [P, NPAIR, PIECE], F16) for h in ("high", "low")]
            a1 = {"qk": as_chunks(a1_late, A1_PIECES["qk"], 2048), "v": as_chunks(a1_late, A1_PIECES["v"], 1024),
                  "o": as_chunks(a1_late, A1_PIECES["o"], D), "range": sb3("a1_range", [P, NPAIR], F32),
                  "scales": sb3("a1_scales", [P, NPAIR], F32), "exp_scale": sb3("a1_exp_scale", [P, 1], F32),
                  "out_scale": sb3("a1_out_scale", [P, 1], F32)}
            with ExitStack() as s2:
                sb2 = opened(s2, nc.sbuf_tensor)
                f0_late = [sb2("f0_late_" + h, [P, NPAIR, PIECE], BF16) for h in ("high", "low")]
                f0 = {"down": as_chunks(f0_late, F0_PIECES["down"], EXPERTS * EDIM), "up": as_chunks(f0_late, F0_PIECES["up"], D),
                      "hash": halves(sb2, "f0_hash", [P, KC, EDIM]), "keys": small(sb2, "f0_keys", [EDIM, EXPERTS]),
                      "scale": small(sb2, "f0_scale", [P, 1])}
                with ExitStack() as s1:
                    sb1 = opened(s1, nc.sbuf_tensor)
                    a0 = {"qk": halves(sb1, "a0_qk", [P, KC, 1024]), "v": halves(sb1, "a0_v", [P, KC, D]),
                          "o": halves(sb1, "a0_o", [P, KC, D]), "qkb": small(sb1, "a0_qkb", [P, 8]),
                          "biases": sb1("a0_biases", [3, 2 * D], BF16), "ones": sb1("a0_ones", [3, P], BF16)}
                    with ExitStack() as s0:
                        embed(nc, t, H, c, made, plain, split, f1, a0, a1_late[0][:].rearrange("p a n -> p (a n)").bitcast(F32), opened(s0, nc.sbuf_tensor), opened(s0, nc.psum_tensor), sem)
                    with ExitStack() as s0:
                        attention(nc, "a0_", H, c, a0, 16, opened(s0, nc.sbuf_tensor), opened(s0, nc.psum_tensor),
                                  opened(s0, nc.semaphore),
                                  late={"split_src": t["f0_late"], "split": f0_late, "look_src": t["a1_late"], "range": a1["range"]})
                with ExitStack() as s0:
                    scale_weights(nc, a1, opened(s0, nc.sbuf_tensor), opened(s0, nc.semaphore))
                with ExitStack() as s0:
                    experts(nc, "f0_", H, c, f0, opened(s0, nc.sbuf_tensor), opened(s0, nc.psum_tensor),
                            opened(s0, nc.semaphore), late={"src": t["a1_late"], "split": a1_late, "scales": a1["scales"]})
            with ExitStack() as s0:
                own = opened(s0, nc.sbuf_tensor)
                final = {"norm": Norm("a1_final_", c, H, own, sem), "x": f1["x"], "absmax": f1["absmax"],
                         "x_done": sem("f1_x_done"), "absmax_done": sem("f1_absmax_done")}
                attention(nc, "a1_", H, c, a1, 64, own, opened(s0, nc.psum_tensor), opened(s0, nc.semaphore), final)
        with ExitStack() as s0:
            quant_ffn(nc, "f1_", H, c, f1, out, opened(s0, nc.sbuf_tensor), opened(s0, nc.psum_tensor),
                      opened(s0, nc.semaphore))


def embed(nc, t, H, c, made, plain, split, f1, a0, room, sb, psum, sem):
    tiles = [(g, min(TOK_G, B - g)) for g in range(0, B, TOK_G)]
    NT, TW = len(tiles), TOK_K * TOK_G * NIMG
    W = sb("tok_W", [P, TOK_K, D], F32)
    pos = sb("tok_pos", [TOK_G * NIMG, D], F32)
    add = sb("tok_add", [TOK_G * NIMG, D], F32)
    rows = sb("tok_rows", [TOK_G * NIMG, NT, D], F32)
    idx = sb("tok_idx", [NTXT, B], I32)
    spare = f1["x"][:].rearrange("p b d -> p (b d)")
    patches = spare[:, 0:NT * TW].rearrange("p (t k n) -> p t k n", k=TOK_K, n=TOK_G * NIMG)
    ps = [psum(f"tok_ps{k}", [P, 512], F32) for k in range(4)]
    idx_in, W_in, pos_in, words_in, images_in, plain_in = (sem(n) for n in (
        "idx_in", "W_in", "pos_in", "words_in", "images_in", "plain_in"))
    patches_in = [sem(f"patches_in{k}") for k in range(NT)]
    pos_done, proj_done, rows_done = sem("pos_done"), sem("proj_done"), sem("rows_done")

    bias_in, bias_step = sem("bias_in"), sem("bias_step")
    whole, rest0, rest1, kept0, kept1 = (room[0:3, k * 2 * D:(k + 1) * 2 * D] for k in range(5))
    parts = [room[0:3, (5 + k) * 2 * D:(6 + k) * 2 * D].bitcast(BF16)[:, 0:2 * D] for k in range(3)]
    rest, kept = (rest0, rest1), (kept0, kept1)

    RING, CHUNK = 3, 768
    raw = [sb(f"raw{k}", [P, CHUNK], F32) for k in range(RING)]
    raw_in = [sem(f"raw_in{k}") for k in range(RING)]
    high_done, low_done = sem("high_done"), sem("low_done")
    chunks = []
    for name, pair in reversed(split):
        flat = [x[:].rearrange("p a n -> p (a n)") for x in pair]
        src = t[name].rearrange("p a n -> p (a n)")
        n = src.shape[1]
        for a in range(0, n, CHUNK):
            b = min(a + CHUNK, n)
            chunks.append((src[:, a:b], flat[0][:, a:b], flat[1][:, a:b], b - a))

    f1_in = sem("f1_in")
    quant = {n: sb("raw_" + n, shape, F32) for n, shape in (
        ("f1_gate", [P, ITILES, D]), ("f1_up", [P, ITILES, D]), ("f1_down", [P, KC, INNER]))}
    wtiles = [(quant[n][0:IROWS[m], m, :], IROWS[m], D) for n in ("f1_gate", "f1_up") for m in range(ITILES)]
    wtiles += [(quant["f1_down"][:, m, :], P, INNER) for m in range(KC)]
    NW = len(wtiles)
    wrange = sb("wrange", [P, NW], F32)
    wrecip = sb("wrecip", [P, NW], F32)
    rounded = spare[:, NT * TW:NT * TW + INNER]
    wq = [sb(f"wq{k}", [P, INNER], BF16) for k in range(2)]
    range_done, scale_done, recip_done = sem("range_done"), sem("scale_done"), sem("recip_done")
    wround_done, wq_done, w_filled, w_copied = sem("wround_done"), sem("wq_done"), sem("w_filled"), sem("w_copied")

    with nc.Block() as block:
        @block.sync
        def _(sp):
            sp.dma_start(idx[:], t["idx"]).then_inc(idx_in, 16)
            for n, q in quant.items():
                sp.dma_start(q[:], t[n]).then_inc(f1_in, 16)
            sp.dma_start(W[:], t["tok_W"]).then_inc(W_in, 16)
            sp.dma_start(pos[:], t["tok_pos"]).then_inc(pos_in, 16)
            sp.dma_start(add[:], t["tok_add"]).then_inc(pos_in, 16)
            sp.dma_start(whole, t["a0_biases"]).then_inc(bias_in, 16)
            for name, dst in plain:
                sp.dma_start(dst, t[name]).then_inc(plain_in, 16)
            for n in range(max(NT, len(chunks))):
                if n < NT:
                    sp.dma_start(patches[:, n].rearrange("p k n -> p (k n)"), t["patches"][n]).then_inc(patches_in[n], 16)
                if n < len(chunks):
                    if n >= RING:
                        sp.wait_ge(low_done, n - RING + 1)
                    sp.dma_start(raw[n % RING][:, 0:chunks[n][3]], chunks[n][0]).then_inc(raw_in[n % RING], 16)
            for n, (b, g) in enumerate(tiles):
                sp.wait_ge(rows_done, n + 1)
                for k in range(g):
                    sp.dma_start(H[0:NIMG, b + k, :], rows[k * NIMG:(k + 1) * NIMG, n, :]).then_inc(images_in, 16)
            sp.wait_ge(plain_in, 16 * len(plain))
            sp.wait_ge(images_in, 16 * B)

        @block.gpsimd
        def _(pool):
            build_consts(pool, c, made)
            pool.wait_ge(idx_in, 16)
            for b in range(B):
                pool.indirect_dma_start(H[NIMG:S, b, :], None, t["emb"],
                                        bass.IndirectOffsetOnAxis(ap=idx[:, b:b + 1].bitcast(U32), axis=0)).then_inc(words_in, 16)
            pool.wait_ge(words_in, 16 * B)

        @block.tensor
        def _(pe):
            def weight_tile(k):
                _, r, width = wtiles[k]
                pe.wait_ge(wq_done, k + 1)
                if k >= 2:
                    pe.wait_ge(w_copied, k - 1)
                o = ps[2 + k % 2][:, :].bitcast(BF16)
                for j in range((width + P - 1) // P):
                    cols = min(P, width - j * P)
                    m = pe.transpose(o[0:cols, j * P:j * P + r], wq[k % 2][0:r, j * P:j * P + cols], c["identb"][0:r, 0:r])
                m.then_inc(w_filled, 1)

            def patch_tile(n):
                r = tiles[n][1] * NIMG
                pe.wait_ge(patches_in[n], 16)
                if n >= 2:
                    pe.wait_ge(rows_done, n - 1)
                for k in range(TOK_K):
                    m = pe.matmul(ps[n % 2][0:r, 0:D], patches[:, n, k, 0:r], W[:, k, :], start=(k == 0),
                                  stop=(k == TOK_K - 1))
                m.then_inc(proj_done, 1)

            pe.wait_ge(W_in, 16)
            pe.wait_ge(made, MADE)
            for k in range(max(NW, NT)):
                if k < NW:
                    weight_tile(k)
                if k < NT:
                    patch_tile(k)

        @block.scalar
        def _(act):
            def copy_out(k):
                _, r, width = wtiles[k]
                act.wait_ge(w_filled, k + 1)
                o = ps[2 + k % 2][:, :].bitcast(BF16)
                if k < 2 * ITILES:
                    which, m = k // ITILES, k % ITILES
                    x = act.activation(f1["guT"][:, which, :, m * P:m * P + r],
                                       o[:, 0:KC * P].rearrange("p (c r) -> p c r", r=P)[:, :, 0:r], ACT.Copy)
                else:
                    half, full = k - 2 * ITILES, INNER // P
                    act.activation(f1["dT"][:, 0:full, half * P:(half + 1) * P],
                                   o[:, 0:full * P].rearrange("p (c r) -> p c r", r=P), ACT.Copy)
                    x = act.activation(f1["dT"][0:IROWS[-1], full, half * P:(half + 1) * P],
                                       o[0:IROWS[-1], full * P:(full + 1) * P], ACT.Copy)
                x.then_inc(w_copied, 1)

            for n in range(max(NW, len(chunks))):
                if n < NW:
                    copy_out(n)
                if n < len(chunks):
                    act.wait_ge(raw_in[n % RING], 16 * (n // RING + 1))
                    act.activation(chunks[n][1], raw[n % RING][:, 0:chunks[n][3]], ACT.Copy).then_inc(high_done, 1)

        @block.vector
        def _(dve):
            def weight_tile(k):
                src, r, width = wtiles[k]
                if k >= 1:
                    dve.wait_ge(wq_done, k)
                dve.tensor_scalar(rounded[0:r, 0:width], src, wrecip[0:r, k:k + 1], ROUND, ALU.mult,
                                  ALU.add).then_inc(wround_done, 1)
                dve.wait_ge(wround_done, k + 1)
                if k >= 2:
                    dve.wait_ge(w_filled, k - 1)
                dve.tensor_scalar(wq[k % 2][0:r, 0:width], rounded[0:r, 0:width], ROUND, None,
                                  ALU.subtract).then_inc(wq_done, 1)

            def bias_parts():
                dve.wait_ge(bias_in, 16)
                dve.wait_ge(made, MADE)
                dve.tensor_copy(parts[0], whole).then_inc(bias_step, 1)
                dve.memset(a0["ones"][:], 1.0).then_inc(bias_step, 1)
                dve.wait_ge(bias_step, 2)
                dve.tensor_tensor(rest[0], whole, parts[0], ALU.subtract).then_inc(bias_step, 1)
                dve.wait_ge(bias_step, 3)
                dve.tensor_copy(parts[1], rest[0]).then_inc(bias_step, 1)
                dve.wait_ge(bias_step, 4)
                dve.tensor_tensor(rest[1], rest[0], parts[1], ALU.subtract).then_inc(bias_step, 1)
                dve.wait_ge(bias_step, 5)
                dve.tensor_copy(parts[2], rest[1]).then_inc(bias_step, 1)
                dve.tensor_scalar(kept[0], parts[0], c["ident"][0:3, 0:1], None, ALU.mult).then_inc(bias_step, 1)
                dve.wait_ge(bias_step, 7)
                dve.scalar_tensor_tensor(kept[1], parts[1], c["ident"][0:3, 1:2], kept[0], ALU.mult,
                                         ALU.add).then_inc(bias_step, 1)
                dve.wait_ge(bias_step, 8)
                dve.scalar_tensor_tensor(a0["biases"][:], parts[2], c["ident"][0:3, 2:3], kept[1], ALU.mult,
                                         ALU.add).then_inc(bias_step, 1)
                dve.wait_ge(bias_step, 9)

            dve.memset(wrange[:], 1.0).then_inc(range_done, 1)
            dve.wait_ge(range_done, 1)
            dve.wait_ge(f1_in, 48)
            for k, (src, r, _) in enumerate(wtiles):
                dve.tensor_reduce(wrange[0:r, k:k + 1], src, AX.X, ALU.max, apply_absolute_value=True).then_inc(range_done, 1)
            dve.wait_ge(range_done, NW + 1)
            dve.tensor_scalar(f1["scale"][:], wrange[:], 1.0 / QMAX, None, ALU.mult).then_inc(scale_done, 1)
            dve.wait_ge(scale_done, 1)
            dve.reciprocal(wrecip[:], f1["scale"][:]).then_inc(recip_done, 1)
            dve.wait_ge(recip_done, 1)
            dve.wait_ge(pos_in, 32)
            dve.tensor_tensor(pos[:], pos[:], add[:], ALU.add).then_inc(pos_done, 1)
            dve.wait_ge(pos_done, 1)
            weight_tile(0)
            for n in range(max(NW, NT, len(chunks))):
                if n + 1 < NW:
                    weight_tile(n + 1)
                if n < len(chunks):
                    dve.wait_ge(high_done, n + 1)
                    dve.tensor_tensor(chunks[n][2], raw[n % RING][:, 0:chunks[n][3]], chunks[n][1],
                                      ALU.subtract).then_inc(low_done, 1)
                if n < NT:
                    r = tiles[n][1] * NIMG
                    dve.wait_ge(proj_done, n + 1)
                    dve.tensor_tensor(rows[0:r, n, :], ps[n % 2][0:r, 0:D], pos[0:r, :], ALU.add).then_inc(rows_done, 1)
                if n == 2:
                    bias_parts()


def kernel(x, x_txt, L0_tok_W, L0_tok_b, L0_tok_pos_embedding, L0_tok_cls_token, L0_txt_embeddings, L0_attn_w_attn,
           L0_attn_b_attn, L0_attn_w_proj, L0_attn_b_proj, L0_ffn_hasher_w, L0_ffn_keys, L0_ffn_values_down,
           L0_ffn_values_up, L0_ffn_scale, L1_attn_w_q, L1_attn_w_k, L1_attn_w_v, L1_attn_w_o, L1_ffn_clip_x,
           L1_ffn_clip_down, L1_ffn_w_gate, L1_ffn_w_up, L1_ffn_w_down):
    import numpy as np
    import concourse.bacc as bacc
    from concourse.bass_utils import run_bass_kernel_spmd

    def chunked(m):
        m = np.asarray(m)
        return m.reshape(-1, P, m.shape[1]).transpose(1, 0, 2)

    def pieces(*weights):
        return np.concatenate([m.reshape(P, -1, PIECE) for m in weights], axis=1)

    def on_partitions(v):
        return np.tile(np.asarray(v).reshape(1, -1), (P, 1))

    G, PX, C = 6, 16, 3
    img = np.asarray(x).reshape(B, C, G, PX, G, PX).transpose(1, 3, 5, 0, 2, 4).reshape(C * PX * PX, B, NIMG - 1)
    patches = np.zeros((C * PX * PX, B, NIMG), img.dtype)
    patches[:, :, 1:] = img
    room = np.zeros((C * PX * PX, -(-B // TOK_G) * TOK_G, NIMG), img.dtype)
    room[:, 0:B] = patches
    patch_tiles = room.reshape(TOK_K, P, -1, TOK_G * NIMG).transpose(2, 1, 0, 3).reshape(-1, P, TOK_K * TOK_G * NIMG)
    tok_add = np.concatenate([np.asarray(L0_tok_cls_token)[0], np.tile(np.asarray(L0_tok_b)[None], (NIMG - 1, 1))])
    wa, ba = np.asarray(L0_attn_w_attn), np.asarray(L0_attn_b_attn)
    qk = np.zeros((2, HEADS, 32, D), wa.dtype)
    qk[:, :, 0:16] = wa[0:2 * D].reshape(2, HEADS, 16, D)
    qkb = np.zeros((2, HEADS, 32), ba.dtype)
    qkb[:, :, 0:16] = ba[0:2 * D].reshape(2, HEADS, 16)
    a1_qk = np.concatenate([np.asarray(L1_attn_w_q).reshape(-1, D), np.asarray(L1_attn_w_k).reshape(-1, D)])

    def rows_padded(m):
        m = np.asarray(m)
        padded = np.zeros((ITILES * P, D), m.dtype)
        padded[0:INNER] = m
        return chunked(padded)

    arrays = {
        "idx": np.asarray(x_txt).T,
        "emb": np.asarray(L0_txt_embeddings),
        "patches": patch_tiles,
        "tok_W": chunked(np.asarray(L0_tok_W).T),
        "tok_pos": np.tile(np.asarray(L0_tok_pos_embedding)[0], (TOK_G, 1)),
        "tok_add": np.tile(tok_add, (TOK_G, 1)),
        "a0_qk": chunked(qk.reshape(-1, D).T),
        "a0_qkb": qkb.reshape(-1, P).T,
        "a0_v": chunked(wa[2 * D:].T),
        "a0_biases": np.tile(np.concatenate([ba[2 * D:], np.asarray(L0_attn_b_proj)]).reshape(1, -1), (3, 1)),
        "a0_o": chunked(np.asarray(L0_attn_w_proj).T),
        "f0_hash": chunked(np.asarray(L0_ffn_hasher_w).T),
        "f0_keys": np.asarray(L0_ffn_keys).T,
        "f0_late": pieces(chunked(np.asarray(L0_ffn_values_down).transpose(1, 0, 2).reshape(D, -1)),
                          chunked(np.asarray(L0_ffn_values_up).reshape(-1, D))),
        "f0_scale": on_partitions(L0_ffn_scale),
        "a1_late": pieces(chunked(a1_qk.T), chunked(np.asarray(L1_attn_w_v).reshape(-1, D).T), chunked(L1_attn_w_o)),
        "f1_gate": rows_padded(L1_ffn_w_gate),
        "f1_up": rows_padded(L1_ffn_w_up),
        "f1_down": chunked(L1_ffn_w_down),
        "f1_clip": on_partitions(np.concatenate([np.asarray(L1_ffn_clip_x), np.asarray(L1_ffn_clip_down)])),
    }
    arrays = {n + "_dram": np.ascontiguousarray(a) for n, a in arrays.items()}
    nc = bacc.Bacc("TRN2", target_bir_lowering=False, num_devices=1)
    t = {n[:-5]: nc.dram_tensor(n, a.shape, mybir.dt.from_np(a.dtype), kind="ExternalInput").ap() for n, a in arrays.items()}
    out = nc.dram_tensor("out_dram", (B, S, D), F32, kind="ExternalOutput").ap()
    program(nc, t, out)
    r = run_bass_kernel_spmd(nc, [arrays], core_ids=[0])
    return r.results[0]["out_dram"]
```
